# Optimizing a Trainium2 kernel written in Bass

```python
import numpy as np
import jax
import jax.numpy as jnp

def _softmax(x, axis=-1):
    return jax.nn.softmax(x, axis=axis)

def _gelu(x):
    return jax.nn.gelu(x, approximate=True)

def _silu(x):
    return jax.nn.silu(x)

def _sigmoid(x):
    return jax.nn.sigmoid(x)

def _layernorm(x, axis=-1, eps=1e-05):
    m = jnp.mean(x, axis=axis, keepdims=True)
    v = jnp.var(x, axis=axis, keepdims=True)
    return (x - m) / jnp.sqrt(v + eps)

def _scatter_add(tgt, idx, src, axis=0):
    return tgt.at[idx].add(src)

def _segment_sum(src, seg, n):
    return jax.ops.segment_sum(src, seg, n)
kernel_name = 'mk_gnn_resnorm_d4_gnn_r64_6f8198'

def setup_inputs(seed: int=0):
    np.random.seed(seed)
    _w = jnp.asarray

    def _rec_inputs():
        import jax
        import jax.numpy as jnp
        _gk = jax.random.key(seed)
        x = -0.0004287 + 1 * jax.random.normal(jax.random.fold_in(_gk, 1), (25000, 160), jnp.float32)
        src = jax.random.randint(jax.random.fold_in(_gk, 2), (12500,), 0, 25000, jnp.int32)
        dst = jax.random.randint(jax.random.fold_in(_gk, 3), (12500,), 0, 25000, jnp.int32)
        _o = jnp.argsort(dst, stable=True)
        src = src[_o]
        dst = dst[_o]
        edge_attr_10 = jax.random.uniform(jax.random.fold_in(_gk, 12), (12500, 10), jnp.float32, 0.0, 1)
        edge_attr_16 = jax.random.uniform(jax.random.fold_in(_gk, 13), (12500, 16), jnp.float32, 0.0, 1)
        edge_attr_4 = 0.000452788 + 0.999756 * jax.random.normal(jax.random.fold_in(_gk, 14), (12500, 4), jnp.float32)
        edge_attr_8 = jax.random.uniform(jax.random.fold_in(_gk, 15), (12500, 8), jnp.float32, 0.0, 1)
        node_vec1 = jax.random.uniform(jax.random.fold_in(_gk, 17), (25000, 1), jnp.float32, 0.0, 1)
        return (x, src, dst, edge_attr_10, edge_attr_16, edge_attr_4, edge_attr_8, node_vec1)
    x, src, dst, edge_attr_10, edge_attr_16, edge_attr_4, edge_attr_8, node_vec1 = _rec_inputs()

    def _L0_gnn_setup():
        import jax, jax.numpy as jnp
        import numpy as np
        N = 25000
        E = 6250
        MUL_S, MUL_V = (64, 32)
        NB, NH = (8, 64)
        WNUM = 64 + 64 + 32 + 32 + 32
        AVG_NEI = 16.0
        EPS = 1e-05
        INV_SQRT3 = 1.0 / np.sqrt(3.0)
        INV_SQRT2 = 1.0 / np.sqrt(2.0)

        def _split(x):
            return (x[:, :MUL_S], x[:, MUL_S:].reshape(-1, MUL_V, 3))

        def _forward(node_hiddens, edge_sh, edge_attr, W1_0, W1_1, Wfc1, Wfc2, Wfc3, W2_0, W2_1, Wsc0, Wsc1, g0, g1, edge_src, edge_dst):
            s_in, v_in = _split(node_hiddens)
            sc_s = s_in @ Wsc0 / np.sqrt(MUL_S)
            sc_v = jnp.einsum('nuc,uv->nvc', v_in, Wsc1) / np.sqrt(MUL_V)
            s = s_in @ W1_0 / np.sqrt(MUL_S)
            v = jnp.einsum('nuc,uv->nvc', v_in, W1_1) / np.sqrt(MUL_V)
            h = jax.nn.silu(edge_attr @ Wfc1 / np.sqrt(NB))
            h = jax.nn.silu(h @ Wfc2 / np.sqrt(NH))
            w = h @ Wfc3 / np.sqrt(NH)
            w0, w1, w2 = (w[:, :64], w[:, 64:128], w[:, 128:160])
            w3, w4 = (w[:, 160:192], w[:, 192:224])
            sd = s[edge_dst]
            vd = v[edge_dst]
            sh0 = edge_sh[:, :1]
            sh1 = edge_sh[:, 1:4]
            m0 = w0 * sd * sh0
            m1 = w3 * jnp.sum(vd * sh1[:, None, :], -1) * INV_SQRT3
            mv0 = (w1 * sd)[:, :, None] * sh1[:, None, :]
            mv1 = w2[:, :, None] * vd * sh0[:, :, None]
            sh1b = jnp.broadcast_to(sh1[:, None, :], vd.shape)
            mv2 = w4[:, :, None] * jnp.cross(vd, sh1b) * INV_SQRT2
            mid_s = jnp.concatenate([m0, m1], -1)
            mid_v = jnp.concatenate([mv0, mv1, mv2], 1)
            ns = jax.ops.segment_sum(mid_s, edge_src, num_segments=N) / np.sqrt(AVG_NEI)
            nv = jax.ops.segment_sum(mid_v, edge_src, num_segments=N) / np.sqrt(AVG_NEI)
            out_s = ns @ W2_0 / np.sqrt(96) + sc_s
            out_v = jnp.einsum('nuc,uv->nvc', nv, W2_1) / np.sqrt(128) + sc_v
            rms_s = jnp.sqrt(jnp.mean(out_s ** 2, -1, keepdims=True) + EPS)
            out_s = out_s / rms_s * g0
            rms_v = jnp.sqrt(jnp.mean(jnp.sum(out_v ** 2, -1), -1) + EPS)
            out_v = out_v / rms_v[:, None, None] * g1[None, :, None]
            return jnp.concatenate([out_s, out_v.reshape(-1, 3 * MUL_V)], -1)
        key = jax.random.key(seed)
        ks = jax.random.split(key, 16)
        inp = {}
        inp['node_hiddens'] = jax.random.normal(ks[0], (N, MUL_S + 3 * MUL_V), jnp.float32)
        inp['edge_index'] = jax.random.randint(ks[1], (2, E), 0, N)
        inp['edge_sh'] = jax.random.normal(ks[2], (E, 4), jnp.float32)
        inp['edge_attr'] = jax.random.uniform(ks[3], (E, NB), jnp.float32)
        inp['W1_0'] = jax.random.normal(ks[4], (MUL_S, MUL_S), jnp.float32)
        inp['W1_1'] = jax.random.normal(ks[5], (MUL_V, MUL_V), jnp.float32)
        inp['Wfc1'] = jax.random.normal(ks[6], (NB, NH), jnp.float32)
        inp['Wfc2'] = jax.random.normal(ks[7], (NH, NH), jnp.float32)
        inp['Wfc3'] = jax.random.normal(ks[8], (NH, WNUM), jnp.float32)
        inp['W2_0'] = jax.random.normal(ks[9], (96, MUL_S), jnp.float32)
        inp['W2_1'] = jax.random.normal(ks[10], (128, MUL_V), jnp.float32)
        inp['Wsc0'] = jax.random.normal(ks[11], (MUL_S, MUL_S), jnp.float32)
        inp['Wsc1'] = jax.random.normal(ks[12], (MUL_V, MUL_V), jnp.float32)
        inp['g0'] = jnp.ones((MUL_S,), jnp.float32)
        inp['g1'] = jnp.ones((MUL_V,), jnp.float32)
        return inp
    _L0_gnn_all = _L0_gnn_setup()
    _L0_gnn_in = {k: v for k, v in _L0_gnn_all.items() if k in ('W1_0', 'W1_1', 'Wfc1', 'Wfc2', 'Wfc3', 'W2_0', 'W2_1', 'Wsc0', 'Wsc1', 'g0', 'g1')}
    del _L0_gnn_all

    def _L1_gnn_setup():
        import jax, jax.numpy as jnp
        import numpy as np
        N_NODES = 50000
        N_EDGES = 12500
        MUL0, MUL1 = (64, 32)
        N_BASIS, N_RADIAL = (10, 100)
        W_NUMEL = 192
        NUM_NEIGHBORS = 16.0
        INV_SQRT3 = np.float32(1.0 / np.sqrt(3.0))
        RELU_GAIN = np.float32(np.sqrt(2.0))
        FAN_L2 = np.float32(np.sqrt(MUL0 + MUL1))

        def _fctp_scalar_attr(x0, x1, a, W0, W1):
            o0 = x0 @ W0 * a * (1.0 / np.sqrt(W0.shape[0]))
            o1 = jnp.einsum('nud,uw->nwd', x1, W1) * a[..., None] * (1.0 / np.sqrt(W1.shape[0]))
            return (o0, o1)
        key = jax.random.key(seed)
        ks = jax.random.split(key, 16)
        return {'node_input': jax.random.normal(ks[0], (N_NODES, MUL0 + 3 * MUL1), jnp.float32), 'node_attr': jnp.ones((N_NODES, 1), jnp.float32), 'edge_attr': jax.random.normal(ks[1], (N_EDGES, 4), jnp.float32), 'edge_length_embedded': jax.random.uniform(ks[2], (N_EDGES, N_BASIS), dtype=jnp.float32), 'W_si0': jax.random.normal(ks[3], (MUL0, MUL0), jnp.float32), 'W_si1': jax.random.normal(ks[4], (MUL1, MUL1), jnp.float32), 'W_l1_0': jax.random.normal(ks[5], (MUL0, MUL0), jnp.float32), 'W_l1_1': jax.random.normal(ks[6], (MUL1, MUL1), jnp.float32), 'W_l2_00': jax.random.normal(ks[7], (MUL0, MUL0), jnp.float32), 'W_l2_10': jax.random.normal(ks[8], (MUL1, MUL0), jnp.float32), 'W_l2_01': jax.random.normal(ks[9], (MUL0, MUL1), jnp.float32), 'W_l2_11': jax.random.normal(ks[10], (MUL1, MUL1), jnp.float32), 'W_fc1': jax.random.normal(ks[11], (N_BASIS, N_RADIAL), jnp.float32), 'W_fc2': jax.random.normal(ks[12], (N_RADIAL, W_NUMEL), jnp.float32), 'edge_src': jax.random.randint(ks[13], (N_EDGES,), 0, N_NODES), 'edge_dst': jax.random.randint(ks[14], (N_EDGES,), 0, N_NODES)}
    _L1_gnn_all = _L1_gnn_setup()
    _L1_gnn_in = {k: v for k, v in _L1_gnn_all.items() if k in ('W_si0', 'W_si1', 'W_l1_0', 'W_l1_1', 'W_l2_00', 'W_l2_10', 'W_l2_01', 'W_l2_11', 'W_fc1', 'W_fc2')}
    del _L1_gnn_all

    def _L2_gnn_setup():
        import jax, jax.numpy as jnp
        import numpy as np
        N, E = (20000, 5000)
        CS, CV = (64, 32)
        AS_, AV, H = (16, 8, 4)
        NB = 16
        SQRT3 = 1.7320508075688772
        SQRT2 = 1.4142135623730951
        EPS = 1e-05

        def _cg_tp(s, v, y0, y1, w_ss, w_sv, w_vs, w_vv0, w_vv1):
            out_s = jnp.concatenate([w_ss * s * y0[:, None], w_vv0 * (jnp.einsum('eci,ei->ec', v, y1) / SQRT3)], axis=-1)
            out_v = jnp.concatenate([(w_sv * s)[:, :, None] * y1[:, None, :], (w_vs * jnp.ones_like(v[..., 0]))[..., None] * v * y0[:, None, None], (w_vv1 * jnp.ones_like(v[..., 0]))[..., None] * (jnp.cross(v, y1[:, None, :]) / SQRT2)], axis=1)
            return (out_s, out_v)

        def _equiv_layernorm(s, v, gamma_s, beta_s, gamma_v):
            mu = jnp.mean(s, axis=-1, keepdims=True)
            var = jnp.var(s, axis=-1, keepdims=True)
            s_n = (s - mu) * jax.lax.rsqrt(var + EPS) * gamma_s + beta_s
            rms = jnp.sqrt(jnp.mean(jnp.sum(v * v, axis=-1), axis=-1, keepdims=True) + EPS)
            v_n = v / rms[..., None] * gamma_v[None, :, None]
            return (s_n, v_n)
        key = jax.random.key(seed)
        ks = jax.random.split(key, 26)

        def rn(k, shape, fan):
            return jax.random.normal(k, shape, jnp.float32) / np.sqrt(fan)
        D1S, D1V = (CS + CV, CS + 2 * CV)
        WN = 2 * CS + 3 * CV
        inp = {'node': jax.random.normal(ks[0], (N, CS + 3 * CV), jnp.float32), 'edge_index': jax.random.randint(ks[1], (2, E), 0, N, jnp.int64 if jax.config.jax_enable_x64 else jnp.int32), 'rbf': jax.random.uniform(ks[2], (E, NB), jnp.float32), 'rsh': jax.random.normal(ks[3], (E, 4), jnp.float32), 'gamma_s': jnp.ones((CS,), jnp.float32), 'beta_s': jnp.zeros((CS,), jnp.float32), 'gamma_v': jnp.ones((CV,), jnp.float32), 'Ws_src': rn(ks[4], (CS, CS), CS), 'Wv_src': rn(ks[5], (CV, CV), CV), 'Ws_dst': rn(ks[6], (CS, CS), CS), 'Wv_dst': rn(ks[7], (CV, CV), CV), 'W_rbf': rn(ks[8], (NB, WN), NB), 'W_alpha': rn(ks[9], (D1S, H * AS_), D1S), 'alpha_dot': rn(ks[10], (1, H, AS_), AS_), 'Ws_val': rn(ks[11], (D1S, CS), D1S), 'Wv_val': rn(ks[12], (D1V, CV), D1V), 'Wg': rn(ks[13], (CS, CV), CS), 'w2_ss': rn(ks[14], (CS,), 1), 'w2_sv': rn(ks[15], (CS,), 1), 'w2_vs': rn(ks[16], (CV,), 1), 'w2_vv0': rn(ks[17], (CV,), 1), 'w2_vv1': rn(ks[18], (CV,), 1), 'Ws_vlin': rn(ks[19], (D1S, H * AS_), D1S), 'Wv_vlin': rn(ks[20], (D1V, H * AV), D1V), 'Wps': rn(ks[21], (H * AS_, CS), H * AS_), 'Wpv': rn(ks[22], (H * AV, CV), H * AV)}
        return inp
    _L2_gnn_all = _L2_gnn_setup()
    _L2_gnn_in = {k: v for k, v in _L2_gnn_all.items() if k in ('gamma_s', 'beta_s', 'gamma_v', 'Ws_src', 'Wv_src', 'Ws_dst', 'Wv_dst', 'W_rbf', 'W_alpha', 'alpha_dot', 'Ws_val', 'Wv_val', 'Wg', 'w2_ss', 'w2_sv', 'w2_vs', 'w2_vv0', 'w2_vv1', 'Ws_vlin', 'Wv_vlin', 'Wps', 'Wpv')}
    del _L2_gnn_all

    def _L3_gnn_setup():
        import jax, jax.numpy as jnp
        import numpy as np
        MUL0, MUL1 = (64, 32)
        INV_SQRT3 = 1.0 / np.sqrt(3.0)

        def _split(x):
            return (x[:, :MUL0], x[:, MUL0:].reshape(x.shape[0], MUL1, 3))

        def _merge(o0, o1):
            return jnp.concatenate([o0, o1.reshape(o1.shape[0], -1)], axis=-1)

        def _tp(x0, x1, y0, y1, w000, w011, w101, w110):
            fan0 = x0.shape[1] * y0.shape[1] + x1.shape[1] * y1.shape[1]
            fan1 = x0.shape[1] * y1.shape[1] + x1.shape[1] * y0.shape[1]
            out0 = (jnp.einsum('eu,ev,uvw->ew', x0, y0, w000) + INV_SQRT3 * jnp.einsum('euk,evk,uvw->ew', x1, y1, w110)) / np.sqrt(fan0)
            out1 = (jnp.einsum('eu,evk,uvw->ewk', x0, y1, w011) + jnp.einsum('euk,ev,uvw->ewk', x1, y0, w101)) / np.sqrt(fan1)
            return (out0, out1)

        def _lin(x0, x1, w0, w1):
            return (x0 @ w0 / np.sqrt(x0.shape[1]), jnp.einsum('euk,uv->evk', x1, w1) / np.sqrt(x1.shape[1]))
        key = jax.random.key(seed)
        ks = jax.random.split(key, 20)
        N, E = (50000, 500000)
        inp = {'node_features': jax.random.normal(ks[0], (N, MUL0 + 3 * MUL1), dtype=jnp.float32), 'edge_index': jax.random.randint(ks[1], (2, E), 0, N, dtype=jnp.int64), 'edge_attr_tensor': jax.random.normal(ks[2], (E, 4), dtype=jnp.float32), 'node_attr_scalar_raw': jax.random.normal(ks[3], (N, 1), dtype=jnp.float32), 'wm000': jax.random.normal(ks[4], (MUL0, 1, MUL0), dtype=jnp.float32), 'wm011': jax.random.normal(ks[5], (MUL0, 1, MUL1), dtype=jnp.float32), 'wm101': jax.random.normal(ks[6], (MUL1, 1, MUL1), dtype=jnp.float32), 'wm110': jax.random.normal(ks[7], (MUL1, 1, MUL0), dtype=jnp.float32), 'lm0': jax.random.normal(ks[8], (MUL0, MUL0), dtype=jnp.float32), 'lm1': jax.random.normal(ks[9], (MUL1, MUL1), dtype=jnp.float32), 'wu000': jax.random.normal(ks[10], (MUL0, MUL0, MUL0), dtype=jnp.float32), 'wu011': jax.random.normal(ks[11], (MUL0, MUL1, MUL1), dtype=jnp.float32), 'wu101': jax.random.normal(ks[12], (MUL1, MUL0, MUL1), dtype=jnp.float32), 'wu110': jax.random.normal(ks[13], (MUL1, MUL1, MUL0), dtype=jnp.float32), 'lu0': jax.random.normal(ks[14], (MUL0, MUL0), dtype=jnp.float32), 'lu1': jax.random.normal(ks[15], (MUL1, MUL1), dtype=jnp.float32)}
        return inp
    _L3_gnn_all = _L3_gnn_setup()
    _L3_gnn_in = {k: v for k, v in _L3_gnn_all.items() if k in ('wm000', 'wm011', 'wm101', 'wm110', 'lm0', 'lm1', 'wu000', 'wu011', 'wu101', 'wu110', 'lu0', 'lu1')}
    del _L3_gnn_all
    return {'x': x, 'src': src, 'dst': dst, 'edge_attr_10': edge_attr_10, 'edge_attr_16': edge_attr_16, 'edge_attr_4': edge_attr_4, 'edge_attr_8': edge_attr_8, 'node_vec1': node_vec1, 'L0_gnn_W1_0': _L0_gnn_in['W1_0'], 'L0_gnn_W1_1': _L0_gnn_in['W1_1'], 'L0_gnn_Wfc1': _L0_gnn_in['Wfc1'], 'L0_gnn_Wfc2': _L0_gnn_in['Wfc2'], 'L0_gnn_Wfc3': _L0_gnn_in['Wfc3'], 'L0_gnn_W2_0': _L0_gnn_in['W2_0'], 'L0_gnn_W2_1': _L0_gnn_in['W2_1'], 'L0_gnn_Wsc0': _L0_gnn_in['Wsc0'], 'L0_gnn_Wsc1': _L0_gnn_in['Wsc1'], 'L0_gnn_g0': _L0_gnn_in['g0'], 'L0_gnn_g1': _L0_gnn_in['g1'], 'L1_gnn_W_si0': _L1_gnn_in['W_si0'], 'L1_gnn_W_si1': _L1_gnn_in['W_si1'], 'L1_gnn_W_l1_0': _L1_gnn_in['W_l1_0'], 'L1_gnn_W_l1_1': _L1_gnn_in['W_l1_1'], 'L1_gnn_W_l2_00': _L1_gnn_in['W_l2_00'], 'L1_gnn_W_l2_10': _L1_gnn_in['W_l2_10'], 'L1_gnn_W_l2_01': _L1_gnn_in['W_l2_01'], 'L1_gnn_W_l2_11': _L1_gnn_in['W_l2_11'], 'L1_gnn_W_fc1': _L1_gnn_in['W_fc1'], 'L1_gnn_W_fc2': _L1_gnn_in['W_fc2'], 'L2_gnn_gamma_s': _L2_gnn_in['gamma_s'], 'L2_gnn_beta_s': _L2_gnn_in['beta_s'], 'L2_gnn_gamma_v': _L2_gnn_in['gamma_v'], 'L2_gnn_Ws_src': _L2_gnn_in['Ws_src'], 'L2_gnn_Wv_src': _L2_gnn_in['Wv_src'], 'L2_gnn_Ws_dst': _L2_gnn_in['Ws_dst'], 'L2_gnn_Wv_dst': _L2_gnn_in['Wv_dst'], 'L2_gnn_W_rbf': _L2_gnn_in['W_rbf'], 'L2_gnn_W_alpha': _L2_gnn_in['W_alpha'], 'L2_gnn_alpha_dot': _L2_gnn_in['alpha_dot'], 'L2_gnn_Ws_val': _L2_gnn_in['Ws_val'], 'L2_gnn_Wv_val': _L2_gnn_in['Wv_val'], 'L2_gnn_Wg': _L2_gnn_in['Wg'], 'L2_gnn_w2_ss': _L2_gnn_in['w2_ss'], 'L2_gnn_w2_sv': _L2_gnn_in['w2_sv'], 'L2_gnn_w2_vs': _L2_gnn_in['w2_vs'], 'L2_gnn_w2_vv0': _L2_gnn_in['w2_vv0'], 'L2_gnn_w2_vv1': _L2_gnn_in['w2_vv1'], 'L2_gnn_Ws_vlin': _L2_gnn_in['Ws_vlin'], 'L2_gnn_Wv_vlin': _L2_gnn_in['Wv_vlin'], 'L2_gnn_Wps': _L2_gnn_in['Wps'], 'L2_gnn_Wpv': _L2_gnn_in['Wpv'], 'L3_gnn_wm000': _L3_gnn_in['wm000'], 'L3_gnn_wm011': _L3_gnn_in['wm011'], 'L3_gnn_wm101': _L3_gnn_in['wm101'], 'L3_gnn_wm110': _L3_gnn_in['wm110'], 'L3_gnn_lm0': _L3_gnn_in['lm0'], 'L3_gnn_lm1': _L3_gnn_in['lm1'], 'L3_gnn_wu000': _L3_gnn_in['wu000'], 'L3_gnn_wu011': _L3_gnn_in['wu011'], 'L3_gnn_wu101': _L3_gnn_in['wu101'], 'L3_gnn_wu110': _L3_gnn_in['wu110'], 'L3_gnn_lu0': _L3_gnn_in['lu0'], 'L3_gnn_lu1': _L3_gnn_in['lu1']}

def reference(x, src, dst, edge_attr_10, edge_attr_16, edge_attr_4, edge_attr_8, node_vec1, L0_gnn_W1_0, L0_gnn_W1_1, L0_gnn_Wfc1, L0_gnn_Wfc2, L0_gnn_Wfc3, L0_gnn_W2_0, L0_gnn_W2_1, L0_gnn_Wsc0, L0_gnn_Wsc1, L0_gnn_g0, L0_gnn_g1, L1_gnn_W_si0, L1_gnn_W_si1, L1_gnn_W_l1_0, L1_gnn_W_l1_1, L1_gnn_W_l2_00, L1_gnn_W_l2_10, L1_gnn_W_l2_01, L1_gnn_W_l2_11, L1_gnn_W_fc1, L1_gnn_W_fc2, L2_gnn_gamma_s, L2_gnn_beta_s, L2_gnn_gamma_v, L2_gnn_Ws_src, L2_gnn_Wv_src, L2_gnn_Ws_dst, L2_gnn_Wv_dst, L2_gnn_W_rbf, L2_gnn_W_alpha, L2_gnn_alpha_dot, L2_gnn_Ws_val, L2_gnn_Wv_val, L2_gnn_Wg, L2_gnn_w2_ss, L2_gnn_w2_sv, L2_gnn_w2_vs, L2_gnn_w2_vv0, L2_gnn_w2_vv1, L2_gnn_Ws_vlin, L2_gnn_Wv_vlin, L2_gnn_Wps, L2_gnn_Wpv, L3_gnn_wm000, L3_gnn_wm011, L3_gnn_wm101, L3_gnn_wm110, L3_gnn_lm0, L3_gnn_lm1, L3_gnn_wu000, L3_gnn_wu011, L3_gnn_wu101, L3_gnn_wu110, L3_gnn_lu0, L3_gnn_lu1):
    import jax
    import jax.numpy as jnp

    def _L0_gnn_ref(node_hiddens, edge_index, edge_sh, edge_attr, W1_0, W1_1, Wfc1, Wfc2, Wfc3, W2_0, W2_1, Wsc0, Wsc1, g0, g1):
        import jax, jax.numpy as jnp
        import numpy as np
        N = 25000
        E = 6250
        MUL_S, MUL_V = (64, 32)
        NB, NH = (8, 64)
        WNUM = 64 + 64 + 32 + 32 + 32
        AVG_NEI = 16.0
        EPS = 1e-05
        INV_SQRT3 = 1.0 / np.sqrt(3.0)
        INV_SQRT2 = 1.0 / np.sqrt(2.0)

        def _split(x):
            return (x[:, :MUL_S], x[:, MUL_S:].reshape(-1, MUL_V, 3))

        def _forward(node_hiddens, edge_sh, edge_attr, W1_0, W1_1, Wfc1, Wfc2, Wfc3, W2_0, W2_1, Wsc0, Wsc1, g0, g1, edge_src, edge_dst):
            s_in, v_in = _split(node_hiddens)
            sc_s = s_in @ Wsc0 / np.sqrt(MUL_S)
            sc_v = jnp.einsum('nuc,uv->nvc', v_in, Wsc1) / np.sqrt(MUL_V)
            s = s_in @ W1_0 / np.sqrt(MUL_S)
            v = jnp.einsum('nuc,uv->nvc', v_in, W1_1) / np.sqrt(MUL_V)
            h = jax.nn.silu(edge_attr @ Wfc1 / np.sqrt(NB))
            h = jax.nn.silu(h @ Wfc2 / np.sqrt(NH))
            w = h @ Wfc3 / np.sqrt(NH)
            w0, w1, w2 = (w[:, :64], w[:, 64:128], w[:, 128:160])
            w3, w4 = (w[:, 160:192], w[:, 192:224])
            sd = s[edge_dst]
            vd = v[edge_dst]
            sh0 = edge_sh[:, :1]
            sh1 = edge_sh[:, 1:4]
            m0 = w0 * sd * sh0
            m1 = w3 * jnp.sum(vd * sh1[:, None, :], -1) * INV_SQRT3
            mv0 = (w1 * sd)[:, :, None] * sh1[:, None, :]
            mv1 = w2[:, :, None] * vd * sh0[:, :, None]
            sh1b = jnp.broadcast_to(sh1[:, None, :], vd.shape)
            mv2 = w4[:, :, None] * jnp.cross(vd, sh1b) * INV_SQRT2
            mid_s = jnp.concatenate([m0, m1], -1)
            mid_v = jnp.concatenate([mv0, mv1, mv2], 1)
            ns = jax.ops.segment_sum(mid_s, edge_src, num_segments=N) / np.sqrt(AVG_NEI)
            nv = jax.ops.segment_sum(mid_v, edge_src, num_segments=N) / np.sqrt(AVG_NEI)
            out_s = ns @ W2_0 / np.sqrt(96) + sc_s
            out_v = jnp.einsum('nuc,uv->nvc', nv, W2_1) / np.sqrt(128) + sc_v
            rms_s = jnp.sqrt(jnp.mean(out_s ** 2, -1, keepdims=True) + EPS)
            out_s = out_s / rms_s * g0
            rms_v = jnp.sqrt(jnp.mean(jnp.sum(out_v ** 2, -1), -1) + EPS)
            out_v = out_v / rms_v[:, None, None] * g1[None, :, None]
            return jnp.concatenate([out_s, out_v.reshape(-1, 3 * MUL_V)], -1)
        edge_src = edge_index[0]
        edge_dst = edge_index[1]
        return _forward(node_hiddens, edge_sh, edge_attr, W1_0, W1_1, Wfc1, Wfc2, Wfc3, W2_0, W2_1, Wsc0, Wsc1, g0, g1, edge_src, edge_dst)

    def _L1_gnn_ref(node_input, node_attr, edge_src, edge_dst, edge_attr, edge_length_embedded, W_si0, W_si1, W_l1_0, W_l1_1, W_l2_00, W_l2_10, W_l2_01, W_l2_11, W_fc1, W_fc2):
        import jax, jax.numpy as jnp
        import numpy as np
        N_NODES = 50000
        N_EDGES = 12500
        MUL0, MUL1 = (64, 32)
        N_BASIS, N_RADIAL = (10, 100)
        W_NUMEL = 192
        NUM_NEIGHBORS = 16.0
        INV_SQRT3 = np.float32(1.0 / np.sqrt(3.0))
        RELU_GAIN = np.float32(np.sqrt(2.0))
        FAN_L2 = np.float32(np.sqrt(MUL0 + MUL1))

        def _fctp_scalar_attr(x0, x1, a, W0, W1):
            o0 = x0 @ W0 * a * (1.0 / np.sqrt(W0.shape[0]))
            o1 = jnp.einsum('nud,uw->nwd', x1, W1) * a[..., None] * (1.0 / np.sqrt(W1.shape[0]))
            return (o0, o1)
        N = node_input.shape[0]
        x0 = node_input[:, :MUL0]
        x1 = node_input[:, MUL0:].reshape(N, MUL1, 3)
        a = node_attr
        h = jax.nn.relu(edge_length_embedded @ W_fc1 * (1.0 / np.sqrt(N_BASIS))) * RELU_GAIN
        w = h @ W_fc2 * (1.0 / np.sqrt(N_RADIAL))
        w0, w1, w2, w3 = (w[:, :64], w[:, 64:128], w[:, 128:160], w[:, 160:192])
        si0, si1 = _fctp_scalar_attr(x0, x1, a, W_si0, W_si1)
        l0, l1 = _fctp_scalar_attr(x0, x1, a, W_l1_0, W_l1_1)
        y0 = l0[edge_src]
        y1 = l1[edge_src]
        e0 = edge_attr[:, :1]
        e1 = edge_attr[:, 1:4]
        m0 = w0 * y0 * e0
        m1 = (w1 * y0)[:, :, None] * e1[:, None, :]
        m2 = (w2 * e0)[:, :, None] * y1
        m3 = w3 * jnp.einsum('eud,ed->eu', y1, e1) * INV_SQRT3
        inv = np.float32(1.0 / np.sqrt(NUM_NEIGHBORS))
        s0 = jax.ops.segment_sum(m0, edge_dst, num_segments=N) * inv
        s1 = jax.ops.segment_sum(m1, edge_dst, num_segments=N) * inv
        s2 = jax.ops.segment_sum(m2, edge_dst, num_segments=N) * inv
        s3 = jax.ops.segment_sum(m3, edge_dst, num_segments=N) * inv
        o0 = (s0 @ W_l2_00 + s3 @ W_l2_10) * a / FAN_L2
        o1 = (jnp.einsum('nud,uw->nwd', s1, W_l2_01) + jnp.einsum('nud,uw->nwd', s2, W_l2_11)) * a[..., None] / FAN_L2
        out0 = si0 + 0.5 * o0
        out1 = si1 + 0.5 * o1
        return jnp.concatenate([out0, out1.reshape(N, 3 * MUL1)], axis=1)

    def _L2_gnn_ref(node, rbf, rsh, gamma_s, beta_s, gamma_v, Ws_src, Wv_src, Ws_dst, Wv_dst, W_rbf, W_alpha, alpha_dot, Ws_val, Wv_val, Wg, w2_ss, w2_sv, w2_vs, w2_vv0, w2_vv1, Ws_vlin, Wv_vlin, Wps, Wpv, edge_index):
        import jax, jax.numpy as jnp
        import numpy as np
        N, E = (20000, 5000)
        CS, CV = (64, 32)
        AS_, AV, H = (16, 8, 4)
        NB = 16
        SQRT3 = 1.7320508075688772
        SQRT2 = 1.4142135623730951
        EPS = 1e-05

        def _cg_tp(s, v, y0, y1, w_ss, w_sv, w_vs, w_vv0, w_vv1):
            out_s = jnp.concatenate([w_ss * s * y0[:, None], w_vv0 * (jnp.einsum('eci,ei->ec', v, y1) / SQRT3)], axis=-1)
            out_v = jnp.concatenate([(w_sv * s)[:, :, None] * y1[:, None, :], (w_vs * jnp.ones_like(v[..., 0]))[..., None] * v * y0[:, None, None], (w_vv1 * jnp.ones_like(v[..., 0]))[..., None] * (jnp.cross(v, y1[:, None, :]) / SQRT2)], axis=1)
            return (out_s, out_v)

        def _equiv_layernorm(s, v, gamma_s, beta_s, gamma_v):
            mu = jnp.mean(s, axis=-1, keepdims=True)
            var = jnp.var(s, axis=-1, keepdims=True)
            s_n = (s - mu) * jax.lax.rsqrt(var + EPS) * gamma_s + beta_s
            rms = jnp.sqrt(jnp.mean(jnp.sum(v * v, axis=-1), axis=-1, keepdims=True) + EPS)
            v_n = v / rms[..., None] * gamma_v[None, :, None]
            return (s_n, v_n)
        n = node.shape[0]
        e = rsh.shape[0]
        s = node[:, :CS]
        v = node[:, CS:].reshape(n, CV, 3)
        s_n, v_n = _equiv_layernorm(s, v, gamma_s, beta_s, gamma_v)
        src, dst = (edge_index[0], edge_index[1])
        msg_s = (s_n @ Ws_src)[src] + (s_n @ Ws_dst)[dst]
        msg_v = jnp.einsum('ncx,cd->ndx', v_n, Wv_src)[src] + jnp.einsum('ncx,cd->ndx', v_n, Wv_dst)[dst]
        y0, y1 = (rsh[:, 0], rsh[:, 1:4])
        w1 = rbf @ W_rbf
        m1_s, m1_v = _cg_tp(msg_s, msg_v, y0, y1, w1[:, :CS], w1[:, CS:2 * CS], w1[:, 2 * CS:2 * CS + CV], w1[:, 2 * CS + CV:2 * CS + 2 * CV], w1[:, 2 * CS + 2 * CV:])
        a = (m1_s @ W_alpha).reshape(e, H, AS_)
        a = jnp.where(a > 0, a, 0.2 * a)
        a = jnp.sum(a * alpha_dot, axis=-1, keepdims=True)
        amax = jax.ops.segment_max(a, dst, num_segments=n)
        amax = jnp.where(jnp.isfinite(amax), amax, 0.0)
        ex = jnp.exp(a - amax[dst])
        den = jax.ops.segment_sum(ex, dst, num_segments=n)
        alpha = ex / (den[dst] + 1e-16)
        val_s = m1_s @ Ws_val
        val_v = jnp.einsum('ecx,cd->edx', m1_v, Wv_val)
        val_v = val_v * jax.nn.sigmoid(val_s @ Wg)[..., None]
        val_s = jax.nn.sigmoid(val_s)
        m2_s, m2_v = _cg_tp(val_s, val_v, y0, y1, w2_ss, w2_sv, w2_vs, w2_vv0, w2_vv1)
        hs = (m2_s @ Ws_vlin).reshape(e, H, AS_)
        hv = jnp.einsum('ecx,cd->edx', m2_v, Wv_vlin).reshape(e, H, AV, 3)
        h = jnp.concatenate([hs, hv.reshape(e, H, AV * 3)], axis=-1)
        agg = jax.ops.segment_sum(alpha * h, dst, num_segments=n)
        agg_s = agg[:, :, :AS_].reshape(n, H * AS_)
        agg_v = agg[:, :, AS_:].reshape(n, H * AV, 3)
        out = node + jnp.concatenate([agg_s @ Wps, jnp.einsum('ncx,cd->ndx', agg_v, Wpv).reshape(n, CV * 3)], axis=-1)
        return out

    def _L3_gnn_ref(node_features, edge_index, edge_attr_tensor, node_attr_scalar_raw, wm000, wm011, wm101, wm110, lm0, lm1, wu000, wu011, wu101, wu110, lu0, lu1):
        import jax, jax.numpy as jnp
        import numpy as np
        MUL0, MUL1 = (64, 32)
        INV_SQRT3 = 1.0 / np.sqrt(3.0)

        def _split(x):
            return (x[:, :MUL0], x[:, MUL0:].reshape(x.shape[0], MUL1, 3))

        def _merge(o0, o1):
            return jnp.concatenate([o0, o1.reshape(o1.shape[0], -1)], axis=-1)

        def _tp(x0, x1, y0, y1, w000, w011, w101, w110):
            fan0 = x0.shape[1] * y0.shape[1] + x1.shape[1] * y1.shape[1]
            fan1 = x0.shape[1] * y1.shape[1] + x1.shape[1] * y0.shape[1]
            out0 = (jnp.einsum('eu,ev,uvw->ew', x0, y0, w000) + INV_SQRT3 * jnp.einsum('euk,evk,uvw->ew', x1, y1, w110)) / np.sqrt(fan0)
            out1 = (jnp.einsum('eu,evk,uvw->ewk', x0, y1, w011) + jnp.einsum('euk,ev,uvw->ewk', x1, y0, w101)) / np.sqrt(fan1)
            return (out0, out1)

        def _lin(x0, x1, w0, w1):
            return (x0 @ w0 / np.sqrt(x0.shape[1]), jnp.einsum('euk,uv->evk', x1, w1) / np.sqrt(x1.shape[1]))
        N = node_features.shape[0]
        row, col = (edge_index[0], edge_index[1])
        r_vec = edge_attr_tensor[:, :3]
        dist = edge_attr_tensor[:, 3:4]
        e0 = dist
        e1 = r_vec[:, None, :]
        xj0, xj1 = _split(node_features[col])
        m0, m1 = _tp(xj0, xj1, e0, e1, wm000, wm011, wm101, wm110)
        d0, d1 = _lin(xj0, xj1, lm0, lm1)
        msgs = _merge(m0 + d0, m1 + d1)
        agg = jax.ops.segment_sum(msgs, row, num_segments=N)
        a0, a1 = _split(agg)
        x0, x1 = _split(node_features)
        u0, u1 = _tp(x0, x1, a0, a1, wu000, wu011, wu101, wu110)
        ud0, ud1 = _lin(x0, x1, lu0, lu1)
        return node_features + _merge(u0 + ud0, u1 + ud1)
    edge_index = jnp.stack([src, dst])
    x = _layernorm(x + _L0_gnn_ref(x, edge_index, edge_attr_4, edge_attr_8, L0_gnn_W1_0, L0_gnn_W1_1, L0_gnn_Wfc1, L0_gnn_Wfc2, L0_gnn_Wfc3, L0_gnn_W2_0, L0_gnn_W2_1, L0_gnn_Wsc0, L0_gnn_Wsc1, L0_gnn_g0, L0_gnn_g1), axis=-1)
    x = _layernorm(x + _L1_gnn_ref(x, node_vec1, src, dst, edge_attr_4, edge_attr_10, L1_gnn_W_si0, L1_gnn_W_si1, L1_gnn_W_l1_0, L1_gnn_W_l1_1, L1_gnn_W_l2_00, L1_gnn_W_l2_10, L1_gnn_W_l2_01, L1_gnn_W_l2_11, L1_gnn_W_fc1, L1_gnn_W_fc2), axis=-1)
    x = _layernorm(x + _L2_gnn_ref(x, edge_attr_16, edge_attr_4, L2_gnn_gamma_s, L2_gnn_beta_s, L2_gnn_gamma_v, L2_gnn_Ws_src, L2_gnn_Wv_src, L2_gnn_Ws_dst, L2_gnn_Wv_dst, L2_gnn_W_rbf, L2_gnn_W_alpha, L2_gnn_alpha_dot, L2_gnn_Ws_val, L2_gnn_Wv_val, L2_gnn_Wg, L2_gnn_w2_ss, L2_gnn_w2_sv, L2_gnn_w2_vs, L2_gnn_w2_vv0, L2_gnn_w2_vv1, L2_gnn_Ws_vlin, L2_gnn_Wv_vlin, L2_gnn_Wps, L2_gnn_Wpv, edge_index), axis=-1)
    x = _layernorm(x + _L3_gnn_ref(x, edge_index, edge_attr_4, node_vec1, L3_gnn_wm000, L3_gnn_wm011, L3_gnn_wm101, L3_gnn_wm110, L3_gnn_lm0, L3_gnn_lm1, L3_gnn_wu000, L3_gnn_wu011, L3_gnn_wu101, L3_gnn_wu110, L3_gnn_lu0, L3_gnn_lu1), axis=-1)
    return x

_drawn_inputs = setup_inputs


def setup_inputs(seed=0):
    import zlib

    import numpy as np

    out = dict(_drawn_inputs(seed))
    spreads = {'L0_gnn_g0': (1.0, 0.2),
     'L0_gnn_g1': (1.0, 0.2),
     'L2_gnn_gamma_s': (1.0, 0.6),
     'L2_gnn_beta_s': (0.0, 0.8),
     'L2_gnn_gamma_v': (1.0, 0.6)}
    factors = {'edge_attr_10': 7.111,
     'edge_attr_8': 5.315,
     'L0_gnn_W1_0': 3.392,
     'L0_gnn_W1_1': 4.727,
     'L0_gnn_Wfc1': 3.082,
     'L0_gnn_W2_0': 3.246,
     'L0_gnn_W2_1': 4.901,
     'L1_gnn_W_l1_0': 4.005,
     'L1_gnn_W_l1_1': 6.904,
     'L1_gnn_W_l2_00': 6.593,
     'L1_gnn_W_l2_10': 8.0,
     'L1_gnn_W_l2_01': 5.219,
     'L1_gnn_W_l2_11': 8.0,
     'L1_gnn_W_fc1': 4.309,
     'L1_gnn_W_fc2': 3.794,
     'L2_gnn_W_alpha': 2.901}
    for name, (base, spread) in spreads.items():
        noise = np.random.default_rng([zlib.crc32(name.encode()), seed]).standard_normal(out[name].shape)
        drawn = base * np.exp(spread * noise) if base else spread * noise
        out[name] = jnp.asarray(drawn.astype(out[name].dtype))
    for name, factor in factors.items():
        out[name] = (out[name] * factor).astype(out[name].dtype)
    return out
```

```python
from contextlib import ExitStack

import numpy as np

import concourse.bass as bass
from concourse import mybir

F32 = mybir.dt.float32
I32 = mybir.dt.int32
ALU = mybir.AluOpType
ACT = mybir.ActivationFunctionType
AX = mybir.AxisListType.X

P = 128
NODES, EDGES = 25000, 12500
F = 160
S, V = 64, 32
NCOL = -(-NODES // P)
NROWS = NCOL * P
ECOL = -(-EDGES // P)
EROWS = ECOL * P
DUMMY = NROWS - 1
HI = -(-NROWS // P)
ROW = 40
A4, A8, A10, A16 = 2, 6, 14, 24
SKIP = 1 << 20
U = 4
GRP = 4
NGRP = NCOL // GRP
EPS = 1e-5
R3, R2 = float(1 / np.sqrt(3.0)), float(1 / np.sqrt(2.0))
Y0, Y1, SAME, FEND, GIDX, GIDX2, WIDX, ESW = 0, 1, 6, 7, 8, 9, 10, 12


class Tile:

    def __init__(self, base, i=None):
        self.base, self.i = base, i

    def is_fix(self):
        return self.i is None and self.base == ECOL

    @property
    def t(self):
        return self.base if self.i is None else self.i * U + self.base

    def slot(self, ring):
        return self.base % ring

    def lap(self, ring):
        n = self.base // ring
        return n if self.i is None else self.i * (U // ring) + n

    def past(self, n):
        return self.base >= n


def sweep(eng, n, stages, depth):
    last = max(st[0] for st in stages)
    lead = last + depth
    lead += (n - lead) % U

    def step(s, i=None):
        for lag, fn, *more in stages:
            if i is not None or 0 <= s - lag < n + sum(more):
                fn(Tile(s - lag, i))

    for s in range(min(lead, n)):
        step(s)
    if n > lead:
        with eng.Fori(0, (n - lead) // U) as i:
            for u in range(U):
                step(lead + u, i)
    for s in range(n, n + last + max(sum(st[2:]) for st in stages)):
        step(s)


class Chain:

    def __init__(self, eng, sem, per, tile):
        self.eng, self.sem, self.per, self.tile, self.n = eng, sem, per, tile, 0

    def __call__(self, ins):
        ins.then_inc(self.sem, 1)
        self.n += 1

    def wait(self, n=None):
        self.eng.wait_ge(self.sem, self.tile.t * self.per + (self.n if n is None else n))


class Shifted:

    def __init__(self, chain, first):
        self.chain, self.first = chain, first

    @property
    def n(self):
        return self.chain.n - self.first

    def __call__(self, ins):
        self.chain(ins)

    def wait(self, n=None):
        self.chain.wait(None if n is None else n + self.first)


class Static:

    def __init__(self, eng, sem):
        self.eng, self.sem, self.n = eng, sem, 0

    def __call__(self, ins, wait=True):
        ins.then_inc(self.sem, 1)
        self.n += 1
        if wait:
            self.eng.wait_ge(self.sem, self.n)


class Mem:
    pass


def scope(nc, ctx, tag):
    sems = []

    def clear():
        if sems:
            nc.clear_and_free_semaphores(sems)
            nc.all_engine_barrier()
    ctx.callback(clear)

    def sb(name, shape, dt=F32):
        return ctx.enter_context(nc.sbuf_tensor(f"{tag}_{name}", shape, dt))

    def ps(name, shape=(P, 512), dt=F32):
        return ctx.enter_context(nc.psum_tensor(f"{tag}_{name}", list(shape), dt))

    def sem(name):
        sems.append(nc.alloc_semaphore(name=f"{tag}_{name}"))
        return sems[-1]

    return sb, ps, sem


def setup(nc, io, m):
    with ExitStack() as ctx:
        sb, ps, sem = scope(nc, ctx, "set")
        zero = sb("zero", [P, NCOL // 4 * F])
        loaded, made, filled, zeroed = sem("loaded"), sem("made"), sem("filled"), sem("zeroed")
        block = ctx.enter_context(nc.Block())

        @block.sync
        def _(sp):
            sp.dma_start(m.edge[:, :, 0:2].bitcast(I32), io.eidx.rearrange("(p j) c -> p j c", p=P)).then_inc(loaded, 16)
            sp.dma_start(m.edge[:, :, 2:ROW], io.eattr.rearrange("(p j) c -> p j c", p=P)).then_inc(loaded, 16)
            sp.wait_ge(filled, 1)
            for agg in (m.agg_src, m.agg_dst):
                a = agg.rearrange("(p j) f -> p (j f)", p=P)
                w = NCOL // 4 * F
                for k in range(4):
                    sp.dma_start(a[:, k * w:(k + 1) * w], zero[:, :]).then_inc(zeroed, 16)
            sp.wait_ge(zeroed, 8 * 16)
            sp.wait_ge(loaded, 32)

        @block.vector
        def _(v):
            v.memset(zero[:, :], 0.0).then_inc(filled, 1)
            v.memset(m.eps[:, :], EPS)

        @block.gpsimd
        def _(g):
            c = Static(g, made)
            c(g.memset(m.ones[:, :], 1.0))
            c(g.affine_select(out=m.ident[:, :], in_=m.ones[:, :], compare_op=ALU.is_equal, fill=0.0, base=0,
                              pattern=[[-1, P]], channel_multiplier=1))
            c(g.affine_select(out=m.before[:, :], in_=m.ones[:, :], compare_op=ALU.is_gt, fill=0.0, base=0,
                              pattern=[[-1, P]], channel_multiplier=1))
            c(g.affine_select(out=m.after[:, :], in_=m.ones[:, :], compare_op=ALU.is_gt, fill=0.0, base=0,
                              pattern=[[1, P]], channel_multiplier=-1))
            c(g.iota(m.iota_i[:, :], pattern=[[1, HI]], base=0, channel_multiplier=0))
            c(g.tensor_copy(m.iota[:, :], m.iota_i[:, :]))


def sort(nc, m):
    with ExitStack() as ctx:
        sb, ps, sem = scope(nc, ctx, "sort")
        ki = sb("ki", [P, 2, ECOL], I32)
        loi = sb("loi", [P, 2, ECOL], I32)
        hii = sb("hii", [P, 2, ECOL], I32)
        key, lo, hi = sb("key", [P, 2, ECOL]), sb("lo", [P, 2, ECOL]), sb("hi", [P, 2, ECOL])
        dig, dig_v, pre, prp, pra, hist_done = (sem(n) for n in ("dig", "digv", "pre", "prp", "pra", "hist"))
        ohl, ohh = sb("ohl", [P, 2, 2, P]), sb("ohh", [P, 2, 2, HI])
        count = [ps(f"count{o}") for o in range(2)]
        with nc.Block() as block:
            @block.vector
            def _(v):
                c = Static(v, dig)
                c(v.tensor_copy(ki[:, :, :], m.edge[:, :, 0:2].bitcast(I32).rearrange("p j o -> p o j")))
                c(v.tensor_single_scalar(loi[:, :, :], ki[:, :, :], P - 1, ALU.bitwise_and), wait=False)
                c(v.tensor_single_scalar(hii[:, :, :], ki[:, :, :], 7, ALU.logical_shift_right))
                c(v.tensor_copy(key[:, :, :], ki[:, :, :]), wait=False)
                c(v.tensor_copy(lo[:, :, :], loi[:, :, :]), wait=False)
                c(v.tensor_copy(hi[:, :, :], hii[:, :, :]))

                def onehot(k):
                    r = k.slot(2)
                    if k.past(2):
                        v.wait_ge(hist_done, k.t - 1)
                    for o in range(2):
                        v.tensor_scalar(ohl[:, r, o, :], m.iota[:, 0:P], lo[:, o, bass.ds(k.t, 1)], None, ALU.is_equal)
                        ins = v.tensor_scalar(ohh[:, r, o, :], m.iota[:, :], hi[:, o, bass.ds(k.t, 1)], None, ALU.is_equal)
                    ins.then_inc(dig_v, 1)
                sweep(v, ECOL, [(0, onehot)], 2)

            @block.tensor
            def _(pe):
                def hist(k):
                    r = k.slot(2)
                    pe.wait_ge(dig_v, k.t + 1)
                    for o in range(2):
                        first = k.i is None and k.base == 0
                        ins = pe.matmul(count[o][:, 0:HI], ohl[:, r, o, :], ohh[:, r, o, :], start=first, stop=True,
                                        skip_group_check=True)
                    ins.then_inc(hist_done, 1)
                sweep(pe, ECOL, [(0, hist)], 2)

        pc = [ps(f"prefix{o}") for o in range(2)]
        hsb, csum, excl = sb("hsb", [P, 2, HI]), sb("csum", [P, 2, HI]), sb("excl", [P, 2, HI])
        with nc.Block() as block:
            @block.vector
            def _(v):
                c = Static(v, pre)
                for o in range(2):
                    c(v.tensor_copy(hsb[:, o, :], count[o][:, 0:HI]), wait=False)
                v.wait_ge(prp, 2)
                for o in range(2):
                    c(v.tensor_copy(csum[:, o, :], pc[o][:, HI:2 * HI]))
                    c(v.tensor_tensor_scan(excl[:, o, :], csum[:, o, :], csum[:, o, :], 0.0, ALU.add, ALU.max))
                    c(v.tensor_tensor(excl[:, o, :], excl[:, o, :], csum[:, o, :], ALU.subtract))
                    c(v.tensor_tensor(excl[:, o, :], excl[:, o, :], pc[o][:, 0:HI], ALU.add))

            @block.tensor
            def _(pe):
                pe.wait_ge(pre, 2)
                for o in range(2):
                    pe.matmul(pc[o][:, 0:HI], m.after[:, :], hsb[:, o, :], start=True, stop=True)
                    pe.matmul(pc[o][:, HI:2 * HI], m.ones[:, :], hsb[:, o, :], start=True, stop=True).then_inc(prp, 1)

        R = 2
        pt = [ps(f"pt{r}") for r in range(R)]
        pg = [ps(f"pg{r}") for r in range(R)]
        tsb = sb("tsb", [P, R, 2, 2, P])
        hcur = sb("hcur", [P, R, 2, HI])
        junk, junk2 = sb("junk", [P, HI]), sb("junk2", [P, P])
        part = sb("part", [P, R, 2, 2])
        rankf = sb("rankf", [P, R, 2])
        rank = sb("rank", [P, 4, 2], I32)
        rowr = sb("rowr", [P, 4, ROW])
        kb = sb("kb", [P, R, 2, P])
        oh, tr, trc, snap, look, rk, rowc, upd = (sem(n) for n in ("oh", "tr", "trc", "snap", "look", "rk", "rowc", "upd"))
        gate = sem("gate")
        sc = [sem(f"sc{r}") for r in range(4)]
        RK = 7

        with nc.Block() as block:
            @block.vector
            def _(v):
                def onehot(k):
                    r = k.slot(R)
                    if k.past(R):
                        v.wait_ge(upd, k.t - 1)
                        v.wait_ge(rk, (k.t - 1) * RK)
                    for o in range(2):
                        v.tensor_scalar(ohl[:, r, o, :], m.iota[:, 0:P], lo[:, o, bass.ds(k.t, 1)], None, ALU.is_equal)
                        v.tensor_scalar(ohh[:, r, o, :], m.iota[:, :], hi[:, o, bass.ds(k.t, 1)], None, ALU.is_equal)
                        ins = v.tensor_scalar(kb[:, r, o, :], m.ones[:, :], key[:, o, bass.ds(k.t, 1)], None, ALU.mult)
                    ins.then_inc(oh, 1)

                def ranks(k):
                    r = k.slot(R)
                    c = Chain(v, rk, RK, k)
                    v.wait_ge(look, k.t + 1)
                    for o in range(2):
                        c(v.scalar_tensor_tensor(junk2[:, :], tsb[:, r, o, 1, :], key[:, o, bass.ds(k.t, 1)],
                                                 m.before[:, :], ALU.is_equal, ALU.mult,
                                                 accum_out=part[:, r, o, 0:1]))
                        c.wait()
                        c(v.tensor_tensor_reduce(junk[:, :], pg[r][:, o * HI:(o + 1) * HI], ohh[:, r, o, :], 1.0, 0.0,
                                                 ALU.mult, ALU.add, part[:, r, o, 1:2]))
                        c.wait()
                    c(v.tensor_tensor(rankf[:, r, :], part[:, r, :, 0], part[:, r, :, 1], ALU.add))
                    c.wait()
                    if k.past(4):
                        v.wait_ge(sc[k.slot(4)], k.lap(4) * 32)
                    c(v.tensor_copy(rank[:, k.slot(4), :], rankf[:, r, :]))
                    c(v.tensor_copy(rowr[:, k.slot(4), :], m.edge[:, bass.ds(k.t, 1), :]))
                sweep(v, ECOL, [(0, onehot), (1, ranks)], 4)

            @block.scalar
            def _(a):
                def copies(k):
                    r = k.slot(R)
                    a.wait_ge(tr, k.t + 1)
                    if k.past(R):
                        a.wait_ge(rk, (k.t - 1) * RK)
                        a.wait_ge(look, k.t - 1)
                    a.copy(tsb[:, r, :, :, :].rearrange("p a b c -> p (a b c)"), pt[r][:, :]).then_inc(trc, 1)
                    if k.past(1):
                        a.wait_ge(upd, k.t)
                    for o in range(2):
                        ins = a.copy(hcur[:, r, o, :], count[o][:, 0:HI])
                    ins.then_inc(snap, 1)
                a.wait_ge(gate, 1)
                sweep(a, ECOL, [(0, copies)], 2)

            @block.tensor
            def _(pe):
                for o in range(2):
                    ins = pe.matmul(count[o][:, 0:HI], m.ident[:, :], excl[:, o, :], start=True, stop=True,
                                    skip_group_check=True)
                ins.then_inc(gate, 1)

                def turn(k):
                    r = k.slot(R)
                    pe.wait_ge(oh, k.t + 1)
                    if k.past(R):
                        pe.wait_ge(trc, k.t - 1)
                    for o in range(2):
                        pe.transpose(pt[r][:, 2 * o * P:(2 * o + 1) * P], ohl[:, r, o, :], m.ident[:, :])
                        ins = pe.transpose(pt[r][:, (2 * o + 1) * P:(2 * o + 2) * P], kb[:, r, o, :], m.ident[:, :])
                    ins.then_inc(tr, 1)

                def lookup(k):
                    r = k.slot(R)
                    pe.wait_ge(trc, k.t + 1)
                    pe.wait_ge(snap, k.t + 1)
                    if k.past(R):
                        pe.wait_ge(rk, (k.t - 1) * RK)
                    for o in range(2):
                        ins = pe.matmul(count[o][:, 0:HI], ohl[:, r, o, :], ohh[:, r, o, :], start=False,
                                        stop=True, skip_group_check=True)
                    ins.then_inc(upd, 1)
                    for o in range(2):
                        ins = pe.matmul(pg[r][:, o * HI:(o + 1) * HI], tsb[:, r, o, 0, :], hcur[:, r, o, :],
                                        start=True, stop=True)
                    ins.then_inc(look, 1)
                sweep(pe, ECOL, [(0, turn), (1, lookup)], 4)

            @block.gpsimd
            def _(g):
                last_row = g.to_reg(EROWS - 1)

                def scatter(k):
                    r = k.slot(4)
                    g.wait_ge(rk, (k.t + 1) * RK)
                    g.sem_inc(rowc, 1)
                    for o, table in enumerate((m.by_src, m.by_dst)):
                        g.indirect_dma_start(table, bass.IndirectOffsetOnAxis(ap=rank[:, r, o:o + 1], axis=0),
                                             rowr[:, r, :], None, bounds_check=last_row,
                                             oob_is_err=False).then_inc(sc[r], 16)
                sweep(g, ECOL, [(0, scatter)], 4)
                for r in range(4):
                    g.wait_ge(sc[r], 32 * len(range(r, ECOL, 4)))


def segments(nc, m):
    for table, key_col, gather_col, e, q in ((m.by_src, 0, 1, m.edge, m.src), (m.by_dst, 1, 0, m.edge, m.dst)):
        with ExitStack() as ctx:
            sb, ps, sem = scope(nc, ctx, f"seg{key_col}")
            ld, ch, ach, mm = sem("ld"), sem("ch"), sem("ach"), sem("mm")
            nb = sb("nb", [P, 2, 2], I32)
            kf, nbf = sb("kf", [P, ECOL]), sb("nbf", [P, 2])
            end, fr, tmp, wid = sb("end", [P, ECOL]), sb("fr", [P, ECOL]), sb("tmp", [P, ECOL]), sb("wid", [P, ECOL])
            one = sb("one", [P, 8])
            diag = sb("diag", [P, P])
            row = ps("row")
            block = ctx.enter_context(nc.Block())
            flat = table.rearrange("(p j) c -> p j c", p=P)
            es = q.es

            @block.sync
            def _(sp):
                sp.dma_start(q.attr[:, :, :], flat).then_inc(ld, 16)
                sp.wait_ge(ch, 1)
                sp.dma_start(nb[1:P, 0, :], flat[0:P - 1, ECOL - 1, 0:2].bitcast(I32)).then_inc(ld, 16)
                sp.dma_start(nb[0:P - 1, 1, :], flat[1:P, 0, 0:2].bitcast(I32)).then_inc(ld, 16)

            @block.vector
            def _(v):
                c = Static(v, ch)
                c(v.memset(nb[:, :, :], -1))
                v.wait_ge(ld, 48)
                c(v.tensor_copy(kf[:, :], q.attr[:, :, key_col].bitcast(I32)), wait=False)
                c(v.tensor_copy(nbf[:, :], nb[:, :, key_col]), wait=False)
                y = q.attr[:, :, q.attr_y0:q.attr_y0 + 1]
                for k, a in ((Y0, q.attr_y0), (Y1, q.attr_y1), (Y1 + 1, q.attr_y1 + 1), (Y1 + 2, q.attr_y1 + 2),
                             (Y1 + 3, q.attr_y1), (Y1 + 4, q.attr_y1 + 1),
                             (GIDX, gather_col), (GIDX2, key_col)):
                    c(v.tensor_copy(es[:, :, k].bitcast(I32), q.attr[:, :, a].bitcast(I32)), wait=False)
                c(v.memset(es[:, 0, SAME:SAME + 1], 0.0))
                c(v.tensor_tensor(es[:, 1:ECOL, SAME], kf[:, 1:ECOL], kf[:, 0:ECOL - 1], ALU.is_equal), wait=False)
                c(v.tensor_tensor(end[:, 0:ECOL - 1], kf[:, 1:ECOL], kf[:, 0:ECOL - 1], ALU.not_equal), wait=False)
                c(v.tensor_tensor(end[:, ECOL - 1:ECOL], kf[:, ECOL - 1:ECOL], nbf[:, 1:2], ALU.not_equal), wait=False)
                c(v.tensor_scalar(fr[:, :], kf[:, :], kf[:, 0:1], None, ALU.is_equal), wait=False)
                c(v.tensor_tensor(one[:, 0:1], kf[:, 0:1], nbf[:, 0:1], ALU.is_equal))
                c(v.tensor_tensor(es[:, :, FEND], fr[:, :], end[:, :], ALU.mult))
                c(v.tensor_reduce(one[:, 1:2], es[:, :, FEND], AX, ALU.max))
                c(v.tensor_scalar(tmp[:, :], es[:, :, FEND], one[:, 0:1], None, ALU.mult))
                c(v.tensor_tensor(tmp[:, :], end[:, :], tmp[:, :], ALU.subtract))
                c(v.tensor_scalar(tmp[:, :], tmp[:, :], float(-SKIP), float(SKIP), ALU.mult, ALU.add))
                c(v.tensor_tensor(wid[:, :], kf[:, :], tmp[:, :], ALU.add))
                c(v.tensor_copy(es[:, :, WIDX].bitcast(I32), wid[:, :]), wait=False)
                c(v.tensor_tensor(one[:, 2:3], one[:, 0:1], one[:, 1:2], ALU.mult))
                c(v.tensor_scalar(one[:, 3:4], one[:, 2:3], float(-SKIP), float(SKIP), ALU.mult, ALU.add))
                c(v.tensor_tensor(one[:, 4:5], kf[:, 0:1], one[:, 3:4], ALU.add))
                c(v.tensor_copy(q.fix_id[:, 0:1], one[:, 4:5]), wait=False)
                c(v.tensor_copy(q.ends[:, 0:1], kf[:, 0:1]), wait=False)
                c(v.tensor_copy(q.ends[:, 1:2], kf[:, ECOL - 1:ECOL]), wait=False)
                c(v.tensor_scalar(q.last_run[:, :], kf[:, :], kf[:, ECOL - 1:ECOL], None, ALU.is_equal), wait=False)
                c(v.tensor_copy(q.first_run[:, :], fr[:, :]), wait=False)
                c(v.tensor_copy(q.first_id[:, 0:1], q.attr[:, 0, key_col:key_col + 1].bitcast(I32)), wait=False)
                c(v.tensor_scalar(diag[:, :], m.ident[:, :], kf[:, 0:1], None, ALU.mult))
                v.sem_inc(ach, 1)
                v.wait_ge(mm, 1)
                c(v.scalar_tensor_tensor(q.carry[:, :], row[:, 0:P], kf[:, ECOL - 1:ECOL], m.after[:, :],
                                         ALU.is_equal, ALU.mult), wait=False)

            @block.tensor
            def _(pe):
                pe.wait_ge(ach, 1)
                pe.matmul(row[:, 0:P], m.ones[:, :], diag[:, :], start=True, stop=True).then_inc(mm, 1)


def bc(ap, at, n):
    ap = ap.unsqueeze(at)
    return ap.broadcast_to([n if d == at else s for d, s in enumerate(ap.shape)])


def chain_loads(eng, sem, pairs):
    for dst, src in pairs:
        eng.dma_start(dst, src).then_inc(sem, 16)
    eng.wait_ge(sem, 16 * len(pairs))


def block_loads(wb, w2, ws, wv):
    return [(wb[0:64, 0:64], ws), (wb[64:96, 64:96], wv), (wb[96:128, 96:128], wv), (w2[0:32, 0:32], wv)]


CG_OPS, CG_OPS_CROSS = 7, 11


def cg(v, c, w, s, vec, y0, y1, dot, mid, tmp, cross):
    vw = 128 if cross else 96
    mv = mid[:, 96:96 + 3 * vw].rearrange("p (c u) -> p c u", c=3)
    t0, t1, t2, t3 = (tmp[:, i * 96:(i + 1) * 96] for i in range(4))
    vec3 = vec[:, 0:96].rearrange("p (c u) -> p c u", c=3)

    def c3(ap):
        return ap.rearrange("p (c u) -> p c u", c=3)

    c(v.tensor_tensor(c3(t0), vec3, bc(y1(0, 3), 2, V), ALU.mult))
    if cross:
        c(v.tensor_tensor(c3(t2), c3(vec[:, 32:128]), bc(y1(2, 5), 2, V), ALU.mult))
        c(v.tensor_tensor(c3(t3), c3(vec[:, 64:160]), bc(y1(1, 4), 2, V), ALU.mult))
    n_cross = c.n
    c(v.scalar_tensor_tensor(mid[:, 0:64], w[:, 0:64], y0, s, ALU.mult, ALU.mult))
    c(v.tensor_tensor(tmp[:, 416:480], w[:, 64:128], s, ALU.mult))
    n_ws = c.n
    c(v.scalar_tensor_tensor(mv[:, :, 64:96], vec3, y0, bc(w[:, 128:160], 1, 3), ALU.mult, ALU.mult))
    c.wait(1)
    c(v.tensor_reduce(tmp[:, 384:416], t0.rearrange("p (c u) -> p u c", c=3), AX, ALU.add))
    n_dot = c.n
    if cross:
        c.wait(n_cross)
        c(v.tensor_tensor(t1, t2, t3, ALU.subtract))
    n_sub = c.n
    c.wait(n_ws)
    c(v.tensor_tensor(mv[:, :, 0:64], bc(tmp[:, 416:480], 1, 3), bc(y1(0, 3), 2, 64), ALU.mult))
    c.wait(n_dot)
    c(v.scalar_tensor_tensor(mid[:, 64:96], tmp[:, 384:416], dot, w[:, 160:192], ALU.mult, ALU.mult))
    if cross:
        c.wait(n_sub)
        c(v.scalar_tensor_tensor(mv[:, :, 96:128], c3(t1), R2, bc(w[:, 192:224], 1, 3), ALU.mult, ALU.mult))


def edge_layer(nc, m, io, layer, x, q, agg):
    cross = layer == 0
    tag = f"e{layer}"
    nb, a_col = ((8, A8), (10, A10))[layer]
    nh = (64, 100)[layer]
    wn, vw = (224, 128) if cross else (192, 96)
    cgn = CG_OPS_CROSS if cross else CG_OPS
    c1 = float(1 / np.sqrt(8.0)) if layer == 0 else float(np.sqrt(2.0) / np.sqrt(10.0))
    with ExitStack() as ctx:
        sb, ps, sem = scope(nc, ctx, tag)
        wb, w2 = sb("wb", [P, P]), sb("w2", [V, V])
        f1, f2, f3 = sb("f1", [nb, nh]), sb("f2", [64, 64]), sb("f3", [nh, wn])
        ws, wv = sb("ws", [96, 64]), sb("wv", [vw, V])
        wl, wz, wsc = sem("wl"), sem("wz"), sem("wsc")
        w = io.w
        if layer == 0:
            loads = block_loads(wb, w2, w["L0_gnn_W1_0"], w["L0_gnn_W1_1"]) + [
                (f1[:, :], w["L0_gnn_Wfc1"]), (f2[:, :], w["L0_gnn_Wfc2"]), (f3[:, :], w["L0_gnn_Wfc3"]),
                (ws[:, :], w["L0_gnn_W2_0"]), (wv[:, :], w["L0_gnn_W2_1"])]
            last, cs, cv = f3, 1 / (4 * np.sqrt(96.0)), 1 / (4 * np.sqrt(128.0))
            cl = 1 / 8.0
        else:
            loads = block_loads(wb, w2, w["L1_gnn_W_l1_0"], w["L1_gnn_W_l1_1"]) + [
                (f1[:, :], w["L1_gnn_W_fc1"]), (f3[:, :], w["L1_gnn_W_fc2"]),
                (ws[0:64, :], w["L1_gnn_W_l2_00"]), (ws[64:96, :], w["L1_gnn_W_l2_10"]),
                (wv[0:64, :], w["L1_gnn_W_l2_01"]), (wv[64:96, :], w["L1_gnn_W_l2_11"])]
            last, cs, cv = f3, 0.5 / (4 * np.sqrt(96.0)), 0.5 / (4 * np.sqrt(96.0))
            cl = 1 / 10.0
        with nc.Block() as block:
            @block.vector
            def _(v):
                v.memset(wb[:, :], 0.0).then_inc(wz, 1)

            @block.sync
            def _(sp):
                sp.wait_ge(wz, 1)
                chain_loads(sp, wl, loads)
                sp.sem_inc(wz, 1)

            @block.scalar
            def _(a):
                a.wait_ge(wz, 2)
                a.mul(wb[0:64, :], wb[0:64, :], 1 / 8.0).then_inc(wsc, 1)
                a.mul(wb[64:128, :], wb[64:128, :], float(1 / np.sqrt(32.0))).then_inc(wsc, 1)
                a.mul(w2[:, :], w2[:, :], float(1 / np.sqrt(32.0))).then_inc(wsc, 1)
                a.mul(last[:, :], last[:, :], float(cl)).then_inc(wsc, 1)
                a.mul(ws[:, :], ws[:, :], float(cs)).then_inc(wsc, 1)
                a.mul(wv[:, :], wv[:, :], float(cv)).then_inc(wsc, 1)

        R = 4
        gi, wi = sb("gi", [P, R, 1], I32), sb("wi", [P, R, 1], I32)
        xg = sb("xg", [P, R, F + 1])
        ar = sb("ar", [P, R, nb])
        t1, t2, ta = sb("t1", [P, 2, P]), sb("t2", [V, 2, P]), sb("ta", [nb, 2, P])
        sv = sb("sv", [P, 4, 224])
        h1, h2 = sb("h1", [nh, 2, P]), sb("h2", [64, 2, P])
        mid, tmp = sb("mid", [P, 2, 96 + 3 * vw]), sb("tmp", [P, 2, 480])
        ms, mvt = sb("ms", [96, 2, P]), sb("mvt", [vw, 2, 3 * P])
        tot = sb("tot", [P, R, F])
        s1, cap = sb("s1", [P, F]), sb("cap", [P, 2, F])
        fix = sb("fix", [P, F])
        pt, py, pm, px = ps("pt"), ps("py"), ps("pm"), ps("px")
        pw = [ps(f"pw{r}") for r in range(2)]
        po = [ps(f"po{r}") for r in range(2)]
        gat = [sem(f"gat{r}") for r in range(R)]
        sct = [sem(f"sct{r}") for r in range(R)]
        gic, wic, arc = sem("gic"), sem("wic"), sem("arc")
        xt, xtc, y, svc, m2, h2c, wr, cgs, mt, mtc, o, acc, gate, fx = (sem(n) for n in (
            "xt", "xtc", "y", "svc", "m2", "h2c", "wr", "cg", "mt", "mtc", "o", "acc", "gate", "fx"))
        init, fixed, order = sem("init"), sem("fixed"), sem("order")
        AC = 3
        LW = 3 if cross else 2
        LE, LF = LW + 2, LW + 3
        LS = LF + 4

        with nc.Block() as block:
            @block.gpsimd
            def _(g):
                top = g.to_reg(NROWS - 1)

                def gather(k):
                    r = k.slot(R)
                    if k.past(R):
                        g.wait_ge(gat[r], k.lap(R) * 16)
                        g.wait_ge(svc, k.t - R + 1)
                        g.wait_ge(xt, k.t - R + 1)
                    g.tensor_copy(ar[:, r, :], q.attr[:, bass.ds(k.t, 1), a_col:a_col + nb]).then_inc(arc, 1)
                    g.tensor_copy(gi[:, r, :], q.es[:, bass.ds(k.t, 1), GIDX].bitcast(I32)).then_inc(gic, 1)
                    g.wait_ge(gic, k.t + 1)
                    g.sem_inc(gate, 1)
                    g.indirect_dma_start(xg[:, r, :], None, x, bass.IndirectOffsetOnAxis(ap=gi[:, r, :], axis=0),
                                         bounds_check=top, oob_is_err=False).then_inc(gat[r], 16)

                def scatter(k):
                    r = k.slot(R)
                    if k.past(R):
                        g.wait_ge(sct[r], k.lap(R) * 16)
                    g.tensor_copy(wi[:, r, :], q.es[:, bass.ds(k.t, 1), WIDX].bitcast(I32)).then_inc(wic, 1)
                    g.wait_ge(wic, k.t + 1)
                    g.wait_ge(acc, (k.t + 1) * AC)
                    g.sem_inc(gate, 1)
                    g.indirect_dma_start(agg, bass.IndirectOffsetOnAxis(ap=wi[:, r, :], axis=0), tot[:, r, :], None,
                                         bounds_check=top, oob_is_err=False).then_inc(sct[r], 16)
                sweep(g, ECOL, [(0, gather), (LS, scatter)], R)
                g.wait_ge(fx, 1)
                g.indirect_dma_start(agg, bass.IndirectOffsetOnAxis(ap=q.fix_id[:, :], axis=0), fix[:, :], None,
                                     bounds_check=top, oob_is_err=False).then_inc(fixed, 16)
                g.wait_ge(fixed, 16)
                for r in range(R):
                    g.wait_ge(sct[r], 16 * len(range(r, ECOL, R)))

            @block.tensor
            def _(pe):
                def turn(k):
                    r = k.slot(2)
                    if k.past(1):
                        pe.wait_ge(xtc, k.t)
                    pe.wait_ge(arc, k.t + 1)
                    pe.wait_ge(gat[k.slot(R)], (k.lap(R) + 1) * 16)
                    pe.transpose(pt[:, 0:P], xg[:, k.slot(R), 0:P], m.ident[:, :])
                    pe.transpose(pt[0:V, P:2 * P], xg[:, k.slot(R), P:F], m.ident[:, :])
                    pe.transpose(pt[0:nb, 2 * P:3 * P], ar[:, k.slot(R), :], m.ident[:, :]).then_inc(xt, 1)

                def maps(k):
                    r = k.slot(2)
                    if k.past(1):
                        pe.wait_ge(svc, k.t)
                    pe.wait_ge(xtc, k.t + 1)
                    pe.matmul(py[:, 0:P], t1[:, r, :], wb[:, :], start=True, stop=True)
                    pe.matmul(py[:, P:F], t2[:, r, :], w2[:, :], start=True, stop=True)
                    pe.matmul(py[0:nh, F:F + P], f1[:, :], ta[:, r, :], start=True, stop=True).then_inc(y, 1)

                def hidden(k):
                    r = k.slot(2)
                    pe.wait_ge(svc, k.t + 1)
                    if k.past(1):
                        pe.wait_ge(h2c, k.t)
                    pe.sem_inc(order, 1)
                    pe.matmul(pm[0:64, 0:P], f2[:, :], h1[:, r, :], start=True, stop=True).then_inc(m2, 1)

                def weights(k):
                    r = k.slot(2)
                    pe.wait_ge(h2c if cross else svc, k.t + 1)
                    if k.past(2):
                        pe.wait_ge(cgs, (k.t - 1) * cgn)
                    pe.matmul(pw[r][:, 0:wn], (h2 if cross else h1)[:, r, :], f3[:, :], start=True,
                              stop=True).then_inc(wr, 1)

                def turn_mid(k):
                    r = k.slot(2)
                    pe.wait_ge(cgs, (k.t + 1) * cgn)
                    if k.past(1):
                        pe.wait_ge(mtc, k.t)
                    pe.transpose(px[0:96, 0:P], mid[:, r, 0:96], m.ident[:, :])
                    for d in range(3):
                        ins = pe.transpose(px[0:vw, (d + 1) * P:(d + 2) * P], mid[:, r, 96 + d * vw:96 + (d + 1) * vw],
                                           m.ident[:, :])
                    ins.then_inc(mt, 1)

                def out(k):
                    r = k.slot(2)
                    pe.wait_ge(mtc, k.t + 1)
                    if k.past(2):
                        pe.wait_ge(acc, (k.t - 1) * AC)
                    pe.matmul(po[r][:, 0:64], ms[:, r, :], ws[:, :], start=True, stop=True)
                    for d in range(3):
                        ins = pe.matmul(po[r][:, 64 + d * V:96 + d * V], mvt[:, r, d * P:(d + 1) * P],
                                        wv[:, :], start=True, stop=True)
                    ins.then_inc(o, 1)
                stages = [(0, turn), (1, maps)] + [(2, hidden)] * cross + [(LW, weights), (LE, turn_mid), (LF, out)]
                sweep(pe, ECOL, stages, 2)
                pe.wait_ge(acc, ECOL * AC)
                pe.matmul(py[:, 0:F], q.carry[:, :], tot[:, (ECOL - 1) % R, :], start=True, stop=True).then_inc(y, 1)

            @block.scalar
            def _(a):
                def copy_x(k):
                    r = k.slot(2)
                    if k.past(2):
                        a.wait_ge(y, k.t - 1)
                    a.wait_ge(xt, k.t + 1)
                    a.copy(t1[:, r, :], pt[:, 0:P])
                    a.copy(t2[:, r, :], pt[0:V, P:2 * P])
                    a.copy(ta[:, r, :], pt[0:nb, 2 * P:3 * P]).then_inc(xtc, 1)

                def copy_y(k):
                    r = k.slot(2)
                    a.wait_ge(y, k.t + 1)
                    if k.past(2):
                        a.wait_ge(m2 if cross else wr, k.t - 1)
                    if k.past(4):
                        a.wait_ge(cgs, (k.t - 3) * cgn)
                    if cross:
                        a.copy(sv[:, k.slot(4), 0:F], py[:, 0:F])
                        a.copy(sv[:, k.slot(4), F:224], py[:, 64:128])
                    else:
                        scale = xg[:, k.slot(R), F:F + 1]
                        a.activation(sv[:, k.slot(4), 0:F], py[:, 0:F], ACT.Copy, scale=scale)
                        a.activation(sv[:, k.slot(4), F:224], py[:, 64:128], ACT.Copy, scale=scale)
                    a.activation(h1[:, r, :], py[0:nh, F:F + P], ACT.Silu if cross else ACT.Relu,
                                 scale=c1).then_inc(svc, 1)

                def act_2(k):
                    r = k.slot(2)
                    a.wait_ge(m2, k.t + 1)
                    if k.past(2):
                        a.wait_ge(wr, k.t - 1)
                    a.activation(h2[:, r, :], pm[0:64, 0:P], ACT.Silu, scale=1 / 8.0).then_inc(h2c, 1)

                def copy_mid(k):
                    r = k.slot(2)
                    a.wait_ge(mt, k.t + 1)
                    if k.past(2):
                        a.wait_ge(o, k.t - 1)
                    a.copy(ms[:, r, :], px[0:96, 0:P])
                    a.copy(mvt[:, r, :], px[0:vw, P:4 * P]).then_inc(mtc, 1)
                sweep(a, ECOL, [(0, copy_x), (1, copy_y)] + [(2, act_2)] * cross + [(LE, copy_mid)], 4)

            @block.vector
            def _(v):
                v.memset(s1[:, :], 0.0).then_inc(init, 1)
                v.memset(tot[:, R - 1, :], 0.0).then_inc(init, 1)
                v.wait_ge(init, 2)

                def product(k):
                    r = k.slot(2)
                    v.wait_ge(wr, k.t + 1)
                    v.wait_ge(svc, k.t + 1)
                    if k.past(2):
                        v.wait_ge(mt, k.t - 1)
                    c = Chain(v, cgs, cgn, k)
                    s = sv[:, k.slot(4), :]
                    edge = bass.ds(k.t, 1)
                    cg(v, c, pw[r][:, 0:wn], s[:, 0:64], s[:, 64:224], q.es[:, edge, Y0],
                       lambda i, j: q.es[:, edge, Y1 + i:Y1 + j].rearrange("p a c -> p (a c)"), R3,
                       mid[:, r, :], tmp[:, r, :], cross)

                def accumulate(k):
                    r = k.slot(R)
                    v.wait_ge(o, k.t + 1)
                    if k.past(R):
                        v.wait_ge(sct[r], k.lap(R) * 16)
                    c = Chain(v, acc, AC, k)
                    if k.past(1):
                        v.wait_ge(acc, k.t * AC)
                    edge = bass.ds(k.t, 1)
                    pos = po[k.slot(2)][:, 0:F]
                    c(v.scalar_tensor_tensor(tot[:, r, :], tot[:, (r - 1) % R, :], q.es[:, edge, SAME], pos,
                                             ALU.mult, ALU.add))
                    c.wait()
                    c(v.tensor_scalar(cap[:, k.slot(2), :], tot[:, r, :], q.es[:, edge, FEND], None, ALU.mult))
                    c.wait()
                    c(v.tensor_tensor(s1[:, :], s1[:, :], cap[:, k.slot(2), :], ALU.add))
                sweep(v, ECOL, [(LW, product), (LF, accumulate)], 4)
                v.wait_ge(y, ECOL + 1)
                v.wait_ge(acc, ECOL * AC)
                v.tensor_tensor(fix[:, :], s1[:, :], py[:, 0:F], ALU.add).then_inc(fx, 1)


def node_layer(nc, m, io, layer, x, agg, out):
    w = io.w
    maps_ = {0: (w["L0_gnn_Wsc0"], w["L0_gnn_Wsc1"]), 1: (w["L1_gnn_W_si0"], w["L1_gnn_W_si1"]),
             2: None, 3: (w["L3_gnn_lu0"], w["L3_gnn_lu1"])}[layer]
    owid = out.shape[1]
    with ExitStack() as ctx:
        sb, ps, sem = scope(nc, ctx, f"n{layer}")
        wb, w2 = sb("wb", [P, P]), sb("w2", [V, V])
        gain = sb("gain", [P, F])
        wl, wz, wsc = sem("wl"), sem("wz"), sem("wsc")
        if maps_:
            loads = block_loads(wb, w2, *maps_)
            if layer == 0:
                g1 = w["L0_gnn_g1"]
                loads += [(gain[:, 0:64], w["L0_gnn_g0"].partition_broadcast(P))] + [
                    (gain[:, 64 + 32 * d:96 + 32 * d], g1.partition_broadcast(P)) for d in range(3)]
            with nc.Block() as block:
                @block.vector
                def _(v):
                    v.memset(wb[:, :], 0.0).then_inc(wz, 1)

                @block.sync
                def _(sp):
                    sp.wait_ge(wz, 1)
                    chain_loads(sp, wl, loads)
                    sp.sem_inc(wz, 1)

                @block.scalar
                def _(a):
                    a.wait_ge(wz, 2)
                    a.mul(wb[0:64, :], wb[0:64, :], 1 / 8.0).then_inc(wsc, 1)
                    a.mul(wb[64:128, :], wb[64:128, :], float(1 / np.sqrt(32.0))).then_inc(wsc, 1)
                    a.mul(w2[:, :], w2[:, :], float(1 / np.sqrt(32.0))).then_inc(wsc, 1)
        R = 4
        xn, ag = sb("xn", [P, R, GRP, F + 1]), sb("ag", [P, R, GRP, F])
        ta, tb = sb("ta", [P, 2, GRP * P]), sb("tb", [V, 2, GRP * P])
        y, sq, z = sb("y", [P, R, GRP, F]), sb("sq", [P, GRP, F]), sb("z", [P, R, GRP, F])
        ssum, rms, rrms = sb("ssum", [P, R, 2, GRP]), sb("rms", [P, R, 2, GRP]), sb("rrms", [P, R, 2, GRP])
        st, mv = sb("st", [P, 2, GRP, 6]), sb("mv", [P, R, GRP, 2])
        sd, rstd = sb("sd", [P, R, GRP]), sb("rstd", [P, R, GRP])
        xo = sb("xo", [P, R, GRP, owid])
        pa = [ps(f"pa{r}") for r in range(2)]
        pb = [ps(f"pb{r}") for r in range(2)]
        pc = [ps(f"pc{r}") for r in range(2)]
        pd = [ps(f"pd{r}") for r in range(2)]
        ldx, lda, sto = ([sem(f"{n}{r}") for r in range(R)] for n in ("ldx", "lda", "sto"))
        tr, trc, mp, c1, c2, c3, rm, sdd, fin, gate, order = (sem(n) for n in (
            "tr", "trc", "mp", "c1", "c2", "c3", "rm", "sd", "fin", "gate", "order"))
        K1 = {0: 5, 1: 2, 2: 1, 3: 2}[layer]
        K2 = {0: 2 * GRP + 2, 1: GRP, 2: 0, 3: 1}[layer] + 2 * GRP
        K3 = 1
        xv = x.rearrange("(p q j) f -> p q (j f)", p=P, j=GRP)
        av = agg.rearrange("(p q j) f -> p q (j f)", p=P, j=GRP)
        ov = out.rearrange("(p q j) f -> p q (j f)", p=P, j=GRP)
        L1_, L2_, L3_, L4_ = 2, 3, 4, 5

        with nc.Block() as block:
            @block.sync
            def _(sp):
                def load(k):
                    r = k.slot(R)
                    if k.past(R):
                        sp.wait_ge(fin, k.t - R + 1)
                    sp.dma_start(xn[:, r, :, :].rearrange("p a b -> p (a b)"), xv[:, bass.ds(k.t, 1), :].rearrange("p a b -> p (a b)")).then_inc(ldx[r], 16)
                    sp.dma_start(ag[:, r, :, :].rearrange("p a b -> p (a b)"), av[:, bass.ds(k.t, 1), :].rearrange("p a b -> p (a b)")).then_inc(lda[r], 16)

                def store(k):
                    r = k.slot(R)
                    sp.wait_ge(fin, k.t + 1)
                    sp.dma_start(ov[:, bass.ds(k.t, 1), :].rearrange("p a b -> p (a b)"), xo[:, r, :, :].rearrange("p a b -> p (a b)")).then_inc(sto[r], 16)
                sweep(sp, NGRP, [(0, load), (4, store)], R)
                for r in range(R):
                    sp.wait_ge(sto[r], 16 * len(range(r, NGRP, R)))

            @block.tensor
            def _(pe):
                if not maps_:
                    return

                def turn(k):
                    r = k.slot(2)
                    pe.wait_ge(ldx[k.slot(R)], (k.lap(R) + 1) * 16)
                    if k.past(2):
                        pe.wait_ge(trc, k.t - 1)
                    for j in range(GRP):
                        pe.transpose(pa[r][:, j * P:(j + 1) * P], xn[:, k.slot(R), j, 0:P], m.ident[:, :])
                        ins = pe.transpose(pb[r][0:V, j * P:(j + 1) * P], xn[:, k.slot(R), j, P:F], m.ident[:, :])
                    ins.then_inc(tr, 1)

                def maps(k):
                    r = k.slot(2)
                    pe.wait_ge(trc, k.t + 1)
                    if k.past(2):
                        pe.wait_ge(c1, (k.t - 1) * K1)
                    for j in range(GRP):
                        pe.matmul(pc[r][:, j * P:(j + 1) * P], ta[:, r, j * P:(j + 1) * P], wb[:, :], start=True,
                                  stop=True)
                        ins = pe.matmul(pd[r][:, j * V:(j + 1) * V], tb[:, r, j * P:(j + 1) * P],
                                        w2[:, :], start=True, stop=True)
                    ins.then_inc(mp, 1)
                sweep(pe, NGRP, [(0, turn), (1, maps)], 4)

            @block.scalar
            def _(a):
                def copy_x(k):
                    r = k.slot(2)
                    if k.past(2):
                        a.wait_ge(mp, k.t - 1)
                    a.wait_ge(tr, k.t + 1)
                    a.copy(ta[:, r, :], pa[r][:, :])
                    a.copy(tb[:, r, :], pb[r][0:V, :]).then_inc(trc, 1)

                def root(k):
                    r = k.slot(R)
                    a.wait_ge(c1, (k.t + 1) * K1)
                    if k.past(R):
                        a.wait_ge(c2, (k.t - R + 1) * K2)
                    a.activation(rms[:, r, 0, :], ssum[:, r, 0, :], ACT.Sqrt, scale=1 / 64.0, bias=m.eps[:, :])
                    a.activation(rms[:, r, 1, :], ssum[:, r, 1, :], ACT.Sqrt, scale=1 / 32.0, bias=m.eps[:, :]).then_inc(rm, 1)

                def deviation(k):
                    r = k.slot(R)
                    a.wait_ge(c2, (k.t + 1) * K2)
                    if k.past(R):
                        a.wait_ge(c3, (k.t - R + 1) * K3)
                    a.activation(sd[:, r, :], mv[:, r, :, 1], ACT.Sqrt, bias=m.eps[:, :]).then_inc(sdd, 1)
                stages = [(0, copy_x)] * bool(maps_) + [(L1_, root)] * (layer == 0) + [(L2_, deviation)]
                sweep(a, NGRP, stages, R)

            @block.vector
            def _(v):
                def raw(k):
                    r = k.slot(R)
                    c = Chain(v, c1, K1, k)
                    v.wait_ge(lda[r], (k.lap(R) + 1) * 16)
                    v.wait_ge(ldx[r], (k.lap(R) + 1) * 16)
                    if maps_:
                        v.wait_ge(mp, k.t + 1)
                        if k.past(R):
                            v.wait_ge(fin, k.t - R + 1)
                        pcv = pc[k.slot(2)][:, :].rearrange("p (j f) -> p j f", j=GRP)
                        pdv = pd[k.slot(2)][:, 0:P].rearrange("p (j f) -> p j f", j=GRP)
                        c(v.tensor_tensor(y[:, r, :, 0:P], pcv, ag[:, r, :, 0:P], ALU.add))
                        c(v.tensor_tensor(y[:, r, :, P:F], pdv, ag[:, r, :, P:F], ALU.add))
                        if layer == 0:
                            c.wait()
                            c(v.tensor_tensor(sq[:, :, :], y[:, r, :, :], y[:, r, :, :], ALU.mult))
                            c.wait()
                            c(v.tensor_reduce(ssum[:, r, 0, :], sq[:, :, 0:64], AX, ALU.add))
                            c(v.tensor_reduce(ssum[:, r, 1, :], sq[:, :, 64:F], AX, ALU.add))
                    else:
                        if k.past(R):
                            v.wait_ge(fin, k.t - R + 1)
                        c(v.scalar_tensor_tensor(z[:, r, :, :], xn[:, r, :, 0:F], 2.0, ag[:, r, :, :], ALU.mult,
                                                 ALU.add))

                def combine(k):
                    r = k.slot(R)
                    c = Chain(v, c2, K2, k)
                    v.wait_ge(c1, (k.t + 1) * K1)
                    if k.past(R):
                        v.wait_ge(fin, k.t - R + 1)
                    if layer == 0:
                        v.wait_ge(rm, k.t + 1)
                        c(v.reciprocal(rrms[:, r, :, :], rms[:, r, :, :]))
                        c.wait()
                        for j in range(GRP):
                            for d, (f, t) in enumerate(((0, 64), (64, F))):
                                c(v.scalar_tensor_tensor(z[:, r, j, f:t], y[:, r, j, f:t], rrms[:, r, d, j:j + 1],
                                                         gain[:, f:t], ALU.mult, ALU.mult))
                        c.wait()
                        c(v.tensor_tensor(z[:, r, :, :], z[:, r, :, :], xn[:, r, :, 0:F], ALU.add))
                        c.wait()
                    elif layer == 1:
                        for j in range(GRP):
                            c(v.scalar_tensor_tensor(z[:, r, j, :], y[:, r, j, :], xn[:, r, j, F:F + 1],
                                                     xn[:, r, j, 0:F], ALU.mult, ALU.add))
                        c.wait()
                    elif layer == 3:
                        c(v.scalar_tensor_tensor(z[:, r, :, :], xn[:, r, :, 0:F], 2.0, y[:, r, :, :], ALU.mult,
                                                 ALU.add))
                        c.wait()
                    for j in range(GRP):
                        c(v.bn_stats(st[:, k.slot(2), j, :], z[:, r, j, :]))
                    c.wait()
                    v.sem_inc(order, 1)
                    for j in range(GRP):
                        c(v.bn_aggr(mv[:, r, j, :], st[:, k.slot(2), j, :]))

                def inverse(k):
                    r = k.slot(R)
                    v.wait_ge(sdd, k.t + 1)
                    v.reciprocal(rstd[:, r, :], sd[:, r, :]).then_inc(c3, 1)
                sweep(v, NGRP, [(L1_, raw), (L2_, combine), (L3_, inverse)], R)

            @block.gpsimd
            def _(g):
                def norm(k):
                    r = k.slot(R)
                    g.wait_ge(c3, k.t + 1)
                    if k.past(R):
                        g.wait_ge(sto[r], k.lap(R) * 16)
                    g.sem_inc(gate, 1)
                    for j in range(GRP):
                        ins = g.tensor_scalar(xo[:, r, j, 0:F], z[:, r, j, :], mv[:, r, j, 0:1], rstd[:, r, j:j + 1],
                                              ALU.subtract, ALU.mult)
                    if owid > F:
                        ins = g.tensor_copy(xo[:, r, :, F:F + 1], xn[:, r, :, F:F + 1])
                    ins.then_inc(fin, 1)
                sweep(g, NGRP, [(0, norm)], R)


BIG = 1e30


def attention_messages(nc, m, io, x, q, logits, hid):
    w = io.w
    with ExitStack() as ctx:
        sb, ps, sem = scope(nc, ctx, "a")
        wbs, wbd, w2 = sb("wbs", [P, P]), sb("wbd", [P, P]), sb("w2", [2 * V, V])
        gam, bet, gam2 = sb("gam", [P, 1]), sb("bet", [P, 1]), sb("gam2", [2 * V, 1])
        wr_, wal, wsv, wvv = sb("wrbf", [16, 224]), sb("wal", [96, 64]), sb("wsv", [96, 64]), sb("wvv", [P, V])
        wg, wsl, wvl = sb("wg", [64, V]), sb("wsl", [96, 64]), sb("wvl", [P, V])
        adot, w2c = sb("adot", [P, 64]), sb("w2c", [P, 224])
        half = sb("half", [P, 4])
        wl, wz = sem("wl"), sem("wz")

        def col(name):
            return w[name].rearrange("(a b) -> a b", b=1)
        gv = col("L2_gnn_gamma_v")
        loads = [(wb[a:b, a:b], w[f"L2_gnn_W{t}_{n}"]) for wb, n in ((wbs, "src"), (wbd, "dst"))
                 for a, b, t in ((0, 64, "s"), (64, 96, "v"), (96, 128, "v"))] + [
            (w2[0:V, :], w["L2_gnn_Wv_src"]), (w2[V:2 * V, :], w["L2_gnn_Wv_dst"]),
            (gam[0:64, :], col("L2_gnn_gamma_s")), (gam[64:96, :], gv), (gam[96:128, :], gv),
            (gam2[0:V, :], gv), (gam2[V:2 * V, :], gv), (bet[0:64, :], col("L2_gnn_beta_s")),
            (wr_[:, :], w["L2_gnn_W_rbf"]), (wal[:, :], w["L2_gnn_W_alpha"]), (wsv[:, :], w["L2_gnn_Ws_val"]),
            (wvv[:, :], w["L2_gnn_Wv_val"]), (wg[:, :], w["L2_gnn_Wg"]), (wsl[:, :], w["L2_gnn_Ws_vlin"]),
            (wvl[:, :], w["L2_gnn_Wv_vlin"]),
            (adot[:, :], w["L2_gnn_alpha_dot"].rearrange("a h k -> (a h k)").partition_broadcast(P))]
        at = 0
        for n in ("ss", "sv", "vs", "vv0", "vv1"):
            wd = w[f"L2_gnn_w2_{n}"]
            loads.append((w2c[:, at:at + wd.shape[0]], wd.partition_broadcast(P)))
            at += wd.shape[0]
        with nc.Block() as block:
            @block.vector
            def _(v):
                v.memset(wbs[:, :], 0.0).then_inc(wz, 1)
                v.memset(wbd[:, :], 0.0).then_inc(wz, 1)
                v.memset(bet[:, :], 0.0).then_inc(wz, 1)
                v.memset(half[:, :], -0.5).then_inc(wz, 1)

            @block.sync
            def _(sp):
                sp.wait_ge(wz, 4)
                chain_loads(sp, wl, loads)

        R = 4
        gi = sb("gi", [P, R, 2], I32)
        xg, ar = sb("xg", [P, R, 2, F + 1]), sb("ar", [P, R, 16])
        st, mvs = sb("st", [P, R, 2, 6]), sb("mvs", [P, R, 2, 3])
        sqj = sb("sqj", [P, 2, 96])
        vse, rsd = sb("vse", [P, R, 2, 2]), sb("rsd", [P, R, 2, 2])
        xn = sb("xn", [P, 2, 2 * P + 2 * V])
        t1, t2, ta = sb("t1", [P, 2, 2 * P]), sb("t2", [2 * V, 2, P]), sb("ta", [16, 2, P])
        sv, we = sb("sv", [P, R, 224]), sb("we", [P, R, 224])
        mid, tmp = sb("mid", [P, 2, 480]), sb("tmp", [P, 2, 480])
        ms, mvt = sb("ms", [96, 2, P]), sb("mvt", [P, 2, 3 * P])
        lg, lg4 = sb("lg", [P, 2, 128]), sb("lg4", [P, 2, 4])
        vt = sb("vt", [64, 2, P])
        val, gate_ = sb("val", [P, R, 224]), sb("gate", [P, R, V])
        vraw = sb("vraw", [P, R, F])
        mid2, tmp2 = sb("mid2", [P, 2, 480]), sb("tmp2", [P, 2, 480])
        ms2, mvt2 = sb("ms2", [96, 2, P]), sb("mvt2", [P, 2, 3 * P])
        hs = sb("hs", [P, R, F])
        pt, py, px, pv, pg, px2, ph = (ps(n) for n in ("pt", "py", "px", "pv", "pg", "px2", "ph"))
        gas, gad, sto = ([sem(f"{n}{r}") for r in range(R)] for n in ("gas", "gad", "sto"))
        gic, arc, gate, sqs, stt, rs, nrm, xt, xtc, y, svc, cg1, mt, mtc, o, oc, pgs, gsg, lgs, cg2, mt2, mtc2, h, hc = (
            sem(n) for n in ("gic", "arc", "gate", "sqs", "stt", "rs", "nrm", "xt", "xtc", "y", "svc", "cg1", "mt",
                             "mtc", "o", "oc", "pgs", "gsg", "lgs", "cg2", "mt2", "mtc2", "h", "hc"))
        order = sem("order")
        N1, N2, LG, C2 = 4, 6, 5, CG_OPS_CROSS + 2
        A_ST, A_RS, A_NRM, A_T, A_MAP, A_CG, A_TM, A_OUT, A_GATE, A_CG2, A_TM2, A_H, A_ST_OUT = (
            0, 1, 2, 2, 3, 3, 4, 5, 6, 6, 7, 8, 9)
        hv_ = hid.rearrange("(p j) f -> p j f", p=P)

        with nc.Block() as block:
            @block.gpsimd
            def _(g):
                top = g.to_reg(NROWS - 1)

                def gather(k):
                    r = k.slot(R)
                    if k.past(R):
                        g.wait_ge(gas[r], k.lap(R) * 16)
                        g.wait_ge(gad[r], k.lap(R) * 16)
                        g.wait_ge(nrm, (k.t - R + 1) * N2)
                        g.wait_ge(xt, k.t - R + 1)
                    g.tensor_copy(ar[:, r, :], q.attr[:, bass.ds(k.t, 1), A16:A16 + 16]).then_inc(arc, 1)
                    g.tensor_copy(gi[:, r, :], q.es[:, bass.ds(k.t, 1), GIDX:GIDX2 + 1].bitcast(I32)).then_inc(gic, 1)
                    g.wait_ge(gic, k.t + 1)
                    g.sem_inc(gate, 1)
                    for d, ga in enumerate((gas, gad)):
                        g.indirect_dma_start(xg[:, r, d, :], None, x,
                                             bass.IndirectOffsetOnAxis(ap=gi[:, r, d:d + 1], axis=0),
                                             bounds_check=top, oob_is_err=False).then_inc(ga[r], 16)

                def invert(k):
                    r = k.slot(R)
                    g.wait_ge(stt, (k.t + 1) * N1)
                    g.wait_ge(sqs, k.t + 1)
                    if k.past(R):
                        g.wait_ge(nrm, (k.t - R + 1) * N2)
                    g.sem_inc(gate, 1)
                    g.tensor_scalar(vse[:, r, :, :], mvs[:, r, :, 1:3], EPS, None, ALU.add).then_inc(rs, 1)
                    g.wait_ge(rs, 2 * k.t + 1)
                    g.sem_inc(gate, 1)
                    g.tensor_tensor(rsd[:, r, :, :].rearrange("p a b -> p (a b)"),
                                    vse[:, r, :, :].rearrange("p a b -> p (a b)"), half[:, :],
                                    ALU.pow).then_inc(rs, 1)
                sweep(g, ECOL, [(0, gather), (A_RS + 2, invert)], R)

            @block.tensor
            def _(pe):
                def turn(k):
                    r = k.slot(2)
                    if k.past(1):
                        pe.wait_ge(xtc, k.t)
                    pe.wait_ge(arc, k.t + 1)
                    pe.wait_ge(nrm, (k.t + 1) * N2)
                    pe.transpose(pt[:, 0:P], xn[:, r, 0:P], m.ident[:, :])
                    pe.transpose(pt[:, P:2 * P], xn[:, r, P:2 * P], m.ident[:, :])
                    pe.transpose(pt[0:2 * V, 2 * P:3 * P], xn[:, r, 2 * P:2 * P + 2 * V], m.ident[:, :])
                    pe.transpose(pt[0:16, 3 * P:4 * P], ar[:, k.slot(R), :], m.ident[:, :]).then_inc(xt, 1)

                def maps(k):
                    r = k.slot(2)
                    if k.past(1):
                        pe.wait_ge(svc, k.t)
                    pe.wait_ge(xtc, k.t + 1)
                    pe.matmul(py[:, 0:P], t1[:, r, 0:P], wbs[:, :], start=True, stop=False)
                    pe.matmul(py[:, 0:P], t1[:, r, P:2 * P], wbd[:, :], start=False, stop=True)
                    pe.matmul(py[:, P:F], t2[:, r, :], w2[:, :], start=True, stop=True)
                    pe.matmul(py[:, F:F + 224], ta[:, r, :], wr_[:, :], start=True, stop=True).then_inc(y, 1)

                def turn_mid(k, mid=mid, px=px, cgs=cg1, n=CG_OPS_CROSS, mtc=mtc, mt=mt):
                    r = k.slot(2)
                    pe.wait_ge(cgs, (k.t + 1) * n)
                    if k.past(1):
                        pe.wait_ge(mtc, k.t)
                    pe.transpose(px[0:96, 0:P], mid[:, r, 0:96], m.ident[:, :])
                    for d in range(3):
                        ins = pe.transpose(px[:, (d + 1) * P:(d + 2) * P], mid[:, r, 96 + d * P:96 + (d + 1) * P],
                                           m.ident[:, :])
                    ins.then_inc(mt, 1)

                def out(k):
                    r = k.slot(2)
                    pe.wait_ge(mtc, k.t + 1)
                    if k.past(1):
                        pe.wait_ge(oc, k.t)
                    pe.matmul(pv[:, 0:64], ms[:, r, :], wal[:, :], start=True, stop=True)
                    pe.matmul(pv[:, 64:128], ms[:, r, :], wsv[:, :], start=True, stop=True)
                    for d in range(3):
                        pe.matmul(pv[:, P + d * V:P + (d + 1) * V], mvt[:, r, d * P:(d + 1) * P], wvv[:, :],
                                  start=True, stop=True)
                    pe.matmul(pv[0:64, 224:224 + P], wsv[:, :], ms[:, r, :], start=True, stop=True).then_inc(o, 1)

                def gates(k):
                    pe.wait_ge(oc, k.t + 1)
                    if k.past(1):
                        pe.wait_ge(gsg, k.t)
                    pe.sem_inc(order, 1)
                    pe.matmul(pg[:, 0:V], vt[:, k.slot(2), :], wg[:, :], start=True, stop=True).then_inc(pgs, 1)

                def turn_mid2(k):
                    turn_mid(k, mid2, px2, cg2, C2, mtc2, mt2)

                def heads(k):
                    r = k.slot(2)
                    pe.wait_ge(mtc2, k.t + 1)
                    if k.past(1):
                        pe.wait_ge(hc, k.t)
                    pe.matmul(ph[:, 0:64], ms2[:, r, :], wsl[:, :], start=True, stop=True)
                    for d in range(3):
                        ins = pe.matmul(ph[:, 64 + d * V:96 + d * V], mvt2[:, r, d * P:(d + 1) * P], wvl[:, :],
                                        start=True, stop=True)
                    ins.then_inc(h, 1)
                sweep(pe, ECOL, [(A_T, turn), (A_MAP, maps), (A_TM, turn_mid), (A_OUT, out), (A_GATE, gates),
                                 (A_TM2, turn_mid2), (A_H, heads)], 2)

            @block.scalar
            def _(a):
                def squares(k):
                    r = k.slot(R)
                    a.wait_ge(gas[r], (k.lap(R) + 1) * 16)
                    a.wait_ge(gad[r], (k.lap(R) + 1) * 16)
                    if k.past(R):
                        a.wait_ge(rs, 2 * (k.t - R + 1))
                    for d in range(2):
                        if d == 0 and k.past(1):
                            a.wait_ge(sqs, k.t)
                        ins = a.activation(sqj[:, d, :], xg[:, r, d, 64:F], ACT.Square, scale=float(1 / np.sqrt(32.0)),
                                           accum_out=mvs[:, r, d, 2:3])
                    ins.then_inc(sqs, 1)

                def copy_x(k):
                    r = k.slot(2)
                    if k.past(2):
                        a.wait_ge(y, k.t - 1)
                    a.wait_ge(xt, k.t + 1)
                    a.activation(t1[:, r, :], pt[:, 0:2 * P], ACT.Identity, scale=gam[:, :], bias=bet[:, :])
                    a.activation(t2[:, r, :], pt[0:2 * V, 2 * P:3 * P], ACT.Copy, scale=gam2[:, :])
                    a.copy(ta[:, r, :], pt[0:16, 3 * P:4 * P]).then_inc(xtc, 1)

                def copy_y(k):
                    r = k.slot(R)
                    a.wait_ge(y, k.t + 1)
                    if k.past(R):
                        a.wait_ge(cg1, (k.t - R + 1) * CG_OPS_CROSS)
                    a.copy(sv[:, r, 0:F], py[:, 0:F])
                    a.copy(sv[:, r, F:224], py[:, 64:128])
                    a.copy(we[:, r, :], py[:, F:F + 224]).then_inc(svc, 1)

                def copy_mid(k, px=px, ms=ms, mvt=mvt, mt=mt, o=o, mtc=mtc):
                    r = k.slot(2)
                    a.wait_ge(mt, k.t + 1)
                    if k.past(2):
                        a.wait_ge(o, k.t - 1)
                    a.copy(ms[:, r, :], px[0:96, 0:P])
                    a.copy(mvt[:, r, :], px[:, P:4 * P]).then_inc(mtc, 1)

                def copy_out(k):
                    r = k.slot(2)
                    a.wait_ge(o, k.t + 1)
                    if k.past(2):
                        a.wait_ge(pgs, k.t - 1)
                    if k.past(R):
                        a.wait_ge(lgs, (k.t - R + 1) * LG)
                        a.wait_ge(cg2, (k.t - R + 1) * C2)
                    a.copy(vt[:, r, :], pv[0:64, 224:224 + P])
                    a.copy(vraw[:, k.slot(R), 0:64], pv[:, 0:64])
                    a.copy(vraw[:, k.slot(R), 64:F], pv[:, P:224])
                    a.activation(val[:, k.slot(R), 0:64], pv[:, 64:128], ACT.Sigmoid).then_inc(oc, 1)

                def gate_sig(k):
                    a.wait_ge(pgs, k.t + 1)
                    if k.past(R):
                        a.wait_ge(cg2, (k.t - R + 1) * C2)
                    a.activation(gate_[:, k.slot(R), :], pg[:, 0:V], ACT.Sigmoid).then_inc(gsg, 1)

                def copy_mid2(k):
                    copy_mid(k, px2, ms2, mvt2, mt2, h, mtc2)

                def copy_h(k):
                    r = k.slot(R)
                    a.wait_ge(h, k.t + 1)
                    if k.past(R):
                        a.wait_ge(sto[r], k.lap(R) * 16)
                    a.copy(hs[:, r, :], ph[:, 0:F]).then_inc(hc, 1)
                sweep(a, ECOL, [(A_ST, squares), (A_T, copy_x), (A_MAP, copy_y), (A_TM, copy_mid), (A_OUT, copy_out),
                                (A_GATE, gate_sig), (A_TM2, copy_mid2), (A_H, copy_h)], R)

            @block.sync
            def _(sp):
                def store(k):
                    r = k.slot(R)
                    sp.wait_ge(hc, k.t + 1)
                    sp.dma_start(hv_[:, bass.ds(k.t, 1), :].rearrange("p a f -> p (a f)"), hs[:, r, :]).then_inc(sto[r], 16)
                sweep(sp, ECOL, [(0, store)], 4)
                for r in range(R):
                    sp.wait_ge(sto[r], 16 * len(range(r, ECOL, R)))

            @block.vector
            def _(v):
                def stats(k):
                    r = k.slot(R)
                    v.wait_ge(gas[r], (k.lap(R) + 1) * 16)
                    v.wait_ge(gad[r], (k.lap(R) + 1) * 16)
                    c = Chain(v, stt, N1, k)
                    if k.past(R):
                        v.wait_ge(rs, 2 * (k.t - R + 1))
                    for d in range(2):
                        c(v.bn_stats(st[:, r, d, :], xg[:, r, d, 0:64]))
                    c.wait()
                    v.sem_inc(order, 1)
                    for d in range(2):
                        c(v.bn_aggr(mvs[:, r, d, 0:2], st[:, r, d, :]))

                def normalize(k):
                    r = k.slot(R)
                    c = Chain(v, nrm, N2, k)
                    v.wait_ge(rs, 2 * k.t + 2)
                    if k.past(2):
                        v.wait_ge(xt, k.t - 1)
                    n = xn[:, k.slot(2), :]
                    for d in range(2):
                        c(v.tensor_scalar(n[:, d * P:d * P + 64], xg[:, r, d, 0:64], mvs[:, r, d, 0:1],
                                          rsd[:, r, d, 0:1], ALU.subtract, ALU.mult))
                        c(v.tensor_scalar(n[:, d * P + 64:(d + 1) * P], xg[:, r, d, 64:P], rsd[:, r, d, 1:2], None,
                                          ALU.mult))
                        c(v.tensor_scalar(n[:, 2 * P + d * V:2 * P + (d + 1) * V], xg[:, r, d, P:F],
                                          rsd[:, r, d, 1:2], None, ALU.mult))

                def y1(k):
                    return lambda i, j: q.es[:, bass.ds(k.t, 1), Y1 + i:Y1 + j].rearrange("p a c -> p (a c)")

                def product(k):
                    r = k.slot(2)
                    v.wait_ge(svc, k.t + 1)
                    if k.past(2):
                        v.wait_ge(mt, k.t - 1)
                    c = Chain(v, cg1, CG_OPS_CROSS, k)
                    s = sv[:, k.slot(R), :]
                    cg(v, c, we[:, k.slot(R), :], s[:, 0:64], s[:, 64:224], q.es[:, bass.ds(k.t, 1), Y0], y1(k), R3,
                       mid[:, r, :], tmp[:, r, :], True)

                def logit(k):
                    r = k.slot(2)
                    c = Chain(v, lgs, LG, k)
                    v.wait_ge(oc, k.t + 1)
                    a = vraw[:, k.slot(R), 0:64]
                    c(v.scalar_tensor_tensor(lg[:, r, 0:64], a, 0.2, a, ALU.mult, ALU.max))
                    c.wait()
                    c(v.tensor_tensor(lg[:, r, 64:128], lg[:, r, 0:64], adot[:, :], ALU.mult))
                    c.wait()
                    c(v.tensor_reduce(lg4[:, r, :], lg[:, r, 64:128].rearrange("p (h a) -> p h a", h=4), AX, ALU.add))
                    c.wait()
                    c(v.tensor_scalar(logits[:, :, bass.ds(k.t, 1)].rearrange("p h a -> p (h a)"), lg4[:, r, :], 1.0,
                                      None, ALU.mult))
                    c(v.tensor_scalar(lg[:, r, 0:1], lg[:, r, 0:1], 1.0, None, ALU.mult))

                def product2(k):
                    r, q4 = k.slot(2), k.slot(R)
                    v.wait_ge(gsg, k.t + 1)
                    if k.past(2):
                        v.wait_ge(mt2, k.t - 1)
                    c = Chain(v, cg2, C2, k)
                    raw = vraw[:, q4, 64:F]
                    c(v.tensor_tensor(val[:, q4, 64:F].rearrange("p (c u) -> p c u", c=3),
                                      raw.rearrange("p (c u) -> p c u", c=3), bc(gate_[:, q4, :], 1, 3), ALU.mult))
                    c(v.tensor_tensor(val[:, q4, F:224].rearrange("p (c u) -> p c u", c=2),
                                      raw[:, 0:64].rearrange("p (c u) -> p c u", c=2), bc(gate_[:, q4, :], 1, 2),
                                      ALU.mult))
                    c.wait()
                    c2 = Shifted(c, 2)
                    s = val[:, q4, :]
                    cg(v, c2, w2c[:, :], s[:, 0:64], s[:, 64:224], q.es[:, bass.ds(k.t, 1), Y0], y1(k), R3,
                       mid2[:, r, :], tmp2[:, r, :], True)
                sweep(v, ECOL, [(A_ST, stats), (A_NRM, normalize), (A_CG, product), (A_OUT, logit),
                                (A_CG2, product2)], R)


def attention_weights(nc, m, q, logits, ex):
    with ExitStack() as ctx:
        sb, ps, sem = scope(nc, ctx, "w")
        ch, pe_s, ex_s = sem("ch"), sem("pe"), sem("ex")
        pf, pb, prun = sb("pf", [P, ECOL]), sb("pb", [P, ECOL]), sb("prun", [P, 2, ECOL])
        fw, bw = sb("fw", [P, 4, ECOL]), sb("bw", [P, 4, ECOL])
        wide = sb("wide", [P, 10, P])
        rows, pen = sb("rows", [P, 10, P]), sb("pen", [P, 2, 2, P])
        cand = sb("cand", [P, 2, 4, 2 * P])
        top = sb("top", [P, 2, 4])
        dif = sb("dif", [P, 4, ECOL])
        pr = [ps(f"pr{b}") for b in range(3)]
        block = ctx.enter_context(nc.Block())

        @block.vector
        def _(v):
            c = Static(v, ch)
            c(v.tensor_scalar(pf[:, :], q.es[:, :, SAME], -1.0, BIG, ALU.add, ALU.mult), wait=False)
            c(v.memset(pb[:, ECOL - 1:ECOL], -BIG), wait=False)
            c(v.tensor_scalar(pb[:, 0:ECOL - 1], q.es[:, 1:ECOL, SAME], -1.0, BIG, ALU.add, ALU.mult), wait=False)
            c(v.tensor_scalar(prun[:, 0, :], q.first_run[:, :], -1.0, BIG, ALU.add, ALU.mult), wait=False)
            c(v.tensor_scalar(prun[:, 1, :], q.last_run[:, :], -1.0, BIG, ALU.add, ALU.mult))
            for h in range(4):
                c(v.tensor_tensor_scan(fw[:, h, :], pf[:, :], logits[:, h, :], 0.0, ALU.add, ALU.max))
                c(v.tensor_tensor_scan(bw[:, h, ::-1], pb[:, ::-1], fw[:, h, ::-1], 0.0, ALU.add, ALU.max))
            for i in range(10):
                src = q.ends[:, i - 8:i - 7] if i >= 8 else bw[:, i % 4, (i // 4) * (ECOL - 1):(i // 4) * (ECOL - 1) + 1]
                c(v.tensor_scalar(wide[:, i, :], m.ones[:, :], src, None, ALU.mult), wait=False)
            v.sem_inc(ex_s, 1)
            v.wait_ge(ch, c.n)
            v.sem_inc(ex_s, 1)
            v.wait_ge(pe_s, 1)
            for i in range(10):
                c(v.tensor_copy(rows[:, i, :], pr[i // 4][:, (i % 4) * P:(i % 4 + 1) * P]), wait=i == 9)
            for t in range(2):
                for e in range(2):
                    c(v.tensor_scalar(pen[:, t, e, :], rows[:, 8 + e, :], q.ends[:, t:t + 1], -1.0, ALU.is_equal,
                                      ALU.add))
                    c(v.tensor_scalar(pen[:, t, e, :], pen[:, t, e, :], BIG, None, ALU.mult))
                for h in range(4):
                    for e in range(2):
                        c(v.tensor_tensor(cand[:, t, h, e * P:(e + 1) * P], rows[:, 4 * e + h, :], pen[:, t, e, :],
                                          ALU.add), wait=False)
                v.wait_ge(ch, c.n)
                c(v.tensor_reduce(top[:, t, :], cand[:, t, :, :], AX, ALU.max))
                for h in range(4):
                    c(v.scalar_tensor_tensor(bw[:, h, :], prun[:, t, :], top[:, t, h:h + 1], bw[:, h, :], ALU.add,
                                             ALU.max), wait=h == 3)
            c(v.tensor_tensor(dif[:, :, :], logits[:, :, :], bw[:, :, :], ALU.subtract))
            v.sem_inc(ex_s, 1)

        @block.tensor
        def _(pe):
            pe.wait_ge(ex_s, 2)
            for i in range(10):
                ins = pe.transpose(pr[i // 4][:, (i % 4) * P:(i % 4 + 1) * P], wide[:, i, :], m.ident[:, :])
            ins.then_inc(pe_s, 1)

        @block.scalar
        def _(a):
            a.wait_ge(ex_s, 3)
            a.activation(ex[:, :, :].rearrange("p j h -> p h j"), dif[:, :, :], ACT.Exp)


def attention_sums(nc, m, io, q, ex, hid, agg):
    w = io.w
    A = F + 4
    with ExitStack() as ctx:
        sb, ps, sem = scope(nc, ctx, "s")
        wb, w2 = sb("wb", [P, P]), sb("w2", [V, V])
        wl, wz = sem("wl"), sem("wz")
        with nc.Block() as block:
            @block.vector
            def _(v):
                v.memset(wb[:, :], 0.0).then_inc(wz, 1)

            @block.sync
            def _(sp):
                sp.wait_ge(wz, 1)
                chain_loads(sp, wl, block_loads(wb, w2, w["L2_gnn_Wps"], w["L2_gnn_Wpv"]))
        R = 4
        wi, hb, eh = sb("wi", [P, R, 1], I32), sb("hb", [P, R, F]), sb("eh", [P, 2, A])
        tot, s1, cap = sb("tot", [P, R, A]), sb("s1", [P, A]), sb("cap", [P, A])
        den, avg = sb("den", [P, 2, 8]), sb("avg", [P, 2, F])
        t1, t2, ob = sb("t1", [P, 2, P]), sb("t2", [V, 2, P]), sb("ob", [P, R, F])
        pt, py = [ps(f"pt{r}") for r in range(2)], [ps(f"py{r}") for r in range(2)]
        pf = ps("pf")
        ld, sct = [sem(f"ld{r}") for r in range(R)], [sem(f"sct{r}") for r in range(R)]
        wic, gate, init, acc, nrm, xt, xtc, y, obc, fx = (sem(n) for n in (
            "wic", "gate", "init", "acc", "nrm", "xt", "xtc", "y", "obc", "fx"))
        AC, NR = 6, 4
        hv_ = hid.rearrange("(p j) f -> p j f", p=P)
        with nc.Block() as block:
            @block.sync
            def _(sp):
                def load(k):
                    r = k.slot(R)
                    if k.past(R):
                        sp.wait_ge(acc, (k.t - R + 1) * AC)
                    sp.dma_start(hb[:, r, :], hv_[:, bass.ds(k.t, 1), :].rearrange("p a f -> p (a f)")).then_inc(ld[r], 16)
                sweep(sp, ECOL, [(0, load)], R)

            @block.vector
            def _(v):
                v.memset(s1[:, :], 0.0).then_inc(init, 1)
                v.memset(tot[:, R - 1, :], 0.0).then_inc(init, 1)
                v.wait_ge(init, 2)

                def accumulate(k):
                    r = k.slot(R)
                    c = Chain(v, acc, AC, k)
                    if k.past(R):
                        v.wait_ge(nrm, (k.t - R + 1) * NR)
                    if k.is_fix():
                        v.wait_ge(fx, 1)
                        v.wait_ge(acc, ECOL * AC)
                        v.tensor_tensor(tot[:, r, :], s1[:, :], pf[:, 0:A], ALU.add).then_inc(acc, AC)
                        return
                    v.wait_ge(ld[r], (k.lap(R) + 1) * 16)
                    e = ex[:, bass.ds(k.t, 1), :].rearrange("p a h -> p (a h)")
                    o = eh[:, k.slot(2), :]
                    c(v.tensor_tensor(o[:, 0:64].rearrange("p (h a) -> p h a", h=4),
                                      hb[:, r, 0:64].rearrange("p (h a) -> p h a", h=4), bc(e, 2, 16), ALU.mult))
                    c(v.tensor_tensor(o[:, 64:F].rearrange("p (c h a) -> p c h a", c=3, h=4),
                                      hb[:, r, 64:F].rearrange("p (c h a) -> p c h a", c=3, h=4),
                                      bc(bc(e, 2, 8), 1, 3), ALU.mult))
                    c(v.tensor_scalar(o[:, F:A], e, 1.0, None, ALU.mult))
                    c.wait()
                    edge = bass.ds(k.t, 1)
                    c(v.scalar_tensor_tensor(tot[:, r, :], tot[:, (r - 1) % R, :], q.es[:, edge, SAME], o, ALU.mult,
                                             ALU.add))
                    c.wait()
                    c(v.tensor_scalar(cap[:, :], tot[:, r, :], q.es[:, edge, FEND], None, ALU.mult))
                    c.wait()
                    c(v.tensor_tensor(s1[:, :], s1[:, :], cap[:, :], ALU.add))

                def divide(k):
                    r, d = k.slot(R), k.slot(2)
                    c = Chain(v, nrm, NR, k)
                    v.wait_ge(acc, (k.t + 1) * AC)
                    if k.past(2):
                        v.wait_ge(xt, k.t - 1)
                    c(v.tensor_scalar(den[:, d, 0:4], tot[:, r, F:A], 1e-16, None, ALU.add))
                    c.wait()
                    c(v.reciprocal(den[:, d, 4:8], den[:, d, 0:4]))
                    c.wait()
                    inv = den[:, d, 4:8]
                    c(v.tensor_tensor(avg[:, d, 0:64].rearrange("p (h a) -> p h a", h=4),
                                      tot[:, r, 0:64].rearrange("p (h a) -> p h a", h=4), bc(inv, 2, 16), ALU.mult))
                    c(v.tensor_tensor(avg[:, d, 64:F].rearrange("p (c h a) -> p c h a", c=3, h=4),
                                      tot[:, r, 64:F].rearrange("p (c h a) -> p c h a", c=3, h=4),
                                      bc(bc(inv, 2, 8), 1, 3), ALU.mult))
                sweep(v, ECOL, [(0, accumulate, 1), (1, divide, 1)], R)

            @block.tensor
            def _(pe):
                def turn(k):
                    r = k.slot(2)
                    pe.wait_ge(nrm, (k.t + 1) * NR)
                    if k.past(2):
                        pe.wait_ge(xtc, k.t - 1)
                    pe.transpose(pt[r][:, 0:P], avg[:, r, 0:P], m.ident[:, :])
                    pe.transpose(pt[r][0:V, P:2 * P], avg[:, r, P:F], m.ident[:, :]).then_inc(xt, 1)

                def maps(k):
                    r = k.slot(2)
                    pe.wait_ge(xtc, k.t + 1)
                    if k.past(2):
                        pe.wait_ge(obc, k.t - 1)
                    pe.matmul(py[r][:, 0:P], t1[:, r, :], wb[:, :], start=True, stop=True)
                    pe.matmul(py[r][:, P:F], t2[:, r, :], w2[:, :], start=True, stop=True).then_inc(y, 1)

                def fix(k):
                    if k.is_fix():
                        pe.wait_ge(acc, ECOL * AC)
                        pe.matmul(pf[:, 0:A], q.carry[:, :], tot[:, (ECOL - 1) % R, :], start=True,
                                  stop=True).then_inc(fx, 1)
                sweep(pe, ECOL, [(0, fix, 1), (1, turn, 1), (2, maps, 1)], 2)

            @block.scalar
            def _(a):
                def copy_x(k):
                    r = k.slot(2)
                    a.wait_ge(xt, k.t + 1)
                    if k.past(2):
                        a.wait_ge(y, k.t - 1)
                    a.copy(t1[:, r, :], pt[r][:, 0:P])
                    a.copy(t2[:, r, :], pt[r][0:V, P:2 * P]).then_inc(xtc, 1)

                def copy_y(k):
                    r = k.slot(R)
                    a.wait_ge(y, k.t + 1)
                    if k.past(R):
                        a.wait_ge(sct[r], k.lap(R) * 16)
                    a.copy(ob[:, r, :], py[k.slot(2)][:, 0:F]).then_inc(obc, 1)
                sweep(a, ECOL, [(0, copy_x, 1), (1, copy_y, 1)], R)

            @block.gpsimd
            def _(g):
                top = g.to_reg(NROWS - 1)

                def scatter(k):
                    r = k.slot(R)
                    if k.past(R):
                        g.wait_ge(sct[r], k.lap(R) * 16)
                    src = q.fix_id[:, :] if k.is_fix() else q.es[:, bass.ds(k.t, 1), WIDX].bitcast(I32)
                    g.tensor_copy(wi[:, r, :], src).then_inc(wic, 1)
                    g.wait_ge(wic, k.t + 1)
                    g.wait_ge(obc, k.t + 1)
                    g.sem_inc(gate, 1)
                    g.indirect_dma_start(agg, bass.IndirectOffsetOnAxis(ap=wi[:, r, :], axis=0), ob[:, r, :], None,
                                         bounds_check=top, oob_is_err=False).then_inc(sct[r], 16)
                sweep(g, ECOL, [(0, scatter, 1)], R)
                for r in range(R):
                    g.wait_ge(sct[r], 16 * len(range(r, ECOL + 1, R)))


def bilinear_layer(nc, m, io, x, q, agg):
    w = io.w
    c96 = float(1 / np.sqrt(96.0))
    f0, f1 = float(1 / np.sqrt(S * S + V * V)), float(1 / np.sqrt(2 * S * V))
    NZ0, NZ1 = S * S // P, 3 * V * V // P
    NG = (NZ0 + NZ1) // 4
    HALF = V * V
    with ExitStack() as ctx:
        sb, ps, sem = scope(nc, ctx, "b")
        wm1, wm2 = sb("wm1", [P, 416]), sb("wm2", [V, P])
        w000, w110 = sb("w000", [P, NZ0, 64]), sb("w110", [P, V * V // P, 64])
        w011, w101 = sb("w011", [S, HALF]), sb("w101", [S, V, V])
        wl, wz, wsc = sem("wl"), sem("wz"), sem("wsc")
        w2d = {n: w[f"L3_gnn_{n}"].rearrange("u a w -> (u a) w") for n in ("wm000", "wm011", "wm101", "wm110")}
        loads = [(wm1[0:64, 0:64], w2d["wm000"]), (wm1[0:64, 64:128], w["L3_gnn_lm0"]),
                 (wm1[0:64, 128:160], w2d["wm011"])]
        for blk, at in ((wm1[64:96, 160:288], 0), (wm1[96:128, 288:416], 1), (wm2[:, :], 2)):
            loads += [(blk[:, 0:64], w2d["wm110"]), (blk[:, 64:96], w2d["wm101"]), (blk[:, 96:128], w["L3_gnn_lm1"])]
        loads += [(w000[:, :, :], w["L3_gnn_wu000"].rearrange("(k a) v w -> (a v) k w", a=2)),
                  (w110[:, :, :], w["L3_gnn_wu110"].rearrange("(k a) v w -> (a v) k w", a=4)),
                  (w011[:, :], w["L3_gnn_wu011"].rearrange("u v w -> u (v w)")),
                  (w101[:, :, :], w["L3_gnn_wu101"].rearrange("u v w -> v u w"))]
        with nc.Block() as block:
            @block.vector
            def _(v):
                v.memset(wm1[:, :], 0.0).then_inc(wz, 1)
                v.tensor_copy(q.es[:, :, Y0], q.attr[:, :, A4 + 3]).then_inc(wsc, 1)
                v.tensor_copy(q.es[:, :, Y1:Y1 + 3], q.attr[:, :, A4:A4 + 3]).then_inc(wsc, 1)

            @block.sync
            def _(sp):
                sp.wait_ge(wz, 1)
                chain_loads(sp, wl, loads)
                sp.sem_inc(wz, 1)

            @block.scalar
            def _(a):
                a.wait_ge(wz, 2)
                blocks = wm1[:, 160:416].rearrange("p (c k) -> p c k", c=2)
                for ap, f in ((wm1[:, 0:64], c96), (wm1[:, 64:128], 1 / 8.0), (wm1[:, 128:160], c96),
                              (blocks[:, :, 0:64], R3 * c96), (blocks[:, :, 64:96], c96),
                              (blocks[:, :, 96:128], float(1 / np.sqrt(32.0))), (wm2[:, 0:64], R3 * c96),
                              (wm2[:, 64:96], c96), (wm2[:, 96:128], float(1 / np.sqrt(32.0))),
                              (w000[:, :, :], f0), (w110[:, :, :], R3 * f0), (w011[:, :], f1), (w101[:, :, :], f1)):
                    a.mul(ap, ap, f).then_inc(wsc, 1)

        R = 4
        gi, gj, wi = (sb(n, [P, R, 1], I32) for n in ("gi", "gj", "wi"))
        xd, xs = sb("xd", [P, R, F + 1]), sb("xs", [P, R, F + 1])
        t1, t2 = sb("t1", [P, 2, P]), sb("t2", [V, 2, P])
        mp, mg, tmp = sb("mp", [P, 2, 544]), sb("mg", [P, 2, F]), sb("tmp", [P, 2, 352])
        tot, s1, cap = sb("tot", [P, R, F]), sb("s1", [P, F]), sb("cap", [P, F])
        xa = sb("xa", [S, 2, 2 * P])
        z = sb("z", [P, 2, (NZ0 + NZ1) * P])
        zt = sb("zt", [P, 2, 512])
        yt, pr = sb("yt", [P, 2 * HALF]), sb("pr", [P, 3, 2 * V, V])
        ub = sb("ub", [P, R, F])
        pt, pm1, pm2, pxa, pyt, po = (ps(n) for n in ("pt", "pm1", "pm2", "pxa", "pyt", "po"))
        pz = [ps(f"pz{r}") for r in range(2)]
        gad, gas, sct = ([sem(f"{n}{r}") for r in range(R)] for n in ("gad", "gas", "sct"))
        (gic, gjc, wic, gate, init, xt, xtc, y, mpc, acc, fx, xat, xac, zp, ztr, ztc, zm, yq, yqc, vd, uc) = (
            sem(n) for n in ("gic", "gjc", "wic", "gate", "init", "xt", "xtc", "y", "mpc", "acc", "fx", "xat", "xac",
                             "zp", "ztr", "ztc", "zm", "yq", "yqc", "vd", "uc"))
        AC, ZP, VD = 10, 2, 3
        YAT = (1, 4, 7, 10)
        L_ACC, L_Z, L_XA, L_BIG, L_VEC, L_SC = 2, 2, 3, 4, 4, 6

        with nc.Block() as block:
            @block.gpsimd
            def _(g):
                top = g.to_reg(NROWS - 1)

                def gather_dst(k):
                    r = k.slot(R)
                    if k.past(R):
                        g.wait_ge(gad[r], k.lap(R) * 16)
                        g.wait_ge(xt, k.t - R + 1)
                    g.tensor_copy(gi[:, r, :], q.es[:, bass.ds(k.t, 1), GIDX].bitcast(I32)).then_inc(gic, 1)
                    g.wait_ge(gic, k.t + 1)
                    g.sem_inc(gate, 1)
                    g.indirect_dma_start(xd[:, r, :], None, x, bass.IndirectOffsetOnAxis(ap=gi[:, r, :], axis=0),
                                         bounds_check=top, oob_is_err=False).then_inc(gad[r], 16)

                def gather_src(k):
                    r = k.slot(R)
                    if k.past(R):
                        g.wait_ge(gas[r], k.lap(R) * 16)
                        g.wait_ge(vd, (k.t - R + 1) * VD)
                        g.wait_ge(xat, k.t - R + 1)
                    src = q.first_id[:, :] if k.is_fix() else q.es[:, bass.ds(k.t, 1), GIDX2].bitcast(I32)
                    g.tensor_copy(gj[:, r, :], src).then_inc(gjc, 1)
                    g.wait_ge(gjc, k.t + 1)
                    g.sem_inc(gate, 1)
                    g.indirect_dma_start(xs[:, r, :], None, x, bass.IndirectOffsetOnAxis(ap=gj[:, r, :], axis=0),
                                         bounds_check=top, oob_is_err=False).then_inc(gas[r], 16)

                def scatter(k):
                    r = k.slot(R)
                    if k.past(R):
                        g.wait_ge(sct[r], k.lap(R) * 16)
                    src = q.fix_id[:, :] if k.is_fix() else q.es[:, bass.ds(k.t, 1), WIDX].bitcast(I32)
                    g.tensor_copy(wi[:, r, :], src).then_inc(wic, 1)
                    g.wait_ge(wic, k.t + 1)
                    g.wait_ge(uc, k.t + 1)
                    g.wait_ge(vd, (k.t + 1) * VD)
                    g.sem_inc(gate, 1)
                    g.indirect_dma_start(agg, bass.IndirectOffsetOnAxis(ap=wi[:, r, :], axis=0), ub[:, r, :], None,
                                         bounds_check=top, oob_is_err=False).then_inc(sct[r], 16)
                sweep(g, ECOL, [(0, gather_dst), (1, gather_src, 1), (L_SC, scatter, 1)], R)
                for r in range(R):
                    g.wait_ge(sct[r], 16 * len(range(r, ECOL + 1, R)))

            @block.tensor
            def _(pe):
                def turn(k):
                    if k.past(1):
                        pe.wait_ge(xtc, k.t)
                    pe.wait_ge(gad[k.slot(R)], (k.lap(R) + 1) * 16)
                    pe.transpose(pt[:, 0:P], xd[:, k.slot(R), 0:P], m.ident[:, :])
                    pe.transpose(pt[0:V, P:2 * P], xd[:, k.slot(R), P:F], m.ident[:, :]).then_inc(xt, 1)

                def maps(k):
                    r = k.slot(2)
                    pe.wait_ge(xtc, k.t + 1)
                    if k.past(1):
                        pe.wait_ge(mpc, k.t)
                    pe.matmul(pm1[:, 0:416], t1[:, r, :], wm1[:, :], start=True, stop=True)
                    pe.matmul(pm2[:, 0:P], t2[:, r, :], wm2[:, :], start=True, stop=True).then_inc(y, 1)

                def fix(k):
                    if k.is_fix():
                        pe.wait_ge(acc, ECOL * AC)
                        pe.wait_ge(mpc, ECOL)
                        pe.matmul(pm1[:, 0:F], q.carry[:, :], tot[:, (ECOL - 1) % R, :], start=True,
                                  stop=True).then_inc(fx, 1)

                def turn_scalars(k):
                    r = k.slot(R)
                    pe.wait_ge(gas[r], (k.lap(R) + 1) * 16)
                    pe.wait_ge(acc, (k.t + 1) * AC)
                    if k.past(1):
                        pe.wait_ge(xac, k.t)
                    pe.sem_inc(gate, 1)
                    pe.transpose(pxa[0:S, 0:P], xs[:, r, 0:S], m.ident[:, :])
                    pe.transpose(pxa[0:S, P:2 * P], tot[:, r, 0:S], m.ident[:, :]).then_inc(xat, 1)

                def big(k):
                    r = k.slot(2)

                    def turn_group(g):
                        n = k.t * NG + g
                        pe.wait_ge(zp, k.t * ZP + (1 if g < NZ0 // 4 else 2))
                        if g >= 2 or k.past(1):
                            pe.wait_ge(ztc, n - 1)
                        for j in range(4):
                            at = (4 * g + j) * P
                            ins = pe.transpose(pz[g % 2][:, j * P:(j + 1) * P], z[:, r, at:at + P], m.ident[:, :])
                        ins.then_inc(ztr, 1)

                    def sum_group(g):
                        pe.wait_ge(ztc, k.t * NG + g + 1)
                        if g == 0 and k.past(1):
                            pe.wait_ge(uc, k.t)
                        for j in range(4):
                            c = 4 * g + j
                            wc = w000[:, c, :] if c < NZ0 else w110[:, (c - NZ0) % (V * V // P), :]
                            ins = pe.matmul(po[:, 0:S], zt[:, g % 2, j * P:(j + 1) * P], wc, start=(c == 0),
                                            stop=(c == NZ0 + NZ1 - 1))
                        ins.then_inc(zm, 1)

                    for g in range(NG):
                        turn_group(g)
                        if g in YAT:
                            i = YAT.index(g)
                            if i == 0:
                                pe.wait_ge(xac, k.t + 1)
                            if i > 0 or k.past(1):
                                pe.wait_ge(yqc, k.t * 4 + i)
                            pe.sem_inc(gate, 1)
                            wt = w011[:, (i % 2) * 512:(i % 2 + 1) * 512] if i < 2 else \
                                w101[:, (i % 2) * 16:(i % 2 + 1) * 16, :].rearrange("p a b -> p (a b)")
                            pe.matmul(pyt[:, :], xa[:, r, (i // 2) * P:(i // 2 + 1) * P], wt, start=True,
                                      stop=True).then_inc(yq, 1)
                        if g > 0:
                            sum_group(g - 1)
                    sum_group(NG - 1)
                sweep(pe, ECOL, [(L_ACC, fix, 1), (0, turn), (1, maps), (L_XA, turn_scalars, 1), (L_BIG, big, 1)], 2)

            @block.scalar
            def _(a):
                def copy_x(k):
                    r = k.slot(2)
                    a.wait_ge(xt, k.t + 1)
                    if k.past(2):
                        a.wait_ge(y, k.t - 1)
                    a.copy(t1[:, r, :], pt[:, 0:P])
                    a.copy(t2[:, r, :], pt[0:V, P:2 * P]).then_inc(xtc, 1)

                def copy_y(k):
                    r = k.slot(2)
                    a.wait_ge(y, k.t + 1)
                    if k.past(2):
                        a.wait_ge(acc, (k.t - 1) * AC)
                    a.copy(mp[:, r, 0:416], pm1[:, 0:416])
                    a.copy(mp[:, r, 416:544], pm2[:, 0:P]).then_inc(mpc, 1)

                def copy_xa(k):
                    a.wait_ge(xat, k.t + 1)
                    if k.past(2):
                        a.wait_ge(yq, (k.t - 1) * 4)
                    a.copy(xa[:, k.slot(2), :], pxa[0:S, 0:2 * P]).then_inc(xac, 1)

                def big(k):
                    for g in range(NG):
                        n = k.t * NG + g
                        a.wait_ge(ztr, n + 1)
                        if g >= 2 or k.past(1):
                            a.wait_ge(zm, n - 1)
                        a.copy(zt[:, g % 2, :], pz[g % 2][:, :]).then_inc(ztc, 1)
                        if g in YAT:
                            i = YAT.index(g)
                            a.wait_ge(yq, k.t * 4 + i + 1)
                            if k.past(1):
                                a.wait_ge(vd, (k.t - 1) * VD + (1 if i < 2 else 2))
                            a.copy(yt[:, i * 512:(i + 1) * 512], pyt[:, :]).then_inc(yqc, 1)
                    a.wait_ge(zm, (k.t + 1) * NG)
                    if k.past(R):
                        a.wait_ge(sct[k.slot(R)], k.lap(R) * 16)
                    a.copy(ub[:, k.slot(R), 0:S], po[:, 0:S]).then_inc(uc, 1)
                sweep(a, ECOL, [(0, copy_x), (1, copy_y), (L_XA, copy_xa, 1), (L_BIG, big, 1)], R)

            @block.vector
            def _(v):
                v.memset(s1[:, :], 0.0).then_inc(init, 1)
                v.memset(tot[:, R - 1, :], 0.0).then_inc(init, 1)
                v.wait_ge(init, 2)

                def accumulate(k):
                    r, d = k.slot(R), k.slot(2)
                    c = Chain(v, acc, AC, k)
                    if k.past(R):
                        v.wait_ge(vd, (k.t - R + 1) * VD)
                        v.wait_ge(xat, k.t - R + 1)
                    if k.is_fix():
                        v.wait_ge(fx, 1)
                        v.wait_ge(acc, ECOL * AC)
                        v.tensor_tensor(tot[:, r, :], s1[:, :], pm1[:, 0:F], ALU.add).then_inc(acc, AC)
                        return
                    v.wait_ge(mpc, k.t + 1)
                    edge = bass.ds(k.t, 1)
                    e0 = q.es[:, edge, Y0]
                    e1 = q.es[:, edge, Y1:Y1 + 3].rearrange("p a c -> p (a c)")
                    sc = mp[:, d, 0:F]
                    vc = mp[:, d, F:544].rearrange("p (c k) -> p c k", c=3)
                    ta, tb, tc = tmp[:, d, 0:192], tmp[:, d, 192:288], tmp[:, d, 288:352]
                    gs, gv = mg[:, d, 0:S], mg[:, d, S:F]
                    g3 = gv.rearrange("p (c u) -> p c u", c=3)
                    tb3 = tb.rearrange("p (c u) -> p c u", c=3)
                    c(v.scalar_tensor_tensor(gs, sc[:, 0:64], e0, sc[:, 64:128], ALU.mult, ALU.add))
                    c(v.tensor_tensor(ta.rearrange("p (c u) -> p c u", c=3), vc[:, :, 0:64], bc(e1, 2, 64), ALU.mult))
                    c(v.scalar_tensor_tensor(g3, vc[:, :, 64:96], e0, vc[:, :, 96:128], ALU.mult, ALU.add))
                    c(v.tensor_tensor(tb3, bc(sc[:, 128:160], 1, 3), bc(e1, 2, V), ALU.mult))
                    c.wait(2)
                    c(v.tensor_reduce(tc, ta.rearrange("p (c u) -> p u c", c=3), AX, ALU.add))
                    c.wait(4)
                    c(v.tensor_tensor(gv, gv, tb, ALU.add))
                    c.wait(5)
                    c(v.tensor_tensor(gs, gs, tc, ALU.add))
                    c.wait()
                    c(v.scalar_tensor_tensor(tot[:, r, :], tot[:, (r - 1) % R, :], q.es[:, edge, SAME], mg[:, d, :],
                                             ALU.mult, ALU.add))
                    c.wait()
                    c(v.tensor_scalar(cap[:, :], tot[:, r, :], q.es[:, edge, FEND], None, ALU.mult))
                    c.wait()
                    c(v.tensor_tensor(s1[:, :], s1[:, :], cap[:, :], ALU.add))

                def outer(k):
                    r, d = k.slot(R), k.slot(2)
                    c = Chain(v, zp, ZP, k)
                    v.wait_ge(gas[r], (k.lap(R) + 1) * 16)
                    v.wait_ge(acc, (k.t + 1) * AC)
                    if k.past(2):
                        v.wait_ge(ztr, (k.t - 1) * NG)
                    c(v.tensor_tensor(z[:, d, 0:S * S].rearrange("p (u v) -> p u v", u=S), bc(xs[:, r, 0:S], 2, S),
                                      bc(tot[:, r, 0:S], 1, S), ALU.mult))
                    xv = xs[:, r, S:F].rearrange("p (c u) -> p c u", c=3)
                    av = tot[:, r, S:F].rearrange("p (c u) -> p c u", c=3)
                    c(v.tensor_tensor(z[:, d, S * S:].rearrange("p (c u v) -> p c u v", c=3, u=V), bc(xv, 3, V),
                                      bc(av, 2, V), ALU.mult))

                def vectors(k):
                    r = k.slot(R)
                    c = Chain(v, vd, VD, k)
                    if k.past(R):
                        v.wait_ge(sct[r], k.lap(R) * 16)
                    if k.past(1):
                        v.wait_ge(vd, k.t * VD)
                    for i, src in enumerate((tot, xs)):
                        v.wait_ge(yqc, k.t * 4 + 2 * i + 2)
                        half = yt[:, i * HALF:(i + 1) * HALF].rearrange("p (q w) -> p q w", w=V)
                        c(v.tensor_tensor(pr[:, :, i * V:(i + 1) * V, :], bc(half, 1, 3),
                                          bc(src[:, r, S:F].rearrange("p (c u) -> p c u", c=3), 3, V), ALU.mult))
                    c.wait()
                    c(v.tensor_reduce(ub[:, r, S:F].rearrange("p (c w) -> p c w", c=3),
                                      pr[:, :, :, :].rearrange("p c q w -> p c w q"), AX, ALU.add))
                sweep(v, ECOL, [(L_ACC, accumulate, 1), (L_Z, outer, 1), (L_VEC, vectors, 1)], R)


def build(nc, io, out):
    with ExitStack() as ctx:
        sb, ps, sem = scope(nc, ctx, "g")
        m = Mem()
        m.ident, m.ones, m.before, m.after = (sb(n, [P, P]) for n in ("ident", "ones", "before", "after"))
        m.iota_i, m.iota, m.eps = sb("iotai", [P, HI], I32), sb("iota", [P, HI]), sb("eps", [P, 1])
        m.edge = sb("edge", [P, ECOL, ROW])
        m.src, m.dst = Mem(), Mem()
        for q, n in ((m.src, "s"), (m.dst, "d")):
            q.attr_y0, q.attr_y1 = A4, A4 + 1
            q.attr, q.es = sb(f"attr{n}", [P, ECOL, ROW]), sb(f"es{n}", [P, ECOL, ESW])
            q.ends, q.first_run, q.last_run = sb(f"ends{n}", [P, 2]), sb(f"fr{n}", [P, ECOL]), sb(f"lr{n}", [P, ECOL])
            q.fix_id, q.first_id, q.carry = sb(f"fix{n}", [P, 1], I32), sb(f"first{n}", [P, 1], I32), sb(f"carry{n}", [P, P])

        def dram(name, shape):
            return nc.dram_tensor(name, shape, F32, kind="Internal").ap()
        m.by_src, m.by_dst = dram("by_src", [EROWS, ROW]), dram("by_dst", [EROWS, ROW])
        m.agg_src, m.agg_dst = dram("agg_src", [NROWS, F]), dram("agg_dst", [NROWS, F])
        x1, x2, x3 = (dram(f"x{k}", [NROWS, F + 1]) for k in (1, 2, 3))
        setup(nc, io, m)
        sort(nc, m)
        segments(nc, m)
        edge_layer(nc, m, io, 0, io.x, m.src, m.agg_src)
        node_layer(nc, m, io, 0, io.x, m.agg_src, x1)
        edge_layer(nc, m, io, 1, x1, m.dst, m.agg_dst)
        node_layer(nc, m, io, 1, x1, m.agg_dst, x2)
        with ExitStack() as heads:
            sb2, _, _ = scope(nc, heads, "at")
            logits, ex = sb2("logits", [P, 4, ECOL]), sb2("ex", [P, ECOL, 4])
            hid = dram("hid", [EROWS, F])
            attention_messages(nc, m, io, x2, m.dst, logits, hid)
            attention_weights(nc, m, m.dst, logits, ex)
            attention_sums(nc, m, io, m.dst, ex, hid, m.agg_dst)
        node_layer(nc, m, io, 2, x2, m.agg_dst, x3)
        bilinear_layer(nc, m, io, x3, m.src, m.agg_src)
        node_layer(nc, m, io, 3, x3, m.agg_src, out)


WEIGHTS = ["L0_gnn_W1_0", "L0_gnn_W1_1", "L0_gnn_Wfc1", "L0_gnn_Wfc2", "L0_gnn_Wfc3", "L0_gnn_W2_0", "L0_gnn_W2_1",
           "L0_gnn_Wsc0", "L0_gnn_Wsc1", "L0_gnn_g0", "L0_gnn_g1", "L1_gnn_W_si0", "L1_gnn_W_si1", "L1_gnn_W_l1_0",
           "L1_gnn_W_l1_1", "L1_gnn_W_l2_00", "L1_gnn_W_l2_10", "L1_gnn_W_l2_01", "L1_gnn_W_l2_11", "L1_gnn_W_fc1",
           "L1_gnn_W_fc2", "L2_gnn_gamma_s", "L2_gnn_beta_s", "L2_gnn_gamma_v", "L2_gnn_Ws_src", "L2_gnn_Wv_src",
           "L2_gnn_Ws_dst", "L2_gnn_Wv_dst", "L2_gnn_W_rbf", "L2_gnn_W_alpha", "L2_gnn_alpha_dot", "L2_gnn_Ws_val",
           "L2_gnn_Wv_val", "L2_gnn_Wg", "L2_gnn_w2_ss", "L2_gnn_w2_sv", "L2_gnn_w2_vs", "L2_gnn_w2_vv0",
           "L2_gnn_w2_vv1", "L2_gnn_Ws_vlin", "L2_gnn_Wv_vlin", "L2_gnn_Wps", "L2_gnn_Wpv", "L3_gnn_wm000",
           "L3_gnn_wm011", "L3_gnn_wm101", "L3_gnn_wm110", "L3_gnn_lm0", "L3_gnn_lm1", "L3_gnn_wu000", "L3_gnn_wu011",
           "L3_gnn_wu101", "L3_gnn_wu110", "L3_gnn_lu0", "L3_gnn_lu1"]


def kernel(**inputs):
    import concourse.bacc as bacc
    from concourse.bass_utils import run_bass_kernel_spmd as run

    nc = bacc.Bacc("TRN2", target_bir_lowering=False, num_devices=1)
    arrays, io = {}, Mem()

    def given(name, a):
        arrays[name] = np.ascontiguousarray(a)
        return nc.dram_tensor(name, a.shape, mybir.dt.from_np(a.dtype), kind="ExternalInput").ap()

    x = np.asarray(inputs["x"])
    rows = np.zeros((NROWS, F + 1), np.float32)
    rows[:NODES, :S] = x[:, :S]
    rows[:NODES, S:F] = x[:, S:].reshape(NODES, V, 3).transpose(0, 2, 1).reshape(NODES, 3 * V)
    rows[:NODES, F:] = inputs["node_vec1"]
    eidx = np.full((EROWS, 2), DUMMY, np.int32)
    eidx[:EDGES, 0], eidx[:EDGES, 1] = inputs["src"], inputs["dst"]
    eattr = np.zeros((EROWS, ROW - 2), np.float32)
    eattr[:EDGES] = np.concatenate([np.asarray(inputs[f"edge_attr_{n}"]) for n in (4, 8, 10, 16)], axis=1)
    io.x, io.eidx, io.eattr = given("x_rows", rows), given("eidx", eidx), given("eattr", eattr)
    io.w = {n: given(n, np.asarray(inputs[n])) for n in WEIGHTS}
    out = nc.dram_tensor("out", [NROWS, F], F32, kind="ExternalOutput").ap()
    build(nc, io, out)
    got = run(nc, [arrays], core_ids=[0]).results[0]["out"][:NODES]
    back = np.empty_like(got)
    back[:, :S] = got[:, :S]
    back[:, S:] = got[:, S:].reshape(NODES, 3, V).transpose(0, 2, 1).reshape(NODES, 3 * V)
    return back
```

```python
from contextlib import ExitStack

import numpy as np

import concourse.bass as bass
from concourse import mybir

F32 = mybir.dt.float32
I32 = mybir.dt.int32
ALU = mybir.AluOpType
ACT = mybir.ActivationFunctionType
AX = mybir.AxisListType.X

P = 128
NODES, EDGES = 25000, 12500
F = 160
S, V = 64, 32
NCOL = -(-NODES // P)
NROWS = NCOL * P
ECOL = -(-EDGES // P)
EROWS = ECOL * P
DUMMY = NROWS - 1
HI = -(-NROWS // P)
ROW = 40
A4, A8, A10, A16 = 2, 6, 14, 24
SKIP = 1 << 20
U = 4
GRP = 4
NGRP = NCOL // GRP
EPS = 1e-5
R3, R2 = float(1 / np.sqrt(3.0)), float(1 / np.sqrt(2.0))
Y0, Y1, SAME, FEND, GIDX, GIDX2, WIDX, ESW = 0, 1, 6, 7, 8, 9, 10, 12


class Tile:

    def __init__(self, base, i=None, unroll=U):
        self.base, self.i, self.unroll = base, i, unroll

    def is_fix(self):
        return self.i is None and self.base == ECOL

    @property
    def t(self):
        return self.base if self.i is None else self.i * self.unroll + self.base

    def slot(self, ring):
        return self.base % ring

    def lap(self, ring):
        n = self.base // ring
        return n if self.i is None else self.i * (self.unroll // ring) + n

    def past(self, n):
        return self.base >= n


def sweep(eng, n, stages, depth, unroll=U):
    last = max(st[0] for st in stages)
    lead = last + depth
    lead += (n - lead) % unroll

    def step(s, i=None):
        for lag, fn, *more in stages:
            if i is not None or 0 <= s - lag < n + sum(more):
                fn(Tile(s - lag, i, unroll))

    for s in range(min(lead, n)):
        step(s)
    if n > lead:
        with eng.Fori(0, (n - lead) // unroll) as i:
            for u in range(unroll):
                step(lead + u, i)
    for s in range(n, n + last + max(sum(st[2:]) for st in stages)):
        step(s)


class Chain:

    def __init__(self, eng, sem, per, tile):
        self.eng, self.sem, self.per, self.tile, self.n = eng, sem, per, tile, 0

    def __call__(self, ins):
        ins.then_inc(self.sem, 1)
        self.n += 1

    def wait(self, n=None):
        self.eng.wait_ge(self.sem, self.tile.t * self.per + (self.n if n is None else n))


class Shifted:

    def __init__(self, chain, first):
        self.chain, self.first = chain, first

    @property
    def n(self):
        return self.chain.n - self.first

    def __call__(self, ins):
        self.chain(ins)

    def wait(self, n=None):
        self.chain.wait(None if n is None else n + self.first)


class Static:

    def __init__(self, eng, sem):
        self.eng, self.sem, self.n = eng, sem, 0

    def __call__(self, ins, wait=True):
        ins.then_inc(self.sem, 1)
        self.n += 1
        if wait:
            self.eng.wait_ge(self.sem, self.n)


class Mem:
    pass


def scope(nc, ctx, tag):
    sems = []

    def clear():
        if sems:
            nc.clear_and_free_semaphores(sems)
            nc.all_engine_barrier()
    ctx.callback(clear)

    def sb(name, shape, dt=F32):
        return ctx.enter_context(nc.sbuf_tensor(f"{tag}_{name}", shape, dt))

    def ps(name, shape=(P, 512), dt=F32):
        return ctx.enter_context(nc.psum_tensor(f"{tag}_{name}", list(shape), dt))

    def sem(name):
        sems.append(nc.alloc_semaphore(name=f"{tag}_{name}"))
        return sems[-1]

    return sb, ps, sem


def setup(nc, io, m, zero, zeroed):
    with ExitStack() as ctx:
        sb, ps, sem = scope(nc, ctx, "set")
        loaded, made, filled = sem("loaded"), sem("made"), sem("filled")
        block = ctx.enter_context(nc.Block())

        @block.sync
        def _(sp):
            sp.dma_start(m.edge[:, :, 0:2].bitcast(I32), io.eidx.rearrange("(p j) c -> p j c", p=P)).then_inc(loaded, 16)
            sp.dma_start(m.edge[:, :, 2:ROW], io.eattr.rearrange("(p j) c -> p j c", p=P)).then_inc(loaded, 16)
            sp.wait_ge(filled, 1)
            for agg in (m.agg_src, m.agg_dst):
                a = agg.rearrange("(p j) f -> p (j f)", p=P)
                w = NCOL // 4 * F
                for k in range(4):
                    sp.dma_start(a[:, k * w:(k + 1) * w], zero[:, :]).then_inc(zeroed, 16)
            sp.wait_ge(loaded, 32)

        @block.vector
        def _(v):
            v.memset(zero[:, :], 0.0).then_inc(filled, 1)
            v.memset(m.eps[:, :], EPS)

        @block.gpsimd
        def _(g):
            c = Static(g, made)
            c(g.memset(m.ones[:, :], 1.0))
            c(g.affine_select(out=m.ident[:, :], in_=m.ones[:, :], compare_op=ALU.is_equal, fill=0.0, base=0,
                              pattern=[[-1, P]], channel_multiplier=1))
            c(g.affine_select(out=m.before[:, :], in_=m.ones[:, :], compare_op=ALU.is_gt, fill=0.0, base=0,
                              pattern=[[-1, P]], channel_multiplier=1))
            c(g.affine_select(out=m.after[:, :], in_=m.ones[:, :], compare_op=ALU.is_gt, fill=0.0, base=0,
                              pattern=[[1, P]], channel_multiplier=-1))
            c(g.iota(m.iota_i[:, :], pattern=[[1, HI]], base=0, channel_multiplier=0))
            c(g.tensor_copy(m.iota[:, :], m.iota_i[:, :]))


def sort(nc, m, zeroed):
    with ExitStack() as ctx:
        sb, ps, sem = scope(nc, ctx, "sort")
        ki = sb("ki", [P, 2, ECOL], I32)
        loi = sb("loi", [P, 2, ECOL], I32)
        hii = sb("hii", [P, 2, ECOL], I32)
        key, lo, hi = sb("key", [P, 2, ECOL]), sb("lo", [P, 2, ECOL]), sb("hi", [P, 2, ECOL])
        dig, dig_v, pre, prp, pra, hist_done = (sem(n) for n in ("dig", "digv", "pre", "prp", "pra", "hist"))
        RO = 4
        ohl, ohh = sb("ohl", [P, RO, 2, P]), sb("ohh", [P, RO, 2, HI])
        count = [ps(f"count{o}") for o in range(2)]
        with nc.Block() as block:
            @block.vector
            def _(v):
                c = Static(v, dig)
                c(v.tensor_copy(ki[:, :, :], m.edge[:, :, 0:2].bitcast(I32).rearrange("p j o -> p o j")))
                c(v.tensor_single_scalar(loi[:, :, :], ki[:, :, :], P - 1, ALU.bitwise_and), wait=False)
                c(v.tensor_single_scalar(hii[:, :, :], ki[:, :, :], 7, ALU.logical_shift_right))
                c(v.tensor_copy(key[:, :, :], ki[:, :, :]), wait=False)
                c(v.tensor_copy(lo[:, :, :], loi[:, :, :]), wait=False)
                c(v.tensor_copy(hi[:, :, :], hii[:, :, :]))

                def onehot(k):
                    r = k.slot(2)
                    if k.past(2):
                        v.wait_ge(hist_done, k.t - 1)
                    for o in range(2):
                        v.tensor_scalar(ohl[:, r, o, :], m.iota[:, 0:P], lo[:, o, bass.ds(k.t, 1)], None, ALU.is_equal)
                        ins = v.tensor_scalar(ohh[:, r, o, :], m.iota[:, :], hi[:, o, bass.ds(k.t, 1)], None, ALU.is_equal)
                    ins.then_inc(dig_v, 1)
                sweep(v, ECOL, [(0, onehot)], 2)

            @block.tensor
            def _(pe):
                def hist(k):
                    r = k.slot(2)
                    pe.wait_ge(dig_v, k.t + 1)
                    for o in range(2):
                        first = k.i is None and k.base == 0
                        ins = pe.matmul(count[o][:, 0:HI], ohl[:, r, o, :], ohh[:, r, o, :], start=first, stop=True,
                                        skip_group_check=True)
                    ins.then_inc(hist_done, 1)
                sweep(pe, ECOL, [(0, hist)], 2)

        pc = [ps(f"prefix{o}") for o in range(2)]
        hsb, csum, excl = sb("hsb", [P, 2, HI]), sb("csum", [P, 2, HI]), sb("excl", [P, 2, HI])
        with nc.Block() as block:
            @block.vector
            def _(v):
                c = Static(v, pre)
                for o in range(2):
                    c(v.tensor_copy(hsb[:, o, :], count[o][:, 0:HI]), wait=False)
                v.wait_ge(prp, 2)
                for o in range(2):
                    c(v.tensor_copy(csum[:, o, :], pc[o][:, HI:2 * HI]))
                    c(v.tensor_tensor_scan(excl[:, o, :], csum[:, o, :], csum[:, o, :], 0.0, ALU.add, ALU.max))
                    c(v.tensor_tensor(excl[:, o, :], excl[:, o, :], csum[:, o, :], ALU.subtract))
                    c(v.tensor_tensor(excl[:, o, :], excl[:, o, :], pc[o][:, 0:HI], ALU.add))

            @block.tensor
            def _(pe):
                pe.wait_ge(pre, 2)
                for o in range(2):
                    pe.matmul(pc[o][:, 0:HI], m.after[:, :], hsb[:, o, :], start=True, stop=True)
                    pe.matmul(pc[o][:, HI:2 * HI], m.ones[:, :], hsb[:, o, :], start=True, stop=True).then_inc(prp, 1)

        R = 2
        pt = [ps(f"pt{r}") for r in range(R)]
        pg = [ps(f"pg{r}") for r in range(R)]
        tsb = sb("tsb", [P, R, 2, 2, P])
        hcur = sb("hcur", [P, R, 2, HI])
        junk, junk2 = sb("junk", [P, HI]), sb("junk2", [P, P])
        part = sb("part", [P, R, 2, 2])
        rankf = sb("rankf", [P, R, 2])
        rank = sb("rank", [P, 4, 2], I32)
        rowr = sb("rowr", [P, 4, ROW])
        kb = sb("kb", [P, RO, 2, P])
        oh, tr, trc, snap, look, rk, rowc, upd = (sem(n) for n in ("oh", "tr", "trc", "snap", "look", "rk", "rowc", "upd"))
        gate = sem("gate")
        sc = [sem(f"sc{r}") for r in range(4)]
        RK = 7

        with nc.Block() as block:
            @block.sync
            def _(sp):
                sp.wait_ge(zeroed, 8 * 16)

            @block.vector
            def _(v):
                def onehot(k):
                    r = k.slot(RO)
                    if k.past(RO):
                        v.wait_ge(upd, k.t - RO + 1)
                        v.wait_ge(rk, (k.t - RO + 1) * RK)
                    for o in range(2):
                        v.tensor_scalar(ohl[:, r, o, :], m.iota[:, 0:P], lo[:, o, bass.ds(k.t, 1)], None, ALU.is_equal)
                        v.tensor_scalar(ohh[:, r, o, :], m.iota[:, :], hi[:, o, bass.ds(k.t, 1)], None, ALU.is_equal)
                        ins = v.tensor_scalar(kb[:, r, o, :], m.ones[:, :], key[:, o, bass.ds(k.t, 1)], None, ALU.mult)
                    ins.then_inc(oh, 1)

                def ranks(k):
                    r = k.slot(R)
                    c = Chain(v, rk, RK, k)
                    v.wait_ge(look, k.t + 1)
                    for o in range(2):
                        c(v.scalar_tensor_tensor(junk2[:, :], tsb[:, r, o, 1, :], key[:, o, bass.ds(k.t, 1)],
                                                 m.before[:, :], ALU.is_equal, ALU.mult,
                                                 accum_out=part[:, r, o, 0:1]))
                        c.wait()
                        c(v.tensor_tensor_reduce(junk[:, :], pg[r][:, o * HI:(o + 1) * HI], ohh[:, k.slot(RO), o, :], 1.0, 0.0,
                                                 ALU.mult, ALU.add, part[:, r, o, 1:2]))
                        c.wait()
                    c(v.tensor_tensor(rankf[:, r, :], part[:, r, :, 0], part[:, r, :, 1], ALU.add))
                    c.wait()
                    if k.past(4):
                        v.wait_ge(sc[k.slot(4)], k.lap(4) * 32)
                    c(v.tensor_copy(rank[:, k.slot(4), :], rankf[:, r, :]))
                    c(v.tensor_copy(rowr[:, k.slot(4), :], m.edge[:, bass.ds(k.t, 1), :]))
                sweep(v, ECOL, [(0, onehot), (2, ranks)], 4)

            @block.scalar
            def _(a):
                def copies(k):
                    r = k.slot(R)
                    a.wait_ge(tr, k.t + 1)
                    if k.past(R):
                        a.wait_ge(rk, (k.t - 1) * RK)
                        a.wait_ge(look, k.t - 1)
                    a.copy(tsb[:, r, :, :, :].rearrange("p a b c -> p (a b c)"), pt[r][:, :]).then_inc(trc, 1)
                    if k.past(1):
                        a.wait_ge(upd, k.t)
                    for o in range(2):
                        ins = a.copy(hcur[:, r, o, :], count[o][:, 0:HI])
                    ins.then_inc(snap, 1)
                a.wait_ge(gate, 1)
                sweep(a, ECOL, [(0, copies)], 2)

            @block.tensor
            def _(pe):
                for o in range(2):
                    ins = pe.matmul(count[o][:, 0:HI], m.ident[:, :], excl[:, o, :], start=True, stop=True,
                                    skip_group_check=True)
                ins.then_inc(gate, 1)

                def turn(k):
                    r = k.slot(R)
                    pe.wait_ge(oh, k.t + 1)
                    if k.past(R):
                        pe.wait_ge(trc, k.t - 1)
                    for o in range(2):
                        pe.transpose(pt[r][:, 2 * o * P:(2 * o + 1) * P], ohl[:, k.slot(RO), o, :], m.ident[:, :])
                        ins = pe.transpose(pt[r][:, (2 * o + 1) * P:(2 * o + 2) * P], kb[:, k.slot(RO), o, :], m.ident[:, :])
                    ins.then_inc(tr, 1)

                def lookup(k):
                    r = k.slot(R)
                    pe.wait_ge(trc, k.t + 1)
                    pe.wait_ge(snap, k.t + 1)
                    if k.past(R):
                        pe.wait_ge(rk, (k.t - 1) * RK)
                    for o in range(2):
                        ins = pe.matmul(count[o][:, 0:HI], ohl[:, k.slot(RO), o, :], ohh[:, k.slot(RO), o, :], start=False,
                                        stop=True, skip_group_check=True)
                    ins.then_inc(upd, 1)
                    for o in range(2):
                        ins = pe.matmul(pg[r][:, o * HI:(o + 1) * HI], tsb[:, r, o, 0, :], hcur[:, r, o, :],
                                        start=True, stop=True)
                    ins.then_inc(look, 1)
                sweep(pe, ECOL, [(1, lookup), (0, turn)], 4)

            @block.gpsimd
            def _(g):
                last_row = g.to_reg(EROWS - 1)

                def scatter(k):
                    r = k.slot(4)
                    g.wait_ge(rk, (k.t + 1) * RK)
                    g.sem_inc(rowc, 1)
                    for o, table in enumerate((m.by_src, m.by_dst)):
                        g.indirect_dma_start(table, bass.IndirectOffsetOnAxis(ap=rank[:, r, o:o + 1], axis=0),
                                             rowr[:, r, :], None, bounds_check=last_row,
                                             oob_is_err=False).then_inc(sc[r], 16)
                sweep(g, ECOL, [(0, scatter)], 4)
                for r in range(4):
                    g.wait_ge(sc[r], 32 * len(range(r, ECOL, 4)))


def segments(nc, m):
    for table, key_col, gather_col, q in ((m.by_src, 0, 1, m.src), (m.by_dst, 1, 0, m.dst)):
        with ExitStack() as ctx:
            sb, ps, sem = scope(nc, ctx, f"seg{key_col}")
            ld, ch, ach, mm = sem("ld"), sem("ch"), sem("ach"), sem("mm")
            nb = sb("nb", [P, 2, 2], I32)
            kf, nbf = sb("kf", [P, ECOL]), sb("nbf", [P, 2])
            end, fr, tmp, wid = sb("end", [P, ECOL]), sb("fr", [P, ECOL]), sb("tmp", [P, ECOL]), sb("wid", [P, ECOL])
            one = sb("one", [P, 8])
            diag = sb("diag", [P, P])
            row = ps("row")
            block = ctx.enter_context(nc.Block())
            flat = table.rearrange("(p j) c -> p j c", p=P)
            es = q.es

            @block.sync
            def _(sp):
                sp.dma_start(q.attr[:, :, :], flat).then_inc(ld, 16)
                sp.wait_ge(ch, 1)
                sp.dma_start(nb[1:P, 0, :], flat[0:P - 1, ECOL - 1, 0:2].bitcast(I32)).then_inc(ld, 16)
                sp.dma_start(nb[0:P - 1, 1, :], flat[1:P, 0, 0:2].bitcast(I32)).then_inc(ld, 16)

            @block.vector
            def _(v):
                c = Static(v, ch)
                c(v.memset(nb[:, :, :], -1))
                v.wait_ge(ld, 48)
                c(v.tensor_copy(kf[:, :], q.attr[:, :, key_col].bitcast(I32)), wait=False)
                c(v.tensor_copy(nbf[:, :], nb[:, :, key_col]), wait=False)
                y = q.attr[:, :, q.attr_y0:q.attr_y0 + 1]
                for k, a in ((Y0, q.attr_y0), (Y1, q.attr_y1), (Y1 + 1, q.attr_y1 + 1), (Y1 + 2, q.attr_y1 + 2),
                             (Y1 + 3, q.attr_y1), (Y1 + 4, q.attr_y1 + 1),
                             (GIDX, gather_col), (GIDX2, key_col)):
                    c(v.tensor_copy(es[:, :, k].bitcast(I32), q.attr[:, :, a].bitcast(I32)), wait=False)
                c(v.memset(es[:, 0, SAME:SAME + 1], 0.0))
                c(v.tensor_tensor(es[:, 1:ECOL, SAME], kf[:, 1:ECOL], kf[:, 0:ECOL - 1], ALU.is_equal), wait=False)
                c(v.tensor_tensor(end[:, 0:ECOL - 1], kf[:, 1:ECOL], kf[:, 0:ECOL - 1], ALU.not_equal), wait=False)
                c(v.tensor_tensor(end[:, ECOL - 1:ECOL], kf[:, ECOL - 1:ECOL], nbf[:, 1:2], ALU.not_equal), wait=False)
                c(v.tensor_scalar(fr[:, :], kf[:, :], kf[:, 0:1], None, ALU.is_equal), wait=False)
                c(v.tensor_tensor(one[:, 0:1], kf[:, 0:1], nbf[:, 0:1], ALU.is_equal))
                c(v.tensor_tensor(es[:, :, FEND], fr[:, :], end[:, :], ALU.mult))
                c(v.tensor_reduce(one[:, 1:2], es[:, :, FEND], AX, ALU.max))
                c(v.tensor_scalar(tmp[:, :], es[:, :, FEND], one[:, 0:1], None, ALU.mult))
                c(v.tensor_tensor(tmp[:, :], end[:, :], tmp[:, :], ALU.subtract))
                c(v.tensor_scalar(tmp[:, :], tmp[:, :], float(-SKIP), float(SKIP), ALU.mult, ALU.add))
                c(v.tensor_tensor(wid[:, :], kf[:, :], tmp[:, :], ALU.add))
                c(v.tensor_copy(es[:, :, WIDX].bitcast(I32), wid[:, :]), wait=False)
                c(v.tensor_tensor(one[:, 2:3], one[:, 0:1], one[:, 1:2], ALU.mult))
                c(v.tensor_scalar(one[:, 3:4], one[:, 2:3], float(-SKIP), float(SKIP), ALU.mult, ALU.add))
                c(v.tensor_tensor(one[:, 4:5], kf[:, 0:1], one[:, 3:4], ALU.add))
                c(v.tensor_copy(q.fix_id[:, 0:1], one[:, 4:5]), wait=False)
                c(v.tensor_copy(q.ends[:, 0:1], kf[:, 0:1]), wait=False)
                c(v.tensor_copy(q.ends[:, 1:2], kf[:, ECOL - 1:ECOL]), wait=False)
                c(v.tensor_scalar(q.last_run[:, :], kf[:, :], kf[:, ECOL - 1:ECOL], None, ALU.is_equal), wait=False)
                c(v.tensor_copy(q.first_run[:, :], fr[:, :]), wait=False)
                c(v.tensor_copy(q.first_id[:, 0:1], q.attr[:, 0, key_col:key_col + 1].bitcast(I32)), wait=False)
                c(v.tensor_scalar(diag[:, :], m.ident[:, :], kf[:, 0:1], None, ALU.mult))
                v.sem_inc(ach, 1)
                v.wait_ge(mm, 1)
                c(v.scalar_tensor_tensor(q.carry[:, :], row[:, 0:P], kf[:, ECOL - 1:ECOL], m.after[:, :],
                                         ALU.is_equal, ALU.mult), wait=False)

            @block.tensor
            def _(pe):
                pe.wait_ge(ach, 1)
                pe.matmul(row[:, 0:P], m.ones[:, :], diag[:, :], start=True, stop=True).then_inc(mm, 1)


def bc(ap, at, n):
    ap = ap.unsqueeze(at)
    return ap.broadcast_to([n if d == at else s for d, s in enumerate(ap.shape)])


def chain_loads(eng, sem, pairs):
    for dst, src in pairs:
        eng.dma_start(dst, src).then_inc(sem, 16)
    eng.wait_ge(sem, 16 * len(pairs))


def block_loads(wb, w2, ws, wv):
    return [(wb[0:64, 0:64], ws), (wb[64:96, 64:96], wv), (wb[96:128, 96:128], wv), (w2[0:32, 0:32], wv)]


CG_OPS, CG_OPS_CROSS = 7, 11


def cg(v, c, w, s, vec, y0, y1, dot, mid, tmp, cross):
    vw = 128 if cross else 96
    mv = mid[:, 96:96 + 3 * vw].rearrange("p (c u) -> p c u", c=3)
    t0, t1, t2, t3 = (tmp[:, i * 96:(i + 1) * 96] for i in range(4))
    vec3 = vec[:, 0:96].rearrange("p (c u) -> p c u", c=3)

    def c3(ap):
        return ap.rearrange("p (c u) -> p c u", c=3)

    c(v.tensor_tensor(c3(t0), vec3, bc(y1(0, 3), 2, V), ALU.mult))
    if cross:
        c(v.tensor_tensor(c3(t2), c3(vec[:, 32:128]), bc(y1(2, 5), 2, V), ALU.mult))
        c(v.tensor_tensor(c3(t3), c3(vec[:, 64:160]), bc(y1(1, 4), 2, V), ALU.mult))
    n_cross = c.n
    c(v.scalar_tensor_tensor(mid[:, 0:64], w[:, 0:64], y0, s, ALU.mult, ALU.mult))
    c(v.tensor_tensor(tmp[:, 416:480], w[:, 64:128], s, ALU.mult))
    n_ws = c.n
    c(v.scalar_tensor_tensor(mv[:, :, 64:96], vec3, y0, bc(w[:, 128:160], 1, 3), ALU.mult, ALU.mult))
    c.wait(1)
    c(v.tensor_reduce(tmp[:, 384:416], t0.rearrange("p (c u) -> p u c", c=3), AX, ALU.add))
    n_dot = c.n
    if cross:
        c.wait(n_cross)
        c(v.tensor_tensor(t1, t2, t3, ALU.subtract))
    n_sub = c.n
    c.wait(n_ws)
    c(v.tensor_tensor(mv[:, :, 0:64], bc(tmp[:, 416:480], 1, 3), bc(y1(0, 3), 2, 64), ALU.mult))
    c.wait(n_dot)
    c(v.scalar_tensor_tensor(mid[:, 64:96], tmp[:, 384:416], dot, w[:, 160:192], ALU.mult, ALU.mult))
    if cross:
        c.wait(n_sub)
        c(v.scalar_tensor_tensor(mv[:, :, 96:128], c3(t1), R2, bc(w[:, 192:224], 1, 3), ALU.mult, ALU.mult))


def edge_layer(nc, m, io, layer, x, q, agg):
    cross = layer == 0
    tag = f"e{layer}"
    nb, a_col = ((8, A8), (10, A10))[layer]
    nh = (64, 100)[layer]
    wn, vw = (224, 128) if cross else (192, 96)
    cgn = CG_OPS_CROSS if cross else CG_OPS
    c1 = float(1 / np.sqrt(8.0)) if layer == 0 else float(np.sqrt(2.0) / np.sqrt(10.0))
    with ExitStack() as ctx:
        sb, ps, sem = scope(nc, ctx, tag)
        wb, w2 = sb("wb", [P, P]), sb("w2", [V, V])
        FE = F + 1 - P
        KT = FE + nb
        f1, f2, f3 = sb("f1", [KT, nh]), sb("f2", [64, 64]), sb("f3", [nh, wn])
        ws, wv = sb("ws", [96, 64]), sb("wv", [vw, V])
        wl, wz, wsc = sem("wl"), sem("wz"), sem("wsc")
        w = io.w
        if layer == 0:
            loads = block_loads(wb, w2, w["L0_gnn_W1_0"], w["L0_gnn_W1_1"]) + [
                (f1[FE:KT, :], w["L0_gnn_Wfc1"]), (f2[:, :], w["L0_gnn_Wfc2"]), (f3[:, :], w["L0_gnn_Wfc3"]),
                (ws[:, :], w["L0_gnn_W2_0"]), (wv[:, :], w["L0_gnn_W2_1"])]
            last, cs, cv = f3, 1 / (4 * np.sqrt(96.0)), 1 / (4 * np.sqrt(128.0))
            cl = 1 / 8.0
        else:
            loads = block_loads(wb, w2, w["L1_gnn_W_l1_0"], w["L1_gnn_W_l1_1"]) + [
                (f1[FE:KT, :], w["L1_gnn_W_fc1"]), (f3[:, :], w["L1_gnn_W_fc2"]),
                (ws[0:64, :], w["L1_gnn_W_l2_00"]), (ws[64:96, :], w["L1_gnn_W_l2_10"]),
                (wv[0:64, :], w["L1_gnn_W_l2_01"]), (wv[64:96, :], w["L1_gnn_W_l2_11"])]
            last, cs, cv = f3, 0.5 / (4 * np.sqrt(96.0)), 0.5 / (4 * np.sqrt(96.0))
            cl = 1 / 10.0
        with nc.Block() as block:
            @block.vector
            def _(v):
                v.memset(wb[:, :], 0.0).then_inc(wz, 1)
                v.memset(f1[:, :], 0.0).then_inc(wz, 1)

            @block.sync
            def _(sp):
                sp.wait_ge(wz, 2)
                chain_loads(sp, wl, loads)
                sp.sem_inc(wz, 1)

            @block.scalar
            def _(a):
                a.wait_ge(wz, 3)
                a.mul(wb[0:64, :], wb[0:64, :], 1 / 8.0).then_inc(wsc, 1)
                a.mul(wb[64:128, :], wb[64:128, :], float(1 / np.sqrt(32.0))).then_inc(wsc, 1)
                a.mul(w2[:, :], w2[:, :], float(1 / np.sqrt(32.0))).then_inc(wsc, 1)
                a.mul(last[:, :], last[:, :], float(cl)).then_inc(wsc, 1)
                a.mul(ws[:, :], ws[:, :], float(cs)).then_inc(wsc, 1)
                a.mul(wv[:, :], wv[:, :], float(cv)).then_inc(wsc, 1)

        R = 4
        gi, wi = sb("gi", [P, R, 1], I32), sb("wi", [P, R, 1], I32)
        xg = sb("xg", [P, R, F + 1 + nb])
        t1, t2 = sb("t1", [P, 2, P]), sb("t2", [KT, 2, P])
        sv = sb("sv", [P, 4, 224])
        h1, h2 = sb("h1", [nh, 2, P]), sb("h2", [64, 2, P])
        mid, tmp = sb("mid", [P, 2, 96 + 3 * vw]), sb("tmp", [P, 2, 480])
        ms, mvt = sb("ms", [96, 2, P]), sb("mvt", [vw, 2, 3 * P])
        tot = sb("tot", [P, R, F])
        s1 = sb("s1", [P, F])
        fix = sb("fix", [P, F])
        pt, py, pm, px = ps("pt"), ps("py"), ps("pm"), ps("px")
        pw = [ps(f"pw{r}") for r in range(2)]
        po = [ps(f"po{r}") for r in range(2)]
        gat = [sem(f"gat{r}") for r in range(R)]
        sct = [sem(f"sct{r}") for r in range(R)]
        gic, wic, arc = sem("gic"), sem("wic"), sem("arc")
        xt, xtc, y, svc, m2, h2c, wr, cgs, mt, mtc, o, acc, gate, fx = (sem(n) for n in (
            "xt", "xtc", "y", "svc", "m2", "h2c", "wr", "cg", "mt", "mtc", "o", "acc", "gate", "fx"))
        init, fixed, order = sem("init"), sem("fixed"), sem("order")
        AC = 2
        LW = 3 if cross else 2
        LE, LF = LW + 2, LW + 3
        LS = LF + 4

        with nc.Block() as block:
            @block.gpsimd
            def _(g):
                top = g.to_reg(NROWS - 1)

                def gather(k):
                    r = k.slot(R)
                    if k.past(R):
                        g.wait_ge(gat[r], k.lap(R) * 16)
                        g.wait_ge(svc, k.t - R + 1)
                        g.wait_ge(xt, k.t - R + 1)
                    g.tensor_copy(xg[:, r, F + 1:], q.attr[:, bass.ds(k.t, 1), a_col:a_col + nb]).then_inc(arc, 1)
                    g.tensor_copy(gi[:, r, :], q.es[:, bass.ds(k.t, 1), GIDX].bitcast(I32)).then_inc(gic, 1)
                    g.wait_ge(gic, k.t + 1)
                    g.sem_inc(gate, 1)
                    g.indirect_dma_start(xg[:, r, 0:F + 1], None, x, bass.IndirectOffsetOnAxis(ap=gi[:, r, :], axis=0),
                                         bounds_check=top, oob_is_err=False).then_inc(gat[r], 16)

                def scatter(k):
                    r = k.slot(R)
                    if k.past(R):
                        g.wait_ge(sct[r], k.lap(R) * 16)
                    g.tensor_copy(wi[:, r, :], q.es[:, bass.ds(k.t, 1), WIDX].bitcast(I32)).then_inc(wic, 1)
                    g.wait_ge(wic, k.t + 1)
                    g.wait_ge(acc, (k.t + 1) * AC)
                    g.sem_inc(gate, 1)
                    g.indirect_dma_start(agg, bass.IndirectOffsetOnAxis(ap=wi[:, r, :], axis=0), tot[:, r, :], None,
                                         bounds_check=top, oob_is_err=False).then_inc(sct[r], 16)
                sweep(g, ECOL, [(0, gather), (LS, scatter)], R)
                g.wait_ge(fx, 1)
                g.indirect_dma_start(agg, bass.IndirectOffsetOnAxis(ap=q.fix_id[:, :], axis=0), fix[:, :], None,
                                     bounds_check=top, oob_is_err=False).then_inc(fixed, 16)
                g.wait_ge(fixed, 16)
                for r in range(R):
                    g.wait_ge(sct[r], 16 * len(range(r, ECOL, R)))

            @block.tensor
            def _(pe):
                def turn(k):
                    r = k.slot(2)
                    if k.past(1):
                        pe.wait_ge(xtc, k.t)
                    pe.wait_ge(arc, k.t + 1)
                    pe.wait_ge(gat[k.slot(R)], (k.lap(R) + 1) * 16)
                    pe.transpose(pt[:, 0:P], xg[:, k.slot(R), 0:P], m.ident[:, :])
                    pe.transpose(pt[0:KT, P:2 * P], xg[:, k.slot(R), P:], m.ident[:, :]).then_inc(xt, 1)

                def maps(k):
                    r = k.slot(2)
                    if k.past(1):
                        pe.wait_ge(svc, k.t)
                    pe.wait_ge(xtc, k.t + 1)
                    pe.matmul(py[:, 0:P], t1[:, r, :], wb[:, :], start=True, stop=True)
                    pe.matmul(py[:, P:F], t2[0:V, r, :], w2[:, :], start=True, stop=True)
                    pe.matmul(py[0:nh, F:F + P], f1[:, :], t2[:, r, :], start=True, stop=True).then_inc(y, 1)

                def hidden(k):
                    r = k.slot(2)
                    pe.wait_ge(svc, k.t + 1)
                    if k.past(1):
                        pe.wait_ge(h2c, k.t)
                    pe.sem_inc(order, 1)
                    pe.matmul(pm[0:64, 0:P], f2[:, :], h1[:, r, :], start=True, stop=True).then_inc(m2, 1)

                def weights(k):
                    r = k.slot(2)
                    pe.wait_ge(h2c if cross else svc, k.t + 1)
                    if k.past(2):
                        pe.wait_ge(cgs, (k.t - 1) * cgn)
                    pe.matmul(pw[r][:, 0:wn], (h2 if cross else h1)[:, r, :], f3[:, :], start=True,
                              stop=True).then_inc(wr, 1)

                def turn_mid(k):
                    r = k.slot(2)
                    pe.wait_ge(cgs, (k.t + 1) * cgn)
                    if k.past(1):
                        pe.wait_ge(mtc, k.t)
                    pe.transpose(px[0:96, 0:P], mid[:, r, 0:96], m.ident[:, :])
                    for d in range(3):
                        ins = pe.transpose(px[0:vw, (d + 1) * P:(d + 2) * P], mid[:, r, 96 + d * vw:96 + (d + 1) * vw],
                                           m.ident[:, :])
                    ins.then_inc(mt, 1)

                def out(k):
                    r = k.slot(2)
                    pe.wait_ge(mtc, k.t + 1)
                    if k.past(2):
                        pe.wait_ge(acc, (k.t - 1) * AC)
                    pe.matmul(po[r][:, 0:64], ms[:, r, :], ws[:, :], start=True, stop=True)
                    for d in range(3):
                        ins = pe.matmul(po[r][:, 64 + d * V:96 + d * V], mvt[:, r, d * P:(d + 1) * P],
                                        wv[:, :], start=True, stop=True)
                    ins.then_inc(o, 1)
                stages = [(0, turn), (1, maps)] + [(2, hidden)] * cross + [(LW, weights), (LE, turn_mid), (LF, out)]
                sweep(pe, ECOL, stages, 2)
                pe.wait_ge(acc, ECOL * AC)
                pe.matmul(py[:, 0:F], q.carry[:, :], tot[:, (ECOL - 1) % R, :], start=True, stop=True).then_inc(y, 1)

            @block.scalar
            def _(a):
                def copy_x(k):
                    r = k.slot(2)
                    if k.past(2):
                        a.wait_ge(y, k.t - 1)
                    a.wait_ge(xt, k.t + 1)
                    a.copy(t1[:, r, :], pt[:, 0:P])
                    a.copy(t2[:, r, :], pt[0:KT, P:2 * P]).then_inc(xtc, 1)

                def copy_y(k):
                    r = k.slot(2)
                    a.wait_ge(y, k.t + 1)
                    if k.past(2):
                        a.wait_ge(m2 if cross else wr, k.t - 1)
                    if k.past(4):
                        a.wait_ge(cgs, (k.t - 3) * cgn)
                    if cross:
                        a.copy(sv[:, k.slot(4), 0:F], py[:, 0:F])
                        a.copy(sv[:, k.slot(4), F:224], py[:, 64:128])
                    else:
                        scale = xg[:, k.slot(R), F:F + 1]
                        a.activation(sv[:, k.slot(4), 0:F], py[:, 0:F], ACT.Copy, scale=scale)
                        a.activation(sv[:, k.slot(4), F:224], py[:, 64:128], ACT.Copy, scale=scale)
                    a.activation(h1[:, r, :], py[0:nh, F:F + P], ACT.Silu if cross else ACT.Relu,
                                 scale=c1).then_inc(svc, 1)

                def act_2(k):
                    r = k.slot(2)
                    a.wait_ge(m2, k.t + 1)
                    if k.past(2):
                        a.wait_ge(wr, k.t - 1)
                    a.activation(h2[:, r, :], pm[0:64, 0:P], ACT.Silu, scale=1 / 8.0).then_inc(h2c, 1)

                def copy_mid(k):
                    r = k.slot(2)
                    a.wait_ge(mt, k.t + 1)
                    if k.past(2):
                        a.wait_ge(o, k.t - 1)
                    a.copy(ms[:, r, :], px[0:96, 0:P])
                    a.copy(mvt[:, r, :], px[0:vw, P:4 * P]).then_inc(mtc, 1)
                sweep(a, ECOL, [(0, copy_x), (1, copy_y)] + [(2, act_2)] * cross + [(LE, copy_mid)], 4)

            @block.vector
            def _(v):
                v.memset(s1[:, :], 0.0).then_inc(init, 1)
                v.memset(tot[:, R - 1, :], 0.0).then_inc(init, 1)
                v.wait_ge(init, 2)

                def product(k):
                    r = k.slot(2)
                    v.wait_ge(wr, k.t + 1)
                    v.wait_ge(svc, k.t + 1)
                    if k.past(2):
                        v.wait_ge(mt, k.t - 1)
                    c = Chain(v, cgs, cgn, k)
                    s = sv[:, k.slot(4), :]
                    edge = bass.ds(k.t, 1)
                    cg(v, c, pw[r][:, 0:wn], s[:, 0:64], s[:, 64:224], q.es[:, edge, Y0],
                       lambda i, j: q.es[:, edge, Y1 + i:Y1 + j].rearrange("p a c -> p (a c)"), R3,
                       mid[:, r, :], tmp[:, r, :], cross)

                def accumulate(k):
                    r = k.slot(R)
                    v.wait_ge(o, k.t + 1)
                    if k.past(R):
                        v.wait_ge(sct[r], k.lap(R) * 16)
                    c = Chain(v, acc, AC, k)
                    if k.past(1):
                        v.wait_ge(acc, k.t * AC)
                    edge = bass.ds(k.t, 1)
                    pos = po[k.slot(2)][:, 0:F]
                    c(v.scalar_tensor_tensor(tot[:, r, :], tot[:, (r - 1) % R, :], q.es[:, edge, SAME], pos,
                                             ALU.mult, ALU.add))
                    c.wait()
                    c(v.scalar_tensor_tensor(s1[:, :], tot[:, r, :], q.es[:, edge, FEND], s1[:, :], ALU.mult, ALU.add))
                sweep(v, ECOL, [(LW, product), (LF, accumulate)], 4)
                v.wait_ge(y, ECOL + 1)
                v.wait_ge(acc, ECOL * AC)
                v.tensor_tensor(fix[:, :], s1[:, :], py[:, 0:F], ALU.add).then_inc(fx, 1)


def node_layer(nc, m, io, layer, x, agg, out):
    w = io.w
    maps_ = {0: (w["L0_gnn_Wsc0"], w["L0_gnn_Wsc1"]), 1: (w["L1_gnn_W_si0"], w["L1_gnn_W_si1"]),
             2: None, 3: (w["L3_gnn_lu0"], w["L3_gnn_lu1"])}[layer]
    owid = out.shape[1]
    with ExitStack() as ctx:
        sb, ps, sem = scope(nc, ctx, f"n{layer}")
        wb, w2 = sb("wb", [P, P]), sb("w2", [V, V])
        gain = sb("gain", [P, F])
        wl, wz, wsc = sem("wl"), sem("wz"), sem("wsc")
        if maps_:
            loads = block_loads(wb, w2, *maps_)
            if layer == 0:
                g1 = w["L0_gnn_g1"]
                loads += [(gain[:, 0:64], w["L0_gnn_g0"].partition_broadcast(P))] + [
                    (gain[:, 64 + 32 * d:96 + 32 * d], g1.partition_broadcast(P)) for d in range(3)]
            with nc.Block() as block:
                @block.vector
                def _(v):
                    v.memset(wb[:, :], 0.0).then_inc(wz, 1)

                @block.sync
                def _(sp):
                    sp.wait_ge(wz, 1)
                    chain_loads(sp, wl, loads)
                    sp.sem_inc(wz, 1)

                @block.scalar
                def _(a):
                    a.wait_ge(wz, 2)
                    a.mul(wb[0:64, :], wb[0:64, :], 1 / 8.0).then_inc(wsc, 1)
                    a.mul(wb[64:128, :], wb[64:128, :], float(1 / np.sqrt(32.0))).then_inc(wsc, 1)
                    a.mul(w2[:, :], w2[:, :], float(1 / np.sqrt(32.0))).then_inc(wsc, 1)
        RL, R = 8, 4
        xn, ag = sb("xn", [P, RL, GRP, F + 1]), sb("ag", [P, RL, GRP, F])
        ta, tb = sb("ta", [P, 2, GRP * P]), sb("tb", [V, 2, GRP * P])
        y, sq, z = sb("y", [P, R, GRP, F]), sb("sq", [P, GRP, F]), sb("z", [P, R, GRP, F])
        ssum, rms, rrms = sb("ssum", [P, R, 2, GRP]), sb("rms", [P, R, 2, GRP]), sb("rrms", [P, R, 2, GRP])
        st, mv = sb("st", [P, 2, GRP, 6]), sb("mv", [P, R, GRP, 2])
        sd, rstd, shift = sb("sd", [P, R, GRP]), sb("rstd", [P, R, GRP]), sb("shift", [P, R, GRP])
        xo = sb("xo", [P, R, GRP, owid])
        pa, pb, pc, pd = ([ps(f"p{n}{r}") for r in range(2)] for n in "abcd")
        ldx, lda = ([sem(f"{n}{r}") for r in range(RL)] for n in ("ldx", "lda"))
        sto = [sem(f"sto{r}") for r in range(R)]
        tr, trc, mp, c1, sqd, rm, c2, sdd, c3, fin, order = (sem(n) for n in (
            "tr", "trc", "mp", "c1", "sqd", "rm", "c2", "sdd", "c3", "fin", "order"))
        K1 = 2 if maps_ else 1
        K2 = {0: 2 * GRP + 2, 1: GRP, 2: 0, 3: 1}[layer] + 2 * GRP
        K3 = 2
        late = int(layer == 0)
        xv = x.rearrange("(p q j) f -> p q (j f)", p=P, j=GRP)
        av = agg.rearrange("(p q j) f -> p q (j f)", p=P, j=GRP)
        ov = out.rearrange("(p q j) f -> p q (j f)", p=P, j=GRP)

        def flat(ap):
            return ap.rearrange("p a b -> p (a b)")

        with nc.Block() as block:
            @block.sync
            def _(sp):
                def load(k):
                    r = k.slot(RL)
                    if k.past(RL):
                        sp.wait_ge(fin, k.t - RL + 1)
                    sp.dma_start(flat(xn[:, r, :, :]), flat(xv[:, bass.ds(k.t, 1), :])).then_inc(ldx[r], 16)
                    sp.dma_start(flat(ag[:, r, :, :]), flat(av[:, bass.ds(k.t, 1), :])).then_inc(lda[r], 16)

                def store(k):
                    r = k.slot(R)
                    sp.wait_ge(fin, k.t + 1)
                    sp.dma_start(flat(ov[:, bass.ds(k.t, 1), :]), flat(xo[:, r, :, :])).then_inc(sto[r], 16)
                sweep(sp, NGRP, [(0, load), (RL - 1, store)], RL, RL)
                for r in range(R):
                    sp.wait_ge(sto[r], 16 * len(range(r, NGRP, R)))

            @block.tensor
            def _(pe):
                if not maps_:
                    return

                def turn(k):
                    r = k.slot(2)
                    pe.wait_ge(ldx[k.slot(RL)], (k.lap(RL) + 1) * 16)
                    if k.past(2):
                        pe.wait_ge(trc, k.t - 1)
                    for j in range(GRP):
                        pe.transpose(pa[r][:, j * P:(j + 1) * P], xn[:, k.slot(RL), j, 0:P], m.ident[:, :])
                        ins = pe.transpose(pb[r][0:V, j * P:(j + 1) * P], xn[:, k.slot(RL), j, P:F], m.ident[:, :])
                    ins.then_inc(tr, 1)

                def maps(k):
                    r = k.slot(2)
                    pe.wait_ge(trc, k.t + 1)
                    if k.past(2):
                        pe.wait_ge(c1, (k.t - 1) * K1)
                    for j in range(GRP):
                        pe.matmul(pc[r][:, j * P:(j + 1) * P], ta[:, r, j * P:(j + 1) * P], wb[:, :], start=True,
                                  stop=True)
                        ins = pe.matmul(pd[r][:, j * V:(j + 1) * V], tb[:, r, j * P:(j + 1) * P],
                                        w2[:, :], start=True, stop=True)
                    ins.then_inc(mp, 1)
                sweep(pe, NGRP, [(0, turn), (1, maps)], RL, RL)

            @block.scalar
            def _(a):
                def copy_x(k):
                    r = k.slot(2)
                    if k.past(2):
                        a.wait_ge(mp, k.t - 1)
                    a.wait_ge(tr, k.t + 1)
                    a.copy(ta[:, r, :], pa[r][:, :])
                    a.copy(tb[:, r, :], pb[r][0:V, :]).then_inc(trc, 1)

                def root(k):
                    r = k.slot(R)
                    a.wait_ge(c1, (k.t + 1) * K1)
                    if k.past(1):
                        a.wait_ge(rm, k.t)
                    if k.past(R):
                        a.wait_ge(c2, (k.t - R + 1) * K2)
                    for d, (f, t, n) in enumerate(((0, 64, 64), (64, F, 32))):
                        for j in range(GRP):
                            ins = a.activation(sq[:, j, f:t], y[:, r, j, f:t], ACT.Square, scale=float(1 / np.sqrt(n)),
                                               accum_out=ssum[:, r, d, j:j + 1])
                    ins.then_inc(sqd, 1)
                    a.wait_ge(sqd, k.t + 1)
                    a.activation(flat(rms[:, r, :, :]), flat(ssum[:, r, :, :]), ACT.Sqrt, bias=m.eps[:, :]).then_inc(rm, 1)

                def deviation(k):
                    r = k.slot(R)
                    a.wait_ge(c2, (k.t + 1) * K2)
                    if k.past(R):
                        a.wait_ge(c3, (k.t - R + 1) * K3)
                    a.activation(sd[:, r, :], mv[:, r, :, 1], ACT.Sqrt, bias=m.eps[:, :]).then_inc(sdd, 1)

                def norm(k):
                    r = k.slot(R)
                    a.wait_ge(c3, (k.t + 1) * K3)
                    if k.past(R):
                        a.wait_ge(sto[r], k.lap(R) * 16)
                    for j in range(GRP):
                        ins = a.activation(xo[:, r, j, 0:F], z[:, r, j, :], ACT.Identity, scale=rstd[:, r, j:j + 1],
                                           bias=shift[:, r, j:j + 1])
                    if owid > F:
                        ins = a.copy(xo[:, r, :, F:F + 1], xn[:, k.slot(RL), :, F:F + 1])
                    ins.then_inc(fin, 1)
                stages = [(0, copy_x)] * bool(maps_) + [(2, root)] * late + [(2 + late, deviation), (3 + late, norm)]
                sweep(a, NGRP, stages, RL, RL)

            @block.vector
            def _(v):
                def raw(k):
                    r, q = k.slot(R), k.slot(RL)
                    c = Chain(v, c1, K1, k)
                    v.wait_ge(lda[q], (k.lap(RL) + 1) * 16)
                    v.wait_ge(ldx[q], (k.lap(RL) + 1) * 16)
                    if maps_:
                        v.wait_ge(mp, k.t + 1)
                        if k.past(R):
                            v.wait_ge(c2, (k.t - R + 1) * K2)
                        pcv = pc[k.slot(2)][:, :].rearrange("p (j f) -> p j f", j=GRP)
                        pdv = pd[k.slot(2)][:, 0:P].rearrange("p (j f) -> p j f", j=GRP)
                        c(v.tensor_tensor(y[:, r, :, 0:P], pcv, ag[:, q, :, 0:P], ALU.add))
                        c(v.tensor_tensor(y[:, r, :, P:F], pdv, ag[:, q, :, P:F], ALU.add))
                    else:
                        if k.past(R):
                            v.wait_ge(fin, k.t - R + 1)
                        c(v.scalar_tensor_tensor(z[:, r, :, :], xn[:, q, :, 0:F], 2.0, ag[:, q, :, :], ALU.mult,
                                                 ALU.add))

                def combine(k):
                    r, q = k.slot(R), k.slot(RL)
                    c = Chain(v, c2, K2, k)
                    v.wait_ge(c1, (k.t + 1) * K1)
                    if k.past(R):
                        v.wait_ge(fin, k.t - R + 1)
                    if layer == 0:
                        v.wait_ge(rm, k.t + 1)
                        c(v.reciprocal(rrms[:, r, :, :], rms[:, r, :, :]))
                        c.wait()
                        for j in range(GRP):
                            for d, (f, t) in enumerate(((0, 64), (64, F))):
                                c(v.scalar_tensor_tensor(z[:, r, j, f:t], y[:, r, j, f:t], rrms[:, r, d, j:j + 1],
                                                         gain[:, f:t], ALU.mult, ALU.mult))
                        c.wait()
                        c(v.tensor_tensor(z[:, r, :, :], z[:, r, :, :], xn[:, q, :, 0:F], ALU.add))
                        c.wait()
                    elif layer == 1:
                        for j in range(GRP):
                            c(v.scalar_tensor_tensor(z[:, r, j, :], y[:, r, j, :], xn[:, q, j, F:F + 1],
                                                     xn[:, q, j, 0:F], ALU.mult, ALU.add))
                        c.wait()
                    elif layer == 3:
                        c(v.scalar_tensor_tensor(z[:, r, :, :], xn[:, q, :, 0:F], 2.0, y[:, r, :, :], ALU.mult,
                                                 ALU.add))
                        c.wait()
                    for j in range(GRP):
                        c(v.bn_stats(st[:, k.slot(2), j, :], z[:, r, j, :]))
                    c.wait()
                    v.sem_inc(order, 1)
                    for j in range(GRP):
                        c(v.bn_aggr(mv[:, r, j, :], st[:, k.slot(2), j, :]))

                def inverse(k):
                    r = k.slot(R)
                    c = Chain(v, c3, K3, k)
                    v.wait_ge(sdd, k.t + 1)
                    c(v.reciprocal(rstd[:, r, :], sd[:, r, :]))
                    c.wait()
                    c(v.scalar_tensor_tensor(shift[:, r, :], mv[:, r, :, 0], -1.0, rstd[:, r, :], ALU.mult, ALU.mult))
                sweep(v, NGRP, [(0, raw), (late, combine), (late + 1, inverse)], RL, RL)


BIG = 1e30


def attention_messages(nc, m, io, x, q, logits, hid):
    w = io.w
    with ExitStack() as ctx:
        sb, ps, sem = scope(nc, ctx, "a")
        wbs, wbd = sb("wbs", [P, P]), sb("wbd", [P, P])
        KZ = 2 * V + 16
        w2 = sb("w2", [KZ, V + 224])
        gam, bet, gam2 = sb("gam", [P, 1]), sb("bet", [P, 1]), sb("gam2", [KZ, 1])
        wsc, wsvt, wvv = sb("wsc", [96, 160]), sb("wsvt", [64, 96]), sb("wvv", [P, V])
        pset = ps("pset")
        wg, wsl, wvl = sb("wg", [64, V]), sb("wsl", [96, 64]), sb("wvl", [P, V])
        adot, w2c = sb("adot", [P, 64]), sb("w2c", [P, 224])
        half = sb("half", [P, 4])
        wl, wz, pes, acs = sem("wl"), sem("wz"), sem("pes"), sem("acs")

        def col(name):
            return w[name].rearrange("(a b) -> a b", b=1)
        gv = col("L2_gnn_gamma_v")
        loads = [(wb[a:b, a:b], w[f"L2_gnn_W{t}_{n}"]) for wb, n in ((wbs, "src"), (wbd, "dst"))
                 for a, b, t in ((0, 64, "s"), (64, 96, "v"), (96, 128, "v"))] + [
            (w2[0:V, 0:V], w["L2_gnn_Wv_src"]), (w2[V:2 * V, 0:V], w["L2_gnn_Wv_dst"]),
            (gam[0:64, :], col("L2_gnn_gamma_s")), (gam[64:96, :], gv), (gam[96:128, :], gv),
            (gam2[0:V, :], gv), (gam2[V:2 * V, :], gv), (bet[0:64, :], col("L2_gnn_beta_s")),
            (w2[2 * V:KZ, V:], w["L2_gnn_W_rbf"]), (wsc[:, 0:64], w["L2_gnn_W_alpha"]), (wsc[:, 64:128], w["L2_gnn_Ws_val"]),
            (wvv[:, :], w["L2_gnn_Wv_val"]), (wg[:, :], w["L2_gnn_Wg"]), (wsl[:, :], w["L2_gnn_Ws_vlin"]),
            (wvl[:, :], w["L2_gnn_Wv_vlin"]),
            (adot[:, :], w["L2_gnn_alpha_dot"].rearrange("a h k -> (a h k)").partition_broadcast(P))]
        at = 0
        for n in ("ss", "sv", "vs", "vv0", "vv1"):
            wd = w[f"L2_gnn_w2_{n}"]
            loads.append((w2c[:, at:at + wd.shape[0]], wd.partition_broadcast(P)))
            at += wd.shape[0]
        with nc.Block() as block:
            @block.vector
            def _(v):
                v.memset(wbs[:, :], 0.0).then_inc(wz, 1)
                v.memset(wbd[:, :], 0.0).then_inc(wz, 1)
                v.memset(bet[:, :], 0.0).then_inc(wz, 1)
                v.memset(half[:, :], -0.5).then_inc(wz, 1)
                v.memset(w2[:, :], 0.0).then_inc(wz, 1)
                v.memset(gam2[:, :], 1.0).then_inc(wz, 1)

            @block.sync
            def _(sp):
                sp.wait_ge(wz, 6)
                chain_loads(sp, wl, loads)
                sp.sem_inc(wz, 1)

            @block.tensor
            def _(pe):
                pe.wait_ge(wz, 7)
                pe.transpose(pset[0:64, 0:96], wsc[:, 64:128], m.ident[0:96, 0:96]).then_inc(pes, 1)
                pe.wait_ge(acs, 1)
                pe.matmul(pset[0:96, P:P + V], wsvt[:, :], wg[:, :], start=True, stop=True).then_inc(pes, 1)

            @block.scalar
            def _(a):
                a.wait_ge(pes, 1)
                a.copy(wsvt[:, :], pset[0:64, 0:96]).then_inc(acs, 1)
                a.wait_ge(pes, 2)
                a.copy(wsc[:, 128:160], pset[0:96, P:P + V]).then_inc(acs, 1)

        RG, R = 8, 4
        gi = sb("gi", [P, RG, 2], I32)
        xg = sb("xg", [P, RG, 2, F + 1])
        st, mvs = sb("st", [P, R, 2, 6]), sb("mvs", [P, R, 2, 3])
        sqj = sb("sqj", [P, 2, 96])
        vse, rsd = sb("vse", [P, R, 2, 2]), sb("rsd", [P, R, 2, 2])
        xn = sb("xn", [P, 2, 2 * P + KZ])
        t1, t2 = sb("t1", [P, 2, 2 * P]), sb("t2", [KZ, 2, P])
        sv, we = sb("sv", [P, R, 224]), sb("we", [P, R, 224])
        mid, tmp = sb("mid", [P, 2, 480]), sb("tmp", [P, 2, 480])
        ms, mvt = sb("ms", [96, 2, P]), sb("mvt", [P, 2, 3 * P])
        lg, lg4 = sb("lg", [P, 2, 128]), sb("lg4", [P, 2, 4])
        sig, val = sb("sig", [P, R, 96]), sb("val", [P, R, F])
        vraw = sb("vraw", [P, R, F])
        mid2, tmp2 = sb("mid2", [P, 2, 480]), sb("tmp2", [P, 2, 480])
        ms2, mvt2 = sb("ms2", [96, 2, P]), sb("mvt2", [P, 2, 3 * P])
        hs = sb("hs", [P, R, F])
        pt, py, px, pv, px2, ph = (ps(n) for n in ("pt", "py", "px", "pv", "px2", "ph"))
        gas, gad = ([sem(f"{n}{r}") for r in range(RG)] for n in ("gas", "gad"))
        sto = [sem(f"sto{r}") for r in range(R)]
        gic, gate, sqs, stt, rs, nrm, xt, xtc, y, svc, cg1, mt, mtc, o, oc, lgs, cg2, mt2, mtc2, h, hc = (
            sem(n) for n in ("gic", "gate", "sqs", "stt", "rs", "nrm", "xt", "xtc", "y", "svc", "cg1", "mt",
                             "mtc", "o", "oc", "lgs", "cg2", "mt2", "mtc2", "h", "hc"))
        order = sem("order")
        N1, N2, LG, C2 = 4, 7, 5, CG_OPS_CROSS + 2
        A_ST, A_INV, A_NRM, A_T, A_MAP, A_CG, A_TM, A_OUT, A_LG, A_CG2, A_TM2, A_H = (
            0, 2, 3, 3, 4, 5, 6, 7, 8, 8, 9, 10)
        hv_ = hid.rearrange("(p j) f -> p j f", p=P)

        with nc.Block() as block:
            @block.gpsimd
            def _(g):
                top = g.to_reg(NROWS - 1)

                def gather(k):
                    r = k.slot(RG)
                    if k.past(RG):
                        g.wait_ge(gas[r], k.lap(RG) * 16)
                        g.wait_ge(gad[r], k.lap(RG) * 16)
                        g.wait_ge(nrm, (k.t - RG + 1) * N2)
                    g.tensor_copy(gi[:, r, :], q.es[:, bass.ds(k.t, 1), GIDX:GIDX2 + 1].bitcast(I32)).then_inc(gic, 1)
                    g.wait_ge(gic, k.t + 1)
                    g.sem_inc(gate, 1)
                    for d, ga in enumerate((gas, gad)):
                        g.indirect_dma_start(xg[:, r, d, :], None, x,
                                             bass.IndirectOffsetOnAxis(ap=gi[:, r, d:d + 1], axis=0),
                                             bounds_check=top, oob_is_err=False).then_inc(ga[r], 16)

                def invert(k):
                    r = k.slot(R)
                    g.wait_ge(stt, (k.t + 1) * N1)
                    g.wait_ge(sqs, k.t + 1)
                    if k.past(R):
                        g.wait_ge(nrm, (k.t - R + 1) * N2)
                    g.sem_inc(gate, 1)
                    g.tensor_scalar(vse[:, r, :, :], mvs[:, r, :, 1:3], EPS, None, ALU.add).then_inc(rs, 1)
                    g.wait_ge(rs, 2 * k.t + 1)
                    g.sem_inc(gate, 1)
                    g.tensor_tensor(rsd[:, r, :, :].rearrange("p a b -> p (a b)"),
                                    vse[:, r, :, :].rearrange("p a b -> p (a b)"), half[:, :],
                                    ALU.pow).then_inc(rs, 1)
                sweep(g, ECOL, [(0, gather), (A_INV, invert)], RG, RG)

            @block.tensor
            def _(pe):
                def turn(k):
                    r = k.slot(2)
                    if k.past(1):
                        pe.wait_ge(xtc, k.t)
                    pe.wait_ge(nrm, (k.t + 1) * N2)
                    pe.transpose(pt[:, 0:P], xn[:, r, 0:P], m.ident[:, :])
                    pe.transpose(pt[:, P:2 * P], xn[:, r, P:2 * P], m.ident[:, :])
                    pe.transpose(pt[0:KZ, 2 * P:3 * P], xn[:, r, 2 * P:], m.ident[:, :]).then_inc(xt, 1)

                def maps(k):
                    r = k.slot(2)
                    if k.past(1):
                        pe.wait_ge(svc, k.t)
                    pe.wait_ge(xtc, k.t + 1)
                    pe.matmul(py[:, 0:P], t1[:, r, 0:P], wbs[:, :], start=True, stop=False)
                    pe.matmul(py[:, 0:P], t1[:, r, P:2 * P], wbd[:, :], start=False, stop=True)
                    pe.matmul(py[:, P:F + 224], t2[:, r, :], w2[:, :], start=True, stop=True).then_inc(y, 1)

                def turn_mid(k, mid=mid, px=px, cgs=cg1, n=CG_OPS_CROSS, mtc=mtc, mt=mt):
                    r = k.slot(2)
                    pe.wait_ge(cgs, (k.t + 1) * n)
                    if k.past(1):
                        pe.wait_ge(mtc, k.t)
                    pe.transpose(px[0:96, 0:P], mid[:, r, 0:96], m.ident[:, :])
                    for d in range(3):
                        ins = pe.transpose(px[:, (d + 1) * P:(d + 2) * P], mid[:, r, 96 + d * P:96 + (d + 1) * P],
                                           m.ident[:, :])
                    ins.then_inc(mt, 1)

                def out(k):
                    r = k.slot(2)
                    pe.wait_ge(mtc, k.t + 1)
                    if k.past(1):
                        pe.wait_ge(oc, k.t)
                    pe.matmul(pv[:, 0:F], ms[:, r, :], wsc[:, :], start=True, stop=True)
                    for d in range(3):
                        ins = pe.matmul(pv[:, F + d * V:F + (d + 1) * V], mvt[:, r, d * P:(d + 1) * P], wvv[:, :],
                                        start=True, stop=True)
                    ins.then_inc(o, 1)

                def turn_mid2(k):
                    turn_mid(k, mid2, px2, cg2, C2, mtc2, mt2)

                def heads(k):
                    r = k.slot(2)
                    pe.wait_ge(mtc2, k.t + 1)
                    if k.past(1):
                        pe.wait_ge(hc, k.t)
                    pe.matmul(ph[:, 0:64], ms2[:, r, :], wsl[:, :], start=True, stop=True)
                    for d in range(3):
                        ins = pe.matmul(ph[:, 64 + d * V:96 + d * V], mvt2[:, r, d * P:(d + 1) * P], wvl[:, :],
                                        start=True, stop=True)
                    ins.then_inc(h, 1)
                sweep(pe, ECOL, [(A_T, turn), (A_MAP, maps), (A_TM, turn_mid), (A_OUT, out),
                                 (A_TM2, turn_mid2), (A_H, heads)], RG, RG)

            @block.scalar
            def _(a):
                def squares(k):
                    r = k.slot(R)
                    a.wait_ge(gas[k.slot(RG)], (k.lap(RG) + 1) * 16)
                    a.wait_ge(gad[k.slot(RG)], (k.lap(RG) + 1) * 16)
                    if k.past(R):
                        a.wait_ge(rs, 2 * (k.t - R + 1))
                    for d in range(2):
                        if d == 0 and k.past(1):
                            a.wait_ge(sqs, k.t)
                        ins = a.activation(sqj[:, d, :], xg[:, k.slot(RG), d, 64:F], ACT.Square, scale=float(1 / np.sqrt(32.0)),
                                           accum_out=mvs[:, r, d, 2:3])
                    ins.then_inc(sqs, 1)

                def copy_x(k):
                    r = k.slot(2)
                    if k.past(2):
                        a.wait_ge(y, k.t - 1)
                    a.wait_ge(xt, k.t + 1)
                    a.activation(t1[:, r, :], pt[:, 0:2 * P], ACT.Identity, scale=gam[:, :], bias=bet[:, :])
                    a.activation(t2[:, r, :], pt[0:KZ, 2 * P:3 * P], ACT.Copy, scale=gam2[:, :]).then_inc(xtc, 1)

                def copy_y(k):
                    r = k.slot(R)
                    a.wait_ge(y, k.t + 1)
                    if k.past(R):
                        a.wait_ge(cg1, (k.t - R + 1) * CG_OPS_CROSS)
                    a.copy(sv[:, r, 0:F], py[:, 0:F])
                    a.copy(sv[:, r, F:224], py[:, 64:128])
                    a.copy(we[:, r, :], py[:, F:F + 224]).then_inc(svc, 1)

                def copy_mid(k, px=px, ms=ms, mvt=mvt, mt=mt, o=o, mtc=mtc):
                    r = k.slot(2)
                    a.wait_ge(mt, k.t + 1)
                    if k.past(2):
                        a.wait_ge(o, k.t - 1)
                    a.copy(ms[:, r, :], px[0:96, 0:P])
                    a.copy(mvt[:, r, :], px[:, P:4 * P]).then_inc(mtc, 1)

                def copy_out(k):
                    r = k.slot(2)
                    a.wait_ge(o, k.t + 1)
                    if k.past(R):
                        a.wait_ge(lgs, (k.t - R + 1) * LG)
                        a.wait_ge(cg2, (k.t - R + 1) * C2)
                    a.copy(vraw[:, k.slot(R), 0:64], pv[:, 0:64])
                    a.copy(vraw[:, k.slot(R), 64:F], pv[:, F:256])
                    a.activation(sig[:, k.slot(R), :], pv[:, 64:F], ACT.Sigmoid).then_inc(oc, 1)

                def copy_mid2(k):
                    copy_mid(k, px2, ms2, mvt2, mt2, h, mtc2)

                def copy_h(k):
                    r = k.slot(R)
                    a.wait_ge(h, k.t + 1)
                    if k.past(R):
                        a.wait_ge(sto[r], k.lap(R) * 16)
                    a.copy(hs[:, r, :], ph[:, 0:F]).then_inc(hc, 1)
                sweep(a, ECOL, [(A_ST, squares), (A_T, copy_x), (A_MAP, copy_y), (A_TM, copy_mid), (A_OUT, copy_out),
                                (A_TM2, copy_mid2), (A_H, copy_h)], RG, RG)

            @block.sync
            def _(sp):
                def store(k):
                    r = k.slot(R)
                    sp.wait_ge(hc, k.t + 1)
                    sp.dma_start(hv_[:, bass.ds(k.t, 1), :].rearrange("p a f -> p (a f)"), hs[:, r, :]).then_inc(sto[r], 16)
                sweep(sp, ECOL, [(0, store)], 4)
                for r in range(R):
                    sp.wait_ge(sto[r], 16 * len(range(r, ECOL, R)))

            @block.vector
            def _(v):
                def stats(k):
                    r = k.slot(R)
                    v.wait_ge(gas[k.slot(RG)], (k.lap(RG) + 1) * 16)
                    v.wait_ge(gad[k.slot(RG)], (k.lap(RG) + 1) * 16)
                    c = Chain(v, stt, N1, k)
                    if k.past(R):
                        v.wait_ge(rs, 2 * (k.t - R + 1))
                    for d in range(2):
                        c(v.bn_stats(st[:, r, d, :], xg[:, k.slot(RG), d, 0:64]))
                    c.wait()
                    v.sem_inc(order, 1)
                    for d in range(2):
                        c(v.bn_aggr(mvs[:, r, d, 0:2], st[:, r, d, :]))

                def normalize(k):
                    r = k.slot(R)
                    c = Chain(v, nrm, N2, k)
                    v.wait_ge(rs, 2 * k.t + 2)
                    if k.past(2):
                        v.wait_ge(xt, k.t - 1)
                    n = xn[:, k.slot(2), :]
                    for d in range(2):
                        c(v.tensor_scalar(n[:, d * P:d * P + 64], xg[:, k.slot(RG), d, 0:64], mvs[:, r, d, 0:1],
                                          rsd[:, r, d, 0:1], ALU.subtract, ALU.mult))
                        c(v.tensor_scalar(n[:, d * P + 64:(d + 1) * P], xg[:, k.slot(RG), d, 64:P], rsd[:, r, d, 1:2], None,
                                          ALU.mult))
                        c(v.tensor_scalar(n[:, 2 * P + d * V:2 * P + (d + 1) * V], xg[:, k.slot(RG), d, P:F],
                                          rsd[:, r, d, 1:2], None, ALU.mult))
                    c(v.tensor_scalar(n[:, 2 * P + 2 * V:], q.attr[:, bass.ds(k.t, 1), A16:A16 + 16].rearrange(
                        "p a c -> p (a c)"), 1.0, None, ALU.mult))

                def y1(k):
                    return lambda i, j: q.es[:, bass.ds(k.t, 1), Y1 + i:Y1 + j].rearrange("p a c -> p (a c)")

                def product(k):
                    r = k.slot(2)
                    v.wait_ge(svc, k.t + 1)
                    if k.past(2):
                        v.wait_ge(mt, k.t - 1)
                    c = Chain(v, cg1, CG_OPS_CROSS, k)
                    s = sv[:, k.slot(R), :]
                    cg(v, c, we[:, k.slot(R), :], s[:, 0:64], s[:, 64:224], q.es[:, bass.ds(k.t, 1), Y0], y1(k), R3,
                       mid[:, r, :], tmp[:, r, :], True)

                def logit(k):
                    r = k.slot(2)
                    c = Chain(v, lgs, LG, k)
                    v.wait_ge(oc, k.t + 1)
                    a = vraw[:, k.slot(R), 0:64]
                    c(v.scalar_tensor_tensor(lg[:, r, 0:64], a, 0.2, a, ALU.mult, ALU.max))
                    c.wait()
                    c(v.tensor_tensor(lg[:, r, 64:128], lg[:, r, 0:64], adot[:, :], ALU.mult))
                    c.wait()
                    c(v.tensor_reduce(lg4[:, r, :], lg[:, r, 64:128].rearrange("p (h a) -> p h a", h=4), AX, ALU.add))
                    c.wait()
                    c(v.tensor_scalar(logits[:, :, bass.ds(k.t, 1)].rearrange("p h a -> p (h a)"), lg4[:, r, :], 1.0,
                                      None, ALU.mult))
                    c(v.tensor_scalar(lg[:, r, 0:1], lg[:, r, 0:1], 1.0, None, ALU.mult))

                def product2(k):
                    r, q4 = k.slot(2), k.slot(R)
                    v.wait_ge(oc, k.t + 1)
                    if k.past(2):
                        v.wait_ge(mt2, k.t - 1)
                    c = Chain(v, cg2, C2, k)
                    raw = vraw[:, q4, 64:F]
                    c(v.tensor_tensor(val[:, q4, 0:96].rearrange("p (c u) -> p c u", c=3),
                                      raw.rearrange("p (c u) -> p c u", c=3), bc(sig[:, q4, 64:96], 1, 3), ALU.mult))
                    c(v.tensor_tensor(val[:, q4, 96:F].rearrange("p (c u) -> p c u", c=2),
                                      raw[:, 0:64].rearrange("p (c u) -> p c u", c=2), bc(sig[:, q4, 64:96], 1, 2),
                                      ALU.mult))
                    c.wait()
                    c2 = Shifted(c, 2)
                    cg(v, c2, w2c[:, :], sig[:, q4, 0:64], val[:, q4, :], q.es[:, bass.ds(k.t, 1), Y0], y1(k), R3,
                       mid2[:, r, :], tmp2[:, r, :], True)
                sweep(v, ECOL, [(A_ST, stats), (A_NRM, normalize), (A_CG, product), (A_LG, logit),
                                (A_CG2, product2)], RG, RG)


def attention_weights(nc, m, q, logits, ex):
    with ExitStack() as ctx:
        sb, ps, sem = scope(nc, ctx, "w")
        ch, pe_s, ex_s = sem("ch"), sem("pe"), sem("ex")
        pf, pb, prun = sb("pf", [P, ECOL]), sb("pb", [P, ECOL]), sb("prun", [P, 2, ECOL])
        fw, bw = sb("fw", [P, 4, ECOL]), sb("bw", [P, 4, ECOL])
        wide = sb("wide", [P, 10, P])
        rows, pen = sb("rows", [P, 10, P]), sb("pen", [P, 2, 2, P])
        cand = sb("cand", [P, 2, 4, 2 * P])
        top = sb("top", [P, 2, 4])
        dif = sb("dif", [P, 4, ECOL])
        pr = [ps(f"pr{b}") for b in range(3)]
        block = ctx.enter_context(nc.Block())

        @block.vector
        def _(v):
            c = Static(v, ch)
            c(v.tensor_scalar(pf[:, :], q.es[:, :, SAME], -1.0, BIG, ALU.add, ALU.mult), wait=False)
            c(v.memset(pb[:, ECOL - 1:ECOL], -BIG), wait=False)
            c(v.tensor_scalar(pb[:, 0:ECOL - 1], q.es[:, 1:ECOL, SAME], -1.0, BIG, ALU.add, ALU.mult), wait=False)
            c(v.tensor_scalar(prun[:, 0, :], q.first_run[:, :], -1.0, BIG, ALU.add, ALU.mult), wait=False)
            c(v.tensor_scalar(prun[:, 1, :], q.last_run[:, :], -1.0, BIG, ALU.add, ALU.mult))
            for h in range(4):
                c(v.tensor_tensor_scan(fw[:, h, :], pf[:, :], logits[:, h, :], 0.0, ALU.add, ALU.max))
                c(v.tensor_tensor_scan(bw[:, h, ::-1], pb[:, ::-1], fw[:, h, ::-1], 0.0, ALU.add, ALU.max))
            for i in range(10):
                src = q.ends[:, i - 8:i - 7] if i >= 8 else bw[:, i % 4, (i // 4) * (ECOL - 1):(i // 4) * (ECOL - 1) + 1]
                c(v.tensor_scalar(wide[:, i, :], m.ones[:, :], src, None, ALU.mult), wait=False)
            v.sem_inc(ex_s, 1)
            v.wait_ge(ch, c.n)
            v.sem_inc(ex_s, 1)
            v.wait_ge(pe_s, 1)
            for i in range(10):
                c(v.tensor_copy(rows[:, i, :], pr[i // 4][:, (i % 4) * P:(i % 4 + 1) * P]), wait=i == 9)
            for t in range(2):
                for e in range(2):
                    c(v.tensor_scalar(pen[:, t, e, :], rows[:, 8 + e, :], q.ends[:, t:t + 1], -1.0, ALU.is_equal,
                                      ALU.add))
                    c(v.tensor_scalar(pen[:, t, e, :], pen[:, t, e, :], BIG, None, ALU.mult))
                for h in range(4):
                    for e in range(2):
                        c(v.tensor_tensor(cand[:, t, h, e * P:(e + 1) * P], rows[:, 4 * e + h, :], pen[:, t, e, :],
                                          ALU.add), wait=False)
                v.wait_ge(ch, c.n)
                c(v.tensor_reduce(top[:, t, :], cand[:, t, :, :], AX, ALU.max))
                for h in range(4):
                    c(v.scalar_tensor_tensor(bw[:, h, :], prun[:, t, :], top[:, t, h:h + 1], bw[:, h, :], ALU.add,
                                             ALU.max), wait=h == 3)
            c(v.tensor_tensor(dif[:, :, :], logits[:, :, :], bw[:, :, :], ALU.subtract))
            v.sem_inc(ex_s, 1)

        @block.tensor
        def _(pe):
            pe.wait_ge(ex_s, 2)
            for i in range(10):
                ins = pe.transpose(pr[i // 4][:, (i % 4) * P:(i % 4 + 1) * P], wide[:, i, :], m.ident[:, :])
            ins.then_inc(pe_s, 1)

        @block.scalar
        def _(a):
            a.wait_ge(ex_s, 3)
            a.activation(ex[:, :, :].rearrange("p j h -> p h j"), dif[:, :, :], ACT.Exp)


def attention_sums(nc, m, io, q, ex, hid, agg):
    w = io.w
    A = F + 4
    with ExitStack() as ctx:
        sb, ps, sem = scope(nc, ctx, "s")
        wb, w2 = sb("wb", [P, P]), sb("w2", [V, V])
        wl, wz = sem("wl"), sem("wz")
        with nc.Block() as block:
            @block.vector
            def _(v):
                v.memset(wb[:, :], 0.0).then_inc(wz, 1)

            @block.sync
            def _(sp):
                sp.wait_ge(wz, 1)
                chain_loads(sp, wl, block_loads(wb, w2, w["L2_gnn_Wps"], w["L2_gnn_Wpv"]))
        R = 4
        wi, hb, eh = sb("wi", [P, R, 1], I32), sb("hb", [P, R, F]), sb("eh", [P, 2, A])
        tot, s1 = sb("tot", [P, R, A]), sb("s1", [P, A])
        den, avg = sb("den", [P, 2, 8]), sb("avg", [P, 2, F])
        t1, t2, ob = sb("t1", [P, 2, P]), sb("t2", [V, 2, P]), sb("ob", [P, R, F])
        pt, py = [ps(f"pt{r}") for r in range(2)], [ps(f"py{r}") for r in range(2)]
        pf = ps("pf")
        ld, sct = [sem(f"ld{r}") for r in range(R)], [sem(f"sct{r}") for r in range(R)]
        wic, gate, init, acc, nrm, xt, xtc, y, obc, fx = (sem(n) for n in (
            "wic", "gate", "init", "acc", "nrm", "xt", "xtc", "y", "obc", "fx"))
        AC, NR = 5, 4
        hv_ = hid.rearrange("(p j) f -> p j f", p=P)
        with nc.Block() as block:
            @block.sync
            def _(sp):
                def load(k):
                    r = k.slot(R)
                    if k.past(R):
                        sp.wait_ge(acc, (k.t - R + 1) * AC)
                    sp.dma_start(hb[:, r, :], hv_[:, bass.ds(k.t, 1), :].rearrange("p a f -> p (a f)")).then_inc(ld[r], 16)
                sweep(sp, ECOL, [(0, load)], R)

            @block.vector
            def _(v):
                v.memset(s1[:, :], 0.0).then_inc(init, 1)
                v.memset(tot[:, R - 1, :], 0.0).then_inc(init, 1)
                v.wait_ge(init, 2)

                def accumulate(k):
                    r = k.slot(R)
                    c = Chain(v, acc, AC, k)
                    if k.past(R):
                        v.wait_ge(nrm, (k.t - R + 1) * NR)
                    if k.is_fix():
                        v.wait_ge(fx, 1)
                        v.wait_ge(acc, ECOL * AC)
                        v.tensor_tensor(tot[:, r, :], s1[:, :], pf[:, 0:A], ALU.add).then_inc(acc, AC)
                        return
                    v.wait_ge(ld[r], (k.lap(R) + 1) * 16)
                    e = ex[:, bass.ds(k.t, 1), :].rearrange("p a h -> p (a h)")
                    o = eh[:, k.slot(2), :]
                    c(v.tensor_tensor(o[:, 0:64].rearrange("p (h a) -> p h a", h=4),
                                      hb[:, r, 0:64].rearrange("p (h a) -> p h a", h=4), bc(e, 2, 16), ALU.mult))
                    c(v.tensor_tensor(o[:, 64:F].rearrange("p (c h a) -> p c h a", c=3, h=4),
                                      hb[:, r, 64:F].rearrange("p (c h a) -> p c h a", c=3, h=4),
                                      bc(bc(e, 2, 8), 1, 3), ALU.mult))
                    c(v.tensor_scalar(o[:, F:A], e, 1.0, None, ALU.mult))
                    c.wait()
                    edge = bass.ds(k.t, 1)
                    c(v.scalar_tensor_tensor(tot[:, r, :], tot[:, (r - 1) % R, :], q.es[:, edge, SAME], o, ALU.mult,
                                             ALU.add))
                    c.wait()
                    c(v.scalar_tensor_tensor(s1[:, :], tot[:, r, :], q.es[:, edge, FEND], s1[:, :], ALU.mult, ALU.add))

                def divide(k):
                    r, d = k.slot(R), k.slot(2)
                    c = Chain(v, nrm, NR, k)
                    v.wait_ge(acc, (k.t + 1) * AC)
                    if k.past(2):
                        v.wait_ge(xt, k.t - 1)
                    c(v.tensor_scalar(den[:, d, 0:4], tot[:, r, F:A], 1e-16, None, ALU.add))
                    c.wait()
                    c(v.reciprocal(den[:, d, 4:8], den[:, d, 0:4]))
                    c.wait()
                    inv = den[:, d, 4:8]
                    c(v.tensor_tensor(avg[:, d, 0:64].rearrange("p (h a) -> p h a", h=4),
                                      tot[:, r, 0:64].rearrange("p (h a) -> p h a", h=4), bc(inv, 2, 16), ALU.mult))
                    c(v.tensor_tensor(avg[:, d, 64:F].rearrange("p (c h a) -> p c h a", c=3, h=4),
                                      tot[:, r, 64:F].rearrange("p (c h a) -> p c h a", c=3, h=4),
                                      bc(bc(inv, 2, 8), 1, 3), ALU.mult))
                sweep(v, ECOL, [(0, accumulate, 1), (1, divide, 1)], R)

            @block.tensor
            def _(pe):
                def turn(k):
                    r = k.slot(2)
                    pe.wait_ge(nrm, (k.t + 1) * NR)
                    if k.past(2):
                        pe.wait_ge(xtc, k.t - 1)
                    pe.transpose(pt[r][:, 0:P], avg[:, r, 0:P], m.ident[:, :])
                    pe.transpose(pt[r][0:V, P:2 * P], avg[:, r, P:F], m.ident[:, :]).then_inc(xt, 1)

                def maps(k):
                    r = k.slot(2)
                    pe.wait_ge(xtc, k.t + 1)
                    if k.past(2):
                        pe.wait_ge(obc, k.t - 1)
                    pe.matmul(py[r][:, 0:P], t1[:, r, :], wb[:, :], start=True, stop=True)
                    pe.matmul(py[r][:, P:F], t2[:, r, :], w2[:, :], start=True, stop=True).then_inc(y, 1)

                def fix(k):
                    if k.is_fix():
                        pe.wait_ge(acc, ECOL * AC)
                        pe.matmul(pf[:, 0:A], q.carry[:, :], tot[:, (ECOL - 1) % R, :], start=True,
                                  stop=True).then_inc(fx, 1)
                sweep(pe, ECOL, [(0, fix, 1), (1, turn, 1), (2, maps, 1)], 2)

            @block.scalar
            def _(a):
                def copy_x(k):
                    r = k.slot(2)
                    a.wait_ge(xt, k.t + 1)
                    if k.past(2):
                        a.wait_ge(y, k.t - 1)
                    a.copy(t1[:, r, :], pt[r][:, 0:P])
                    a.copy(t2[:, r, :], pt[r][0:V, P:2 * P]).then_inc(xtc, 1)

                def copy_y(k):
                    r = k.slot(R)
                    a.wait_ge(y, k.t + 1)
                    if k.past(R):
                        a.wait_ge(sct[r], k.lap(R) * 16)
                    a.copy(ob[:, r, :], py[k.slot(2)][:, 0:F]).then_inc(obc, 1)
                sweep(a, ECOL, [(0, copy_x, 1), (1, copy_y, 1)], R)

            @block.gpsimd
            def _(g):
                top = g.to_reg(NROWS - 1)

                def scatter(k):
                    r = k.slot(R)
                    if k.past(R):
                        g.wait_ge(sct[r], k.lap(R) * 16)
                    src = q.fix_id[:, :] if k.is_fix() else q.es[:, bass.ds(k.t, 1), WIDX].bitcast(I32)
                    g.tensor_copy(wi[:, r, :], src).then_inc(wic, 1)
                    g.wait_ge(wic, k.t + 1)
                    g.wait_ge(obc, k.t + 1)
                    g.sem_inc(gate, 1)
                    g.indirect_dma_start(agg, bass.IndirectOffsetOnAxis(ap=wi[:, r, :], axis=0), ob[:, r, :], None,
                                         bounds_check=top, oob_is_err=False).then_inc(sct[r], 16)
                sweep(g, ECOL, [(0, scatter, 1)], R)
                for r in range(R):
                    g.wait_ge(sct[r], 16 * len(range(r, ECOL + 1, R)))


def bilinear_layer(nc, m, io, x, q, agg):
    w = io.w
    c96 = float(1 / np.sqrt(96.0))
    f0, f1 = float(1 / np.sqrt(S * S + V * V)), float(1 / np.sqrt(2 * S * V))
    NZ0, NZ1 = S * S // P, V * V // P
    NG = (NZ0 + NZ1) // 4
    HALF = V * V
    with ExitStack() as ctx:
        sb, ps, sem = scope(nc, ctx, "b")
        wm1, wm2 = sb("wm1", [P, 416]), sb("wm2", [V, P])
        w000, w110 = sb("w000", [P, NZ0, 64]), sb("w110", [P, V * V // P, 64])
        w011, w101 = sb("w011", [S, HALF]), sb("w101", [S, V, V])
        wl, wz, wsc = sem("wl"), sem("wz"), sem("wsc")
        w2d = {n: w[f"L3_gnn_{n}"].rearrange("u a w -> (u a) w") for n in ("wm000", "wm011", "wm101", "wm110")}
        loads = [(wm1[0:64, 0:64], w2d["wm000"]), (wm1[0:64, 64:128], w["L3_gnn_lm0"]),
                 (wm1[0:64, 128:160], w2d["wm011"])]
        for blk, at in ((wm1[64:96, 160:288], 0), (wm1[96:128, 288:416], 1), (wm2[:, :], 2)):
            loads += [(blk[:, 0:64], w2d["wm110"]), (blk[:, 64:96], w2d["wm101"]), (blk[:, 96:128], w["L3_gnn_lm1"])]
        loads += [(w000[:, :, :], w["L3_gnn_wu000"].rearrange("(k a) v w -> (a v) k w", a=2)),
                  (w110[:, :, :], w["L3_gnn_wu110"].rearrange("(k a) v w -> (a v) k w", a=4)),
                  (w011[:, :], w["L3_gnn_wu011"].rearrange("u v w -> u (v w)")),
                  (w101[:, :, :], w["L3_gnn_wu101"].rearrange("u v w -> v u w"))]
        with nc.Block() as block:
            @block.vector
            def _(v):
                v.memset(wm1[:, :], 0.0).then_inc(wz, 1)
                v.tensor_copy(q.es[:, :, Y0], q.attr[:, :, A4 + 3]).then_inc(wsc, 1)
                v.tensor_copy(q.es[:, :, Y1:Y1 + 3], q.attr[:, :, A4:A4 + 3]).then_inc(wsc, 1)

            @block.sync
            def _(sp):
                sp.wait_ge(wz, 1)
                chain_loads(sp, wl, loads)
                sp.sem_inc(wz, 1)

            @block.scalar
            def _(a):
                a.wait_ge(wz, 2)
                blocks = wm1[:, 160:416].rearrange("p (c k) -> p c k", c=2)
                for ap, f in ((wm1[:, 0:64], c96), (wm1[:, 64:128], 1 / 8.0), (wm1[:, 128:160], c96),
                              (blocks[:, :, 0:64], R3 * c96), (blocks[:, :, 64:96], c96),
                              (blocks[:, :, 96:128], float(1 / np.sqrt(32.0))), (wm2[:, 0:64], R3 * c96),
                              (wm2[:, 64:96], c96), (wm2[:, 96:128], float(1 / np.sqrt(32.0))),
                              (w000[:, :, :], f0), (w110[:, :, :], R3 * f0), (w011[:, :], f1), (w101[:, :, :], f1)):
                    a.mul(ap, ap, f).then_inc(wsc, 1)

        R = 4
        gi, gj, wi = (sb(n, [P, R, 1], I32) for n in ("gi", "gj", "wi"))
        xd, xs = sb("xd", [P, R, F + 1]), sb("xs", [P, R, F + 1])
        t1, t2 = sb("t1", [P, 2, P]), sb("t2", [V, 2, P])
        mp, mg, tmp = sb("mp", [P, 2, 544]), sb("mg", [P, 2, F]), sb("tmp", [P, 2, 352])
        tot, s1 = sb("tot", [P, R, F]), sb("s1", [P, F])
        xa = sb("xa", [S, 2, 2 * P])
        z, zv = sb("z", [P, 2, (NZ0 + NZ1) * P]), sb("zv", [P, 2, 3, V * V])
        zt = sb("zt", [P, 2, 512])
        yt, pr = sb("yt", [P, 2, 2 * HALF]), sb("pr", [P, 3, 2 * V, V])
        ub = sb("ub", [P, R, F])
        pt, pm1, pm2, pxa, pyt, po = (ps(n) for n in ("pt", "pm1", "pm2", "pxa", "pyt", "po"))
        pz = [ps(f"pz{r}") for r in range(2)]
        gad, gas, sct = ([sem(f"{n}{r}") for r in range(R)] for n in ("gad", "gas", "sct"))
        (gic, gjc, wic, gate, init, xt, xtc, y, mpc, acc, fx, xat, xac, zp, ztr, ztc, zm, yq, yqc, vd, uc) = (
            sem(n) for n in ("gic", "gjc", "wic", "gate", "init", "xt", "xtc", "y", "mpc", "acc", "fx", "xat", "xac",
                             "zp", "ztr", "ztc", "zm", "yq", "yqc", "vd", "uc"))
        za, zs = sem("za"), sem("zs")
        AC, ZP, ZS, VD = 9, 2, 4, 3
        U_POOL, U_ACT = 8, 32
        YAT = (0, 1, 2, 3)
        L_ACC, L_Z, L_XA, L_BIG, L_VEC, L_SC = 1, 2, 3, 4, 4, 6

        with nc.Block() as block:
            @block.gpsimd
            def _(g):
                top = g.to_reg(NROWS - 1)

                def gather_dst(k):
                    r = k.slot(R)
                    if k.past(R):
                        g.wait_ge(gad[r], k.lap(R) * 16)
                        g.wait_ge(xt, k.t - R + 1)
                    g.tensor_copy(gi[:, r, :], q.es[:, bass.ds(k.t, 1), GIDX].bitcast(I32)).then_inc(gic, 1)
                    g.wait_ge(gic, k.t + 1)
                    g.sem_inc(gate, 1)
                    g.indirect_dma_start(xd[:, r, :], None, x, bass.IndirectOffsetOnAxis(ap=gi[:, r, :], axis=0),
                                         bounds_check=top, oob_is_err=False).then_inc(gad[r], 16)

                def gather_src(k):
                    r = k.slot(R)
                    if k.past(R):
                        g.wait_ge(gas[r], k.lap(R) * 16)
                        g.wait_ge(vd, (k.t - R + 1) * VD)
                        g.wait_ge(xat, k.t - R + 1)
                    src = q.first_id[:, :] if k.is_fix() else q.es[:, bass.ds(k.t, 1), GIDX2].bitcast(I32)
                    g.tensor_copy(gj[:, r, :], src).then_inc(gjc, 1)
                    g.wait_ge(gjc, k.t + 1)
                    g.sem_inc(gate, 1)
                    g.indirect_dma_start(xs[:, r, :], None, x, bass.IndirectOffsetOnAxis(ap=gj[:, r, :], axis=0),
                                         bounds_check=top, oob_is_err=False).then_inc(gas[r], 16)

                def scatter(k):
                    r = k.slot(R)
                    if k.past(R):
                        g.wait_ge(sct[r], k.lap(R) * 16)
                    src = q.fix_id[:, :] if k.is_fix() else q.es[:, bass.ds(k.t, 1), WIDX].bitcast(I32)
                    g.tensor_copy(wi[:, r, :], src).then_inc(wic, 1)
                    g.wait_ge(wic, k.t + 1)
                    g.wait_ge(uc, k.t + 1)
                    g.wait_ge(vd, (k.t + 1) * VD)
                    g.sem_inc(gate, 1)
                    g.indirect_dma_start(agg, bass.IndirectOffsetOnAxis(ap=wi[:, r, :], axis=0), ub[:, r, :], None,
                                         bounds_check=top, oob_is_err=False).then_inc(sct[r], 16)

                def outer_share(k):
                    d, r = k.slot(2), k.slot(R)
                    dots = z[:, d, S * S:]
                    g.wait_ge(gas[r], (k.lap(R) + 1) * 16)
                    g.wait_ge(acc, (k.t + 1) * AC)
                    if k.past(2):
                        g.wait_ge(ztr, (k.t - 1) * NG)
                    g.sem_inc(gate, 1)
                    g.tensor_tensor(z[:, d, U_POOL * S:U_ACT * S].rearrange("p (u v) -> p u v", v=S),
                                    bc(xs[:, r, U_POOL:U_ACT], 2, S), bc(tot[:, r, 0:S], 1, U_ACT - U_POOL),
                                    ALU.mult).then_inc(zs, 1)
                    g.tensor_tensor(zv[:, d, 2, :].rearrange("p (u v) -> p u v", u=V), bc(xs[:, r, P:F], 2, V),
                                    bc(tot[:, r, P:F], 1, V), ALU.mult).then_inc(zs, 1)
                    g.wait_ge(zp, (k.t + 1) * ZP)
                    g.sem_inc(gate, 1)
                    g.tensor_tensor(dots, zv[:, d, 0, :], zv[:, d, 1, :], ALU.add).then_inc(zs, 1)
                    g.wait_ge(zs, k.t * ZS + 3)
                    g.sem_inc(gate, 1)
                    g.tensor_tensor(dots, dots, zv[:, d, 2, :], ALU.add).then_inc(zs, 1)
                sweep(g, ECOL, [(0, gather_dst), (1, gather_src, 1), (L_SC, scatter, 1), (L_Z + 1, outer_share, 1)], R)
                for r in range(R):
                    g.wait_ge(sct[r], 16 * len(range(r, ECOL + 1, R)))

            @block.tensor
            def _(pe):
                def turn(k):
                    if k.past(1):
                        pe.wait_ge(xtc, k.t)
                    pe.wait_ge(gad[k.slot(R)], (k.lap(R) + 1) * 16)
                    pe.transpose(pt[:, 0:P], xd[:, k.slot(R), 0:P], m.ident[:, :])
                    pe.transpose(pt[0:V, P:2 * P], xd[:, k.slot(R), P:F], m.ident[:, :]).then_inc(xt, 1)

                def maps(k):
                    r = k.slot(2)
                    pe.wait_ge(xtc, k.t + 1)
                    if k.past(1):
                        pe.wait_ge(mpc, k.t)
                    pe.matmul(pm1[:, 0:416], t1[:, r, :], wm1[:, :], start=True, stop=True)
                    pe.matmul(pm2[:, 0:P], t2[:, r, :], wm2[:, :], start=True, stop=True).then_inc(y, 1)

                def fix(k):
                    if k.is_fix():
                        pe.wait_ge(acc, ECOL * AC)
                        pe.wait_ge(mpc, ECOL)
                        pe.matmul(pm1[:, 0:F], q.carry[:, :], tot[:, (ECOL - 1) % R, :], start=True,
                                  stop=True).then_inc(fx, 1)

                def turn_scalars(k):
                    r = k.slot(R)
                    pe.wait_ge(gas[r], (k.lap(R) + 1) * 16)
                    pe.wait_ge(acc, (k.t + 1) * AC)
                    if k.past(1):
                        pe.wait_ge(xac, k.t)
                    pe.sem_inc(gate, 1)
                    pe.transpose(pxa[0:S, 0:P], xs[:, r, 0:S], m.ident[:, :])
                    pe.transpose(pxa[0:S, P:2 * P], tot[:, r, 0:S], m.ident[:, :]).then_inc(xat, 1)

                def sum_group(k, g):
                    pe.wait_ge(ztc, k.t * NG + g + 1)
                    if g == 0 and k.past(1):
                        pe.wait_ge(uc, k.t)
                    for j in range(4):
                        c = 4 * g + j
                        wc = w000[:, c, :] if c < NZ0 else w110[:, c - NZ0, :]
                        ins = pe.matmul(po[:, 0:S], zt[:, g % 2, j * P:(j + 1) * P], wc, start=(c == 0),
                                        stop=(c == NZ0 + NZ1 - 1))
                    ins.then_inc(zm, 1)

                def big(k):
                    r = k.slot(2)

                    def turn_group(g):
                        n = k.t * NG + g
                        if g < U_POOL // 8:
                            pe.wait_ge(zp, k.t * ZP + 1)
                        elif g < U_ACT // 8:
                            pe.wait_ge(zs, k.t * ZS + 1)
                        elif g < NZ0 // 4:
                            pe.wait_ge(za, k.t + 1)
                        else:
                            pe.wait_ge(zs, (k.t + 1) * ZS)
                        if g >= 2 or k.past(1):
                            pe.wait_ge(ztc, n - 1)
                        for j in range(4):
                            at = (4 * g + j) * P
                            ins = pe.transpose(pz[g % 2][:, j * P:(j + 1) * P], z[:, r, at:at + P], m.ident[:, :])
                        ins.then_inc(ztr, 1)

                    for g in range(NG):
                        turn_group(g)
                        if g in YAT:
                            i = YAT.index(g)
                            if i == 0:
                                pe.wait_ge(xac, k.t + 1)
                            if i > 0 or k.past(1):
                                pe.wait_ge(yqc, k.t * 4 + i)
                            pe.sem_inc(gate, 1)
                            wt = w011[:, (i % 2) * 512:(i % 2 + 1) * 512] if i < 2 else \
                                w101[:, (i % 2) * 16:(i % 2 + 1) * 16, :].rearrange("p a b -> p (a b)")
                            pe.matmul(pyt[:, :], xa[:, r, (i // 2) * P:(i // 2 + 1) * P], wt, start=True,
                                      stop=True).then_inc(yq, 1)
                        if g > 0:
                            sum_group(k, g - 1)

                def last_sum(k):
                    sum_group(k, NG - 1)
                sweep(pe, ECOL, [(L_ACC, fix, 1), (0, turn), (L_BIG + 1, last_sum, 1), (1, maps),
                                 (L_XA, turn_scalars, 1), (L_BIG, big, 1)], 2)

            @block.scalar
            def _(a):
                def copy_x(k):
                    r = k.slot(2)
                    a.wait_ge(xt, k.t + 1)
                    if k.past(2):
                        a.wait_ge(y, k.t - 1)
                    a.copy(t1[:, r, :], pt[:, 0:P])
                    a.copy(t2[:, r, :], pt[0:V, P:2 * P]).then_inc(xtc, 1)

                def copy_y(k):
                    r = k.slot(2)
                    a.wait_ge(y, k.t + 1)
                    if k.past(2):
                        a.wait_ge(acc, (k.t - 1) * AC)
                    a.copy(mp[:, r, 0:416], pm1[:, 0:416])
                    a.copy(mp[:, r, 416:544], pm2[:, 0:P]).then_inc(mpc, 1)

                def copy_xa(k):
                    a.wait_ge(xat, k.t + 1)
                    if k.past(2):
                        a.wait_ge(yq, (k.t - 1) * 4)
                    a.copy(xa[:, k.slot(2), :], pxa[0:S, 0:2 * P]).then_inc(xac, 1)

                def outer_rows(k, first, last):
                    r = k.slot(R)
                    if first == U_ACT:
                        a.wait_ge(gas[r], (k.lap(R) + 1) * 16)
                        a.wait_ge(acc, (k.t + 1) * AC)
                        if k.past(2):
                            a.wait_ge(ztr, (k.t - 1) * NG)
                    for u in range(first, last):
                        ins = a.activation(z[:, k.slot(2), u * S:(u + 1) * S], tot[:, r, 0:S], ACT.Copy,
                                           scale=xs[:, r, u:u + 1])
                    if last == S:
                        ins.then_inc(za, 1)

                def outer_first(k):
                    if k.i is None and k.base == 0:
                        outer_rows(k, U_ACT, S)

                def big(k):
                    nxt = Tile(k.base + 1, k.i)
                    more = k.i is not None or k.base < ECOL
                    cuts = [U_ACT + (S - U_ACT) * g // NG for g in range(NG + 1)]
                    for g in range(NG):
                        if more:
                            outer_rows(nxt, cuts[g], cuts[g + 1])
                        n = k.t * NG + g
                        a.wait_ge(ztr, n + 1)
                        if g >= 2 or k.past(1):
                            a.wait_ge(zm, n - 1)
                        a.copy(zt[:, g % 2, :], pz[g % 2][:, :]).then_inc(ztc, 1)
                        if g in YAT:
                            i = YAT.index(g)
                            a.wait_ge(yq, k.t * 4 + i + 1)
                            if k.past(2):
                                a.wait_ge(vd, (k.t - 2) * VD + (1 if i < 2 else 2))
                            a.copy(yt[:, k.slot(2), i * 512:(i + 1) * 512], pyt[:, :]).then_inc(yqc, 1)
                    a.wait_ge(zm, (k.t + 1) * NG)
                    if k.past(R):
                        a.wait_ge(sct[k.slot(R)], k.lap(R) * 16)
                    a.copy(ub[:, k.slot(R), 0:S], po[:, 0:S]).then_inc(uc, 1)
                sweep(a, ECOL, [(0, copy_x), (1, copy_y), (L_XA, outer_first), (L_XA, copy_xa, 1), (L_BIG, big, 1)], R)

            @block.vector
            def _(v):
                v.memset(s1[:, :], 0.0).then_inc(init, 1)
                v.memset(tot[:, R - 1, :], 0.0).then_inc(init, 1)
                v.wait_ge(init, 2)

                def accumulate(k):
                    r, d = k.slot(R), k.slot(2)
                    c = Chain(v, acc, AC, k)
                    if k.past(R):
                        v.wait_ge(vd, (k.t - R + 1) * VD)
                        v.wait_ge(xat, k.t - R + 1)
                    if k.is_fix():
                        v.wait_ge(fx, 1)
                        v.wait_ge(acc, ECOL * AC)
                        v.tensor_tensor(tot[:, r, :], s1[:, :], pm1[:, 0:F], ALU.add).then_inc(acc, AC)
                        return
                    v.wait_ge(mpc, k.t + 1)
                    edge = bass.ds(k.t, 1)
                    e0 = q.es[:, edge, Y0]
                    e1 = q.es[:, edge, Y1:Y1 + 3].rearrange("p a c -> p (a c)")
                    sc = mp[:, d, 0:F]
                    vc = mp[:, d, F:544].rearrange("p (c k) -> p c k", c=3)
                    ta, tb, tc = tmp[:, d, 0:192], tmp[:, d, 192:288], tmp[:, d, 288:352]
                    gs, gv = mg[:, d, 0:S], mg[:, d, S:F]
                    g3 = gv.rearrange("p (c u) -> p c u", c=3)
                    tb3 = tb.rearrange("p (c u) -> p c u", c=3)
                    c(v.scalar_tensor_tensor(gs, sc[:, 0:64], e0, sc[:, 64:128], ALU.mult, ALU.add))
                    c(v.tensor_tensor(ta.rearrange("p (c u) -> p c u", c=3), vc[:, :, 0:64], bc(e1, 2, 64), ALU.mult))
                    c(v.scalar_tensor_tensor(g3, vc[:, :, 64:96], e0, vc[:, :, 96:128], ALU.mult, ALU.add))
                    c(v.tensor_tensor(tb3, bc(sc[:, 128:160], 1, 3), bc(e1, 2, V), ALU.mult))
                    c.wait(2)
                    c(v.tensor_reduce(tc, ta.rearrange("p (c u) -> p u c", c=3), AX, ALU.add))
                    c.wait(4)
                    c(v.tensor_tensor(gv, gv, tb, ALU.add))
                    c.wait(5)
                    c(v.tensor_tensor(gs, gs, tc, ALU.add))
                    c.wait()
                    c(v.scalar_tensor_tensor(tot[:, r, :], tot[:, (r - 1) % R, :], q.es[:, edge, SAME], mg[:, d, :],
                                             ALU.mult, ALU.add))
                    c.wait()
                    c(v.scalar_tensor_tensor(s1[:, :], tot[:, r, :], q.es[:, edge, FEND], s1[:, :], ALU.mult, ALU.add))

                def outer(k):
                    r, d = k.slot(R), k.slot(2)
                    c = Chain(v, zp, ZP, k)
                    v.wait_ge(gas[r], (k.lap(R) + 1) * 16)
                    v.wait_ge(acc, (k.t + 1) * AC)
                    if k.past(2):
                        v.wait_ge(ztr, (k.t - 1) * NG)
                    c(v.tensor_tensor(z[:, d, 0:U_POOL * S].rearrange("p (u v) -> p u v", v=S),
                                      bc(xs[:, r, 0:U_POOL], 2, S), bc(tot[:, r, 0:S], 1, U_POOL), ALU.mult))
                    xv = xs[:, r, S:P].rearrange("p (c u) -> p c u", c=2)
                    av = tot[:, r, S:P].rearrange("p (c u) -> p c u", c=2)
                    if k.past(2):
                        v.wait_ge(zs, (k.t - 1) * ZS)
                    c(v.tensor_tensor(zv[:, d, 0:2, :].rearrange("p c (u v) -> p c u v", u=V), bc(xv, 3, V),
                                      bc(av, 2, V), ALU.mult))

                def vectors(k):
                    r = k.slot(R)
                    c = Chain(v, vd, VD, k)
                    if k.past(R):
                        v.wait_ge(sct[r], k.lap(R) * 16)
                    if k.past(1):
                        v.wait_ge(vd, k.t * VD)
                    for i, src in enumerate((tot, xs)):
                        v.wait_ge(yqc, k.t * 4 + 2 * i + 2)
                        half = yt[:, k.slot(2), i * HALF:(i + 1) * HALF].rearrange("p (q w) -> p q w", w=V)
                        c(v.tensor_tensor(pr[:, :, i * V:(i + 1) * V, :], bc(half, 1, 3),
                                          bc(src[:, r, S:F].rearrange("p (c u) -> p c u", c=3), 3, V), ALU.mult))
                    c.wait()
                    c(v.tensor_reduce(ub[:, r, S:F].rearrange("p (c w) -> p c w", c=3),
                                      pr[:, :, :, :].rearrange("p c q w -> p c w q"), AX, ALU.add))
                sweep(v, ECOL, [(L_VEC, vectors, 1), (L_ACC, accumulate, 1), (L_Z, outer, 1)], R)


def build(nc, io, out):
    with ExitStack() as ctx:
        sb, ps, sem = scope(nc, ctx, "g")
        m = Mem()
        m.ident, m.ones, m.before, m.after = (sb(n, [P, P]) for n in ("ident", "ones", "before", "after"))
        m.iota_i, m.iota, m.eps = sb("iotai", [P, HI], I32), sb("iota", [P, HI]), sb("eps", [P, 1])
        m.src, m.dst = Mem(), Mem()
        for q, n in ((m.src, "s"), (m.dst, "d")):
            q.attr_y0, q.attr_y1 = A4, A4 + 1
            q.attr, q.es = sb(f"attr{n}", [P, ECOL, ROW]), sb(f"es{n}", [P, ECOL, ESW])
            q.ends, q.first_run, q.last_run = sb(f"ends{n}", [P, 2]), sb(f"fr{n}", [P, ECOL]), sb(f"lr{n}", [P, ECOL])
            q.fix_id, q.first_id, q.carry = sb(f"fix{n}", [P, 1], I32), sb(f"first{n}", [P, 1], I32), sb(f"carry{n}", [P, P])

        def dram(name, shape):
            return nc.dram_tensor(name, shape, F32, kind="Internal").ap()
        m.by_src, m.by_dst = dram("by_src", [EROWS, ROW]), dram("by_dst", [EROWS, ROW])
        m.agg_src, m.agg_dst = dram("agg_src", [NROWS, F]), dram("agg_dst", [NROWS, F])
        x1, x2, x3 = (dram(f"x{k}", [NROWS, F + 1]) for k in (1, 2, 3))
        with ExitStack() as zeroing:
            sb0, _, sem0 = scope(nc, zeroing, "zero")
            zero, zeroed = sb0("rows", [P, NCOL // 4 * F]), sem0("zeroed")
            m.edge = sb0("edge", [P, ECOL, ROW])
            setup(nc, io, m, zero, zeroed)
            sort(nc, m, zeroed)
        segments(nc, m)
        edge_layer(nc, m, io, 0, io.x, m.src, m.agg_src)
        node_layer(nc, m, io, 0, io.x, m.agg_src, x1)
        edge_layer(nc, m, io, 1, x1, m.dst, m.agg_dst)
        node_layer(nc, m, io, 1, x1, m.agg_dst, x2)
        with ExitStack() as heads:
            sb2, _, _ = scope(nc, heads, "at")
            logits, ex = sb2("logits", [P, 4, ECOL]), sb2("ex", [P, ECOL, 4])
            hid = dram("hid", [EROWS, F])
            attention_messages(nc, m, io, x2, m.dst, logits, hid)
            attention_weights(nc, m, m.dst, logits, ex)
            attention_sums(nc, m, io, m.dst, ex, hid, m.agg_dst)
        node_layer(nc, m, io, 2, x2, m.agg_dst, x3)
        bilinear_layer(nc, m, io, x3, m.src, m.agg_src)
        node_layer(nc, m, io, 3, x3, m.agg_src, out)


WEIGHTS = ["L0_gnn_W1_0", "L0_gnn_W1_1", "L0_gnn_Wfc1", "L0_gnn_Wfc2", "L0_gnn_Wfc3", "L0_gnn_W2_0", "L0_gnn_W2_1",
           "L0_gnn_Wsc0", "L0_gnn_Wsc1", "L0_gnn_g0", "L0_gnn_g1", "L1_gnn_W_si0", "L1_gnn_W_si1", "L1_gnn_W_l1_0",
           "L1_gnn_W_l1_1", "L1_gnn_W_l2_00", "L1_gnn_W_l2_10", "L1_gnn_W_l2_01", "L1_gnn_W_l2_11", "L1_gnn_W_fc1",
           "L1_gnn_W_fc2", "L2_gnn_gamma_s", "L2_gnn_beta_s", "L2_gnn_gamma_v", "L2_gnn_Ws_src", "L2_gnn_Wv_src",
           "L2_gnn_Ws_dst", "L2_gnn_Wv_dst", "L2_gnn_W_rbf", "L2_gnn_W_alpha", "L2_gnn_alpha_dot", "L2_gnn_Ws_val",
           "L2_gnn_Wv_val", "L2_gnn_Wg", "L2_gnn_w2_ss", "L2_gnn_w2_sv", "L2_gnn_w2_vs", "L2_gnn_w2_vv0",
           "L2_gnn_w2_vv1", "L2_gnn_Ws_vlin", "L2_gnn_Wv_vlin", "L2_gnn_Wps", "L2_gnn_Wpv", "L3_gnn_wm000",
           "L3_gnn_wm011", "L3_gnn_wm101", "L3_gnn_wm110", "L3_gnn_lm0", "L3_gnn_lm1", "L3_gnn_wu000", "L3_gnn_wu011",
           "L3_gnn_wu101", "L3_gnn_wu110", "L3_gnn_lu0", "L3_gnn_lu1"]


def kernel(**inputs):
    import concourse.bacc as bacc
    from concourse.bass_utils import run_bass_kernel_spmd as run

    nc = bacc.Bacc("TRN2", target_bir_lowering=False, num_devices=1)
    arrays, io = {}, Mem()

    def given(name, a):
        arrays[name] = np.ascontiguousarray(a)
        return nc.dram_tensor(name, a.shape, mybir.dt.from_np(a.dtype), kind="ExternalInput").ap()

    x = np.asarray(inputs["x"])
    rows = np.zeros((NROWS, F + 1), np.float32)
    rows[:NODES, :S] = x[:, :S]
    rows[:NODES, S:F] = x[:, S:].reshape(NODES, V, 3).transpose(0, 2, 1).reshape(NODES, 3 * V)
    rows[:NODES, F:] = inputs["node_vec1"]
    eidx = np.full((EROWS, 2), DUMMY, np.int32)
    eidx[:EDGES, 0], eidx[:EDGES, 1] = inputs["src"], inputs["dst"]
    eattr = np.zeros((EROWS, ROW - 2), np.float32)
    eattr[:EDGES] = np.concatenate([np.asarray(inputs[f"edge_attr_{n}"]) for n in (4, 8, 10, 16)], axis=1)
    io.x, io.eidx, io.eattr = given("x_rows", rows), given("eidx", eidx), given("eattr", eattr)
    io.w = {n: given(n, np.asarray(inputs[n])) for n in WEIGHTS}
    out = nc.dram_tensor("out", [NROWS, F], F32, kind="ExternalOutput").ap()
    build(nc, io, out)
    got = run(nc, [arrays], core_ids=[0]).results[0]["out"][:NODES]
    back = np.empty_like(got)
    back[:, :S] = got[:, :S]
    back[:, S:] = got[:, S:].reshape(NODES, 3, V).transpose(0, 2, 1).reshape(NODES, 3 * V)
    return back
```
